# Optimizing a Trainium2 kernel written in Bass

```python
import numpy as np
import jax
import jax.numpy as jnp

def _softmax(x, axis=-1):
    return jax.nn.softmax(x, axis=axis)

def _gelu(x):
    return jax.nn.gelu(x, approximate=True)

def _silu(x):
    return jax.nn.silu(x)

def _sigmoid(x):
    return jax.nn.sigmoid(x)

def _layernorm(x, axis=-1, eps=1e-05):
    m = jnp.mean(x, axis=axis, keepdims=True)
    v = jnp.var(x, axis=axis, keepdims=True)
    return (x - m) / jnp.sqrt(v + eps)

def _scatter_add(tgt, idx, src, axis=0):
    return tgt.at[idx].add(src)

def _segment_sum(src, seg, n):
    return jax.ops.segment_sum(src, seg, n)
kernel_name = 'mk_flamingo_gated_d2_seqx_r8_7bd7d8'

def setup_inputs(seed: int=0):
    np.random.seed(seed)
    _w = jnp.asarray

    def _rec_inputs():
        import jax
        import jax.numpy as jnp
        _rk = jax.random.key(seed)
        x = -7.109e-05 + 0.9999 * jax.random.normal(jax.random.fold_in(_rk, 1), (4, 256, 256), jnp.float32)
        _lenS = 256 - jax.random.randint(jax.random.fold_in(_rk, 7), (4,), 0, max(1, 256 // 4) + 1, jnp.int32)
        _lenS2 = 256 - jax.random.randint(jax.random.fold_in(_rk, 8), (4,), 0, max(1, 256 // 4) + 1, jnp.int32)
        _ctx_2048P = jax.random.normal(jax.random.fold_in(_rk, 11), (4, 16, 256), jnp.float32)
        _ctx_2048c = jax.random.dirichlet(jax.random.fold_in(_rk, 511), 0.3 * jnp.ones((16,), jnp.float32), (4, 256))
        _ctx_2048t = jnp.einsum('bsk,bkd->bsd', _ctx_2048c, _ctx_2048P)
        _ctx_2048t = _ctx_2048t * jax.lax.rsqrt(jnp.mean(jnp.square(_ctx_2048t)) + 1e-12) * 0.953939
        ctx_2048 = -3.05549e-07 + 0.0199987 * (_ctx_2048t + 0.3 * jax.random.normal(jax.random.fold_in(_rk, 611), (4, 256, 256), jnp.float32))
        _g = jax.random.normal(jax.random.fold_in(_rk, 9001), (2, 2), jnp.float32)
        _g = jnp.sign(_g) * jnp.maximum(jnp.abs(_g), 1.0) + (_g == 0) * 1.0
        g_xattn = _g[0]
        g_ffn = _g[1]
        return (x, ctx_2048, g_xattn, g_ffn)
    x, ctx_2048, g_xattn, g_ffn = _rec_inputs()

    def _L0_xattn_setup():
        import jax, jax.numpy as jnp
        import numpy as np
        FP8_MAX = 448.0
        ACT_EPS = 0.0001
        W_EPS = 1e-06
        BLK = 128

        def quant_dequant_act_1x128(x):
            E, M, K = x.shape
            xb = x.reshape(E, M, K // BLK, BLK)
            amax = jnp.max(jnp.abs(xb), axis=-1, keepdims=True)
            safe = jnp.maximum(amax, ACT_EPS)
            q = (xb * (FP8_MAX / safe)).astype(jnp.float8_e4m3fn)
            return (q.astype(jnp.float32) * (safe / FP8_MAX)).reshape(E, M, K)

        def quant_dequant_weight_128x128(w):
            E, N, K = w.shape
            wb = w.reshape(E, N // BLK, BLK, K // BLK, BLK)
            amax = jnp.max(jnp.abs(wb), axis=(2, 4), keepdims=True)
            safe = jnp.maximum(amax, W_EPS)
            q = (wb * (FP8_MAX / safe)).astype(jnp.float8_e4m3fn)
            return (q.astype(jnp.float32) * (safe / FP8_MAX)).reshape(E, N, K)
        key = jax.random.key(seed)
        kx, kw = jax.random.split(key)
        E, M, K, N = (8, 512, 256, 256)
        x = jax.random.normal(kx, (E, M, K), dtype=jnp.float32)
        weight = jax.random.normal(kw, (E, N, K), dtype=jnp.float32) * 0.02
        return {'x': x, 'weight': weight}
    _L0_xattn_all = _L0_xattn_setup()
    _L0_xattn_in = {k: v for k, v in _L0_xattn_all.items() if k in ()}
    del _L0_xattn_all

    def _L0_ffn_setup():
        import jax, jax.numpy as jnp
        import numpy as np
        K = 2

        def gelu(v):
            return jax.nn.gelu(v, approximate=False)
        key = jax.random.key(seed)
        ks = jax.random.split(key, 10)
        B, S, D, H, E = (4, 256, 256, 128, 8)
        SH = 2 * H
        u = lambda k_, shape, b: jax.random.uniform(k_, shape, jnp.float32, -b, b)
        return {'x': jax.random.normal(ks[0], (B, S, D), jnp.float32), 'gate_w': u(ks[1], (D, E), 1.0 / D), 'w1': u(ks[2], (E, D, H), 1.0 / D), 'b1': u(ks[3], (E, H), 1.0 / np.sqrt(D)), 'w2': u(ks[4], (E, H, D), 1.0 / H), 'b2': u(ks[5], (E, D), 1.0 / np.sqrt(H)), 'shared_w1': u(ks[6], (D, SH), 1.0 / D), 'shared_b1': u(ks[7], (SH,), 1.0 / np.sqrt(D)), 'shared_w2': u(ks[8], (SH, D), 1.0 / SH), 'shared_b2': u(ks[9], (D,), 1.0 / np.sqrt(SH))}
    _L0_ffn_all = _L0_ffn_setup()
    _L0_ffn_in = {k: v for k, v in _L0_ffn_all.items() if k in ('gate_w', 'w1', 'b1', 'w2', 'b2', 'shared_w1', 'shared_b1', 'shared_w2', 'shared_b2')}
    del _L0_ffn_all

    def _L1_xattn_setup():
        import math
        import jax, jax.numpy as jnp
        import numpy as np
        HEADS = 16
        MASKED_BIAS = -10000.0

        def _mha(q, k, v):
            B, Sq, D = q.shape
            Sk = k.shape[-2]
            hd = D // HEADS
            qh = q.reshape(B, Sq, HEADS, hd).transpose(0, 2, 1, 3)
            kh = k.reshape(B, Sk, HEADS, hd).transpose(0, 2, 1, 3)
            vh = v.reshape(B, Sk, HEADS, hd).transpose(0, 2, 1, 3)
            scores = jnp.einsum('bhqd,bhkd->bhqk', qh, kh) / math.sqrt(hd)
            qi = jnp.arange(Sq)[:, None] + (Sk - Sq)
            ki = jnp.arange(Sk)[None, :]
            causal = ki <= qi
            scores = jnp.where(causal[None, None], scores, jnp.asarray(MASKED_BIAS, scores.dtype))
            attn = jax.nn.softmax(scores, axis=-1)
            out = jnp.einsum('bhqk,bhkd->bhqd', attn, vh)
            return out.transpose(0, 2, 1, 3).reshape(B, Sq, D)
        key = jax.random.key(seed)
        kq, kk, kv = jax.random.split(key, 3)
        B, S, D = (4, 128, 256)
        q = jax.random.normal(kq, (B, S, D), dtype=jnp.float32)
        k = jax.random.normal(kk, (B, S, D), dtype=jnp.float32)
        v = jax.random.normal(kv, (B, S, D), dtype=jnp.float32)
        return {'q': q, 'k': k, 'v': v}
    _L1_xattn_all = _L1_xattn_setup()
    _L1_xattn_in = {k: v for k, v in _L1_xattn_all.items() if k in ()}
    del _L1_xattn_all

    def _L1_ffn_setup():
        import jax, jax.numpy as jnp
        import numpy as np
        TOP_K = 2

        def _gelu(v):
            return jax.nn.gelu(v, approximate=False)
        key = jax.random.key(seed)
        ks = jax.random.split(key, 7)
        B, T, D, I, E = (2, 256, 256, 1024, 8)
        s = 0.02
        return {'x': jax.random.normal(ks[0], (B, T, D), jnp.float32), 'rw1': jax.random.normal(ks[1], (D, D // 2), jnp.float32) * s, 'rw2': jax.random.normal(ks[2], (D // 2, E), jnp.float32) * s, 'w1': jax.random.normal(ks[3], (E, D, I), jnp.float32) * s, 'b1': jax.random.normal(ks[4], (E, I), jnp.float32) * s, 'w2': jax.random.normal(ks[5], (E, I, D), jnp.float32) * s, 'b2': jax.random.normal(ks[6], (E, D), jnp.float32) * s}
    _L1_ffn_all = _L1_ffn_setup()
    _L1_ffn_in = {k: v for k, v in _L1_ffn_all.items() if k in ('rw1', 'rw2', 'w1', 'b1', 'w2', 'b2')}
    del _L1_ffn_all
    return {'x': x, 'ctx_2048': ctx_2048, 'g_xattn': g_xattn, 'g_ffn': g_ffn, 'L0_ffn_gate_w': _L0_ffn_in['gate_w'], 'L0_ffn_w1': _L0_ffn_in['w1'], 'L0_ffn_b1': _L0_ffn_in['b1'], 'L0_ffn_w2': _L0_ffn_in['w2'], 'L0_ffn_b2': _L0_ffn_in['b2'], 'L0_ffn_shared_w1': _L0_ffn_in['shared_w1'], 'L0_ffn_shared_b1': _L0_ffn_in['shared_b1'], 'L0_ffn_shared_w2': _L0_ffn_in['shared_w2'], 'L0_ffn_shared_b2': _L0_ffn_in['shared_b2'], 'L1_ffn_rw1': _L1_ffn_in['rw1'], 'L1_ffn_rw2': _L1_ffn_in['rw2'], 'L1_ffn_w1': _L1_ffn_in['w1'], 'L1_ffn_b1': _L1_ffn_in['b1'], 'L1_ffn_w2': _L1_ffn_in['w2'], 'L1_ffn_b2': _L1_ffn_in['b2']}

def reference(x, ctx_2048, g_xattn, g_ffn, L0_ffn_gate_w, L0_ffn_w1, L0_ffn_b1, L0_ffn_w2, L0_ffn_b2, L0_ffn_shared_w1, L0_ffn_shared_b1, L0_ffn_shared_w2, L0_ffn_shared_b2, L1_ffn_rw1, L1_ffn_rw2, L1_ffn_w1, L1_ffn_b1, L1_ffn_w2, L1_ffn_b2):
    import jax
    import jax.numpy as jnp

    def _L0_xattn_ref(x, weight):
        import jax, jax.numpy as jnp
        import numpy as np
        FP8_MAX = 448.0
        ACT_EPS = 0.0001
        W_EPS = 1e-06
        BLK = 128

        def quant_dequant_act_1x128(x):
            E, M, K = x.shape
            xb = x.reshape(E, M, K // BLK, BLK)
            amax = jnp.max(jnp.abs(xb), axis=-1, keepdims=True)
            safe = jnp.maximum(amax, ACT_EPS)
            q = (xb * (FP8_MAX / safe)).astype(jnp.float8_e4m3fn)
            return (q.astype(jnp.float32) * (safe / FP8_MAX)).reshape(E, M, K)

        def quant_dequant_weight_128x128(w):
            E, N, K = w.shape
            wb = w.reshape(E, N // BLK, BLK, K // BLK, BLK)
            amax = jnp.max(jnp.abs(wb), axis=(2, 4), keepdims=True)
            safe = jnp.maximum(amax, W_EPS)
            q = (wb * (FP8_MAX / safe)).astype(jnp.float8_e4m3fn)
            return (q.astype(jnp.float32) * (safe / FP8_MAX)).reshape(E, N, K)
        xq = quant_dequant_act_1x128(x)
        wq = quant_dequant_weight_128x128(weight)
        return jnp.einsum('emk,enk->emn', xq, wq)

    def _L0_ffn_ref(x, gate_w, w1, b1, w2, b2, shared_w1, shared_b1, shared_w2, shared_b2):
        import jax, jax.numpy as jnp
        import numpy as np
        K = 2

        def gelu(v):
            return jax.nn.gelu(v, approximate=False)
        B, S, D = x.shape
        E = gate_w.shape[1]
        xf = x.reshape(-1, D)
        logits = xf @ gate_w
        top_logits, top_idx = jax.lax.top_k(logits, K)
        top_gates = jax.nn.softmax(top_logits, axis=-1)
        gates = jnp.sum(jax.nn.one_hot(top_idx, E, dtype=xf.dtype) * top_gates[..., None], axis=1)
        h = gelu(jnp.einsum('nd,edh->neh', xf, w1) + b1)
        out_e = jnp.einsum('neh,ehd->ned', h, w2) + b2
        routed = jnp.einsum('ne,ned->nd', gates, out_e)
        shared = gelu(xf @ shared_w1 + shared_b1) @ shared_w2 + shared_b2
        return (routed + shared).reshape(B, S, D)

    def _L1_xattn_ref(q, k, v):
        import math
        import jax, jax.numpy as jnp
        import numpy as np
        HEADS = 16
        MASKED_BIAS = -10000.0

        def _mha(q, k, v):
            B, Sq, D = q.shape
            Sk = k.shape[-2]
            hd = D // HEADS
            qh = q.reshape(B, Sq, HEADS, hd).transpose(0, 2, 1, 3)
            kh = k.reshape(B, Sk, HEADS, hd).transpose(0, 2, 1, 3)
            vh = v.reshape(B, Sk, HEADS, hd).transpose(0, 2, 1, 3)
            scores = jnp.einsum('bhqd,bhkd->bhqk', qh, kh) / math.sqrt(hd)
            qi = jnp.arange(Sq)[:, None] + (Sk - Sq)
            ki = jnp.arange(Sk)[None, :]
            causal = ki <= qi
            scores = jnp.where(causal[None, None], scores, jnp.asarray(MASKED_BIAS, scores.dtype))
            attn = jax.nn.softmax(scores, axis=-1)
            out = jnp.einsum('bhqk,bhkd->bhqd', attn, vh)
            return out.transpose(0, 2, 1, 3).reshape(B, Sq, D)
        return _mha(q, k, v)

    def _L1_ffn_ref(x, rw1, rw2, w1, b1, w2, b2):
        import jax, jax.numpy as jnp
        import numpy as np
        TOP_K = 2

        def _gelu(v):
            return jax.nn.gelu(v, approximate=False)
        logits = _gelu(x @ rw1) @ rw2
        probs = jax.nn.softmax(logits, axis=-1)
        wgt, idx = jax.lax.top_k(probs, TOP_K)
        E = w1.shape[0]
        out = jnp.zeros_like(x)
        for e in range(E):
            Ye = _gelu(x @ w1[e] + b1[e]) @ w2[e] + b2[e]
            Ce = _gelu(b1[e]) @ w2[e] + b2[e]
            for k in range(TOP_K):
                mask = idx[..., k] == e
                active = jnp.any(mask).astype(x.dtype)
                term = jnp.where(mask[..., None], Ye, Ce)
                out = out + active * wgt[..., k:k + 1] * term
        return out
    x = x + jnp.tanh(g_xattn[0]) * _L0_xattn_ref(_layernorm(x, axis=-1), ctx_2048)
    x = x + jnp.tanh(g_ffn[0]) * _L0_ffn_ref(_layernorm(x, axis=-1), L0_ffn_gate_w, L0_ffn_w1, L0_ffn_b1, L0_ffn_w2, L0_ffn_b2, L0_ffn_shared_w1, L0_ffn_shared_b1, L0_ffn_shared_w2, L0_ffn_shared_b2)
    x = x + jnp.tanh(g_xattn[1]) * _L1_xattn_ref(_layernorm(x, axis=-1), ctx_2048, ctx_2048)
    x = x + jnp.tanh(g_ffn[1]) * _L1_ffn_ref(_layernorm(x, axis=-1), L1_ffn_rw1, L1_ffn_rw2, L1_ffn_w1, L1_ffn_b1, L1_ffn_w2, L1_ffn_b2)
    return x

_drawn_inputs = setup_inputs


def setup_inputs(seed=0):
    import zlib

    import numpy as np

    out = dict(_drawn_inputs(seed))
    spreads = {'g_ffn': (-1.0, 0.6)}
    factors = {'L0_ffn_w1': 8.0,
     'L0_ffn_b1': 8.0,
     'L0_ffn_w2': 8.0,
     'L0_ffn_shared_w1': 8.0,
     'L0_ffn_shared_b1': 8.0,
     'L0_ffn_shared_w2': 8.0,
     'L1_ffn_rw1': 4.052,
     'L1_ffn_rw2': 3.987,
     'L1_ffn_w1': 3.534,
     'L1_ffn_b1': 8.0,
     'L1_ffn_w2': 3.335,
     'L1_ffn_b2': 4.786}
    for name, (base, spread) in spreads.items():
        noise = np.random.default_rng([zlib.crc32(name.encode()), seed]).standard_normal(out[name].shape)
        drawn = base * np.exp(spread * noise) if base else spread * noise
        out[name] = jnp.asarray(drawn.astype(out[name].dtype))
    for name, factor in factors.items():
        out[name] = (out[name] * factor).astype(out[name].dtype)
    return out
```

```python
from contextlib import ExitStack

import numpy as np

import concourse.bass as bass
from concourse import mybir

F32 = mybir.dt.float32
BF16 = mybir.dt.bfloat16
F16 = mybir.dt.float16
I32 = mybir.dt.int32
U32 = mybir.dt.uint32
ALU = mybir.AluOpType
ACT = mybir.ActivationFunctionType
AX = mybir.AxisListType

P = 128
EPS = 1e-5
FP8_MAX = 448.0
ROUND_FP8 = 1.5 * 2.0 ** 20
FP8_MIN_NORMAL = 2.0 ** -6
X_SCALE = 256.0
W_SCALE = 64.0
G_SCALE = 16.0


class Count:

    def __init__(self, sem, step=1):
        self.sem, self.step, self.n = sem, step, 0

    def on(self, instruction):
        instruction.then_inc(self.sem, self.step)
        self.n += self.step
        return self.n


CAUSAL_FILL = -1e4 * 4.0
NEVER = -1e30
Q_PART = (0, 0, 0, 1, 1, 2)
K_PART = (0, 1, 2, 0, 1, 0)


def flamingo(nc, x, ctx, ctx_t, gates2, gate_w, w1a, b1a, w2a, b2a, rw1, rw2, w1d, b1d, w2d, b2d, out):
    N, D = x.shape
    T = N // P
    KC = D // P
    E = gate_w.shape[2]
    B = 4
    S = N // B
    HT = T // 2
    CA = w1a.shape[1]

    with ExitStack() as stack:
        def sb(name, shape, dt):
            return stack.enter_context(nc.sbuf_tensor(name, shape, dt))

        def sem(name):
            return stack.enter_context(nc.semaphore(name))

        HEADS = 16
        DH = D // HEADS
        ROWS = len(Q_PART) * DH
        HID = w1d.shape[3]
        HC8 = HID // P
        PAIRS = 2 * N
        TILES = PAIRS // P + E - 1
        sorted_rows = nc.dram_tensor("sorted_rows", [TILES * P, D], U32).ap()
        routed_rows = nc.dram_tensor("routed_rows", [TILES * P, D], F32).ap()
        k_parts = nc.dram_tensor("k_parts", [3, D, N], BF16).ap()

        W1_ = sb("W1", [P, 64 * 256], F32)
        arena = sb("arena", [P, 113 * 256], F32)

        def at(kb, shape, dt):
            size = 1
            for n in shape:
                size *= n
            words = size * mybir.dt.size(dt) // 4
            o = int(kb * 256)
            v = arena[:, o:o + words].bitcast(dt) if dt != F32 else arena[:, o:o + words]
            if len(shape) == 1:
                return v
            names = "abcd"[:len(shape)]
            return v.rearrange(f"p ({' '.join(names)}) -> p {' '.join(names)}",
                               **{c: n for c, n in zip(names, shape)})

        X = sb("X", [P, T, D], F32)
        ident = sb("ident", [P, P], F32)
        ident_h = sb("ident_h", [P, P], F16)
        ident_b = sb("ident_b", [P, P], BF16)
        iota_e = sb("iota_e", [P, E], F32)
        g_raw = sb("g_raw", [P, 4], F32)
        tg = sb("tg", [P, 4], F32)
        stats = sb("stats", [P, T, 6], F32)
        mv = sb("mv", [P, T, 2], F32)
        ve = sb("ve", [P, T], F32)
        rstd0 = sb("rstd0", [P, T], F32)
        rt = sb("rt", [P, T], F32)
        rstd = sb("rstd", [P, T], F32)
        neg_half = sb("neg_half", [P, T], F32)
        KS = W1_[:, 48 * 256:60 * 256].bitcast(BF16).rearrange("p (s k n) -> p s k n", s=3, k=KC)
        KR = W1_[:, 40 * 256:48 * 256].rearrange("p (k n) -> p k n", k=KC)
        CN = W1_[:, 32 * 256:40 * 256].rearrange("p (t d) -> p t d", t=T)
        KST = [W1_[:, 56 * 256:64 * 256].bitcast(BF16).rearrange("p (h n) -> p h n", h=HEADS),
               at(68, [HEADS, S], BF16)]
        QST = [at(0, [HEADS, S], BF16), at(8, [HEADS, S], BF16)]
        HC = at(16, [2, D], F32)
        RC = at(18, [2, D], F32)
        RC2 = at(20, [2, D], F32)
        QTOK = at(22, [2, HEADS, len(Q_PART), DH], BF16)
        OT = at(28, [2, 512], F32)
        PT = at(76, [6, 512], F32)
        VA = at(89, [T, HEADS, DH + 1], F32)
        SUFV = at(97.5, [T, D], F32)
        neg_mask = sb("neg_mask", [P, P], BF16)
        after = sb("after", [P, P], F32)
        ones = sb("ones", [P, P], F32)
        hidden_n = sb("hidden_n", [P, 2], F32)
        floor = sb("floor", [P, 2], F32)
        MX = sb("MX", [P, 2, 2, HEADS], F32)
        NM = sb("NM", [P, 2, 2, HEADS], F32)
        NMR = sb("NMR", [P, 2, HEADS], F32)
        NMR2 = sb("NMR2", [P, 2, HEADS], F32)
        NMP = sb("NMP", [P, 2, 3, HEADS], BF16)
        NMS = sb("NMS", [3 * HEADS, S], BF16)
        WZ = sb("WZ", [P, 2, 2, HEADS], F32)
        WM = sb("WM", [P, 2, 2, HEADS], F32)
        DEN = sb("DEN", [P, HEADS], F32)
        DENR = sb("DENR", [P, HEADS], F32)
        HV = sb("HV", [P, 2, D], F32)
        NUM = at(111, [D], F32)
        W1 = W1_[:, :].bitcast(F16).rearrange("p (e s k n) -> p e s k n", e=E, s=2, k=KC)
        W2 = at(0, [E, 2, HC8, D], F16)
        STG = sb("STG", [P, 2, HID], F32)
        DHS = at(64, [T, D], F32)
        DHL = at(72, [T, 2, D], F16)
        DHT = at(80, [KC, 2, N], F16)
        R32 = at(88, [N], F32)
        RHL = at(92, [2, N], F16)
        GB16 = at(96, [HC8, E, 2 * E], F16)
        COEF_T = at(98, [N], F32)
        B24 = at(102, [D], F32)
        XR = at(104, [2, 2, D], F16)
        XT = at(106, [2, KC, 2, P], F16)
        YS = at(108, [2, D], F32)
        GD = at(64, [2, HID], F32)
        GDL = at(88, [2, 2, HID], F16)
        YG = at(72, [T, 2, D], F32)
        RW1R = at(110, [KC, P], F32)
        RW1 = at(111, [2, KC, P], F16)
        RW2R = sb("RW2R", [P, E], F32)
        RW2 = sb("RW2", [P, 2, E], F16)
        B1D = sb("B1D", [P, E, HC8], F32)
        GB = sb("GB", [P, E, HC8], F32)
        GBH = sb("GBH", [P, E, HC8], F16)
        GBL = sb("GBL", [P, E, HC8], F16)
        before_b = sb("before_b", [P, P], BF16)
        ones_b = sb("ones_b", [P, P], BF16)
        iota_tile = sb("iota_tile", [P, TILES], F32)
        iota_full = sb("iota_full", [P, T], F32)
        LG = at(112, [T, E], F32)
        LM = sb("LM", [P, T], F32)
        PR = at(112.25, [T, E], F32)
        DTOP = sb("DTOP", [P, T, 8], F32)
        DTOPI = sb("DTOPI", [P, T, 8], U32)
        DTOPF = sb("DTOPF", [P, T, 2], F32)
        M01 = at(112.5, [T, 2, E], F32)
        M01B = sb("M01B", [P, T, 2, E], BF16)
        MSB = sb("MSB", [P, T, E], BF16)
        NE01 = sb("NE01", [P, 2, E], F32)
        NE = sb("NE", [P, E], F32)
        USED = sb("USED", [P, E, T], F32)
        NT = sb("NT", [P, E], F32)
        ENDT = sb("ENDT", [P, E], F32)
        BASE = sb("BASE", [P, E], F32)
        SLOTQ = sb("SLOTQ", [P, T, E], F32)
        SLOTM = sb("SLOTM", [P, 2, T, E], F32)
        SLOTF = sb("SLOTF", [P, 2, T], F32)
        SLOT = sb("SLOT", [P, 2, T], U32)
        EOF_ = sb("EOF", [P, TILES, E], F32)
        EIDF = sb("EIDF", [P, TILES], F32)
        EID = sb("EID", [P, TILES], I32)
        ACTV = sb("ACTV", [P, 2, E], F32)
        COEF = sb("COEF", [P, T, 3 * E], F32)
        CF = sb("CF", [P, 2, T, E], F32)
        WKD = sb("WKD", [P, 2, T], F32)
        CT = at(0, [KC, N], F32)
        XC = at(8, [T, D], F32)
        V = at(16, [T, D], F32)
        C1 = at(24, [T, D], F32)
        XQ = at(32, [T, D], BF16)
        XQT = at(36, [2, KC, HT * P], BF16)
        VC = at(40, [KC, N], F32)
        C2 = at(48, [KC, N], F32)
        CQT = at(56, [KC, N], BF16)
        HS = at(0, [T, D], F32)
        HHL = at(8, [T, 2, D], F16)
        HT_ = at(16, [KC, 2, N], F16)
        G32 = at(24, [2, 512], F32)
        GHL = at(28, [2, CA, N], F16)
        W1A = at(68, [2, CA, KC, P], F16)
        W2A = at(78, [2, CA, D], F16)
        GWA = at(88, [2, KC, E], F16)
        WRAW = at(89, [CA * D], F32)
        WRAW2 = at(99, [CA * D], F32)
        GWR = at(109, [KC, E], F32)
        B1A = sb("B1A", [P, CA], F32)
        B9 = at(110, [D], F32)[0:E + 1]
        camax = sb("camax", [P, KC, T], F32)
        camax_all = sb("camax_all", [P, KC, T], F32)
        xamax = sb("xamax", [P, T, KC], F32)
        sx = sb("sx", [P, T, KC], F32)
        rx = sb("rx", [P, T, KC], F32)
        sw = sb("sw", [P, KC, T], F32)
        rw = sb("rw", [P, KC, T], F32)
        sxw = sb("sxw", [P, T, 2, KC], F32)
        logits = LG
        top = DTOP
        topi = DTOPI
        topf = DTOPF
        mask0 = CF[:, 0]
        mask1 = CF[:, 1]
        z12 = sb("z12", [P, T], F32)
        th = sb("th", [P, T], F32)
        wk = WKD
        gates = sb("gates", [P, T, E + 1], F32)
        gates_s = sb("gates_s", [P, T, E + 1], F32)
        gates_t = at(0, [N], F32)[0:E + 1]

        bank = [stack.enter_context(nc.psum_tensor(f"bank{i}", [P, 512], F32)) for i in range(8)]

        s1_bank, s2_bank, o_bank, qt_bank = bank[0:2], bank[2:5], bank[5:7], bank[7]
        up_bank = bank[2:6]

        s_x = [sem(f"x_landed{i}") for i in range(2)]
        s_ct = sem("ctx_t_landed")
        s_g = sem("layer_gates_landed")
        s_wl0 = sem("l0_weights_landed")
        s_const = sem("constants_made")
        s_dve = sem("dve_step")
        s_act = sem("act_step")
        s_pool = sem("pool_step")
        s_camax = sem("ctx_amax_local")
        s_camax_all = sem("ctx_amax_all")
        s_ve = sem("variance_ready")
        s_rstd0 = sem("rstd_estimated")
        s_tg = sem("tanh_gates_ready")
        s_xq = sem("x_quantised")
        s_xqt_ps = sem("xq_transposed")
        s_xqt = sem("xq_t_in_sbuf")
        s_cqt = sem("ctx_quantised")
        s_da = sem("stage_a_product")
        s_da_used = sem("stage_a_product_used")
        s_w0 = sem("l0_weights_split")
        s_hhl = sem("ln_split")
        s_hs = sem("ln_scaled")
        s_hhi = sem("ln_high")
        s_ht_ps = sem("ln_transposed")
        s_ht = sem("ln_t_in_sbuf")
        s_lg = sem("logits_product")
        s_z12 = sem("logit_gap")
        s_th = sem("tanh_gap")
        s_gates = sem("gates_ready")
        s_gt_ps = sem("gates_transposed")
        s_gt = sem("gates_t_in_sbuf")
        s_up = sem("up_product")
        s_gelu = sem("gelu_done")
        s_ghl = sem("hidden_split")
        s_down = sem("down_product")
        s_down_used = sem("down_product_used")
        s_ctx = sem("ctx_landed")
        s_kparts = sem("k_parts_split")
        s_kparts_out = sem("k_parts_stored")
        s_kst = [sem(f"k_stack_landed{i}") for i in range(2)]
        s_masks = sem("masks_made")
        s_va = sem("v_with_ones_ready")
        s_suf_ps = sem("suffix_sums_product")
        s_suf = sem("suffix_sums_ready")
        s_q1 = sem("q_parts_ready")
        s_qtok = sem("q_parts_repeated")
        s_qt_ps = sem("q_stack_transposed")
        s_qst = sem("q_stack_in_sbuf")
        s_p1 = sem("scores_for_maximum")
        s_mx = sem("maximum_taken")
        s_nmp = sem("minus_maximum_split")
        s_nm_ps = sem("minus_maximum_transposed")
        s_nms = sem("minus_maximum_in_sbuf")
        s_nmrow = sem("minus_maximum_rows_landed")
        s_wz = sem("hidden_exponent")
        s_wm = sem("hidden_weight")
        s_p2 = sem("scores_by_key")
        s_pt = sem("exponentials_ready")
        s_pv = sem("values_product")
        s_ot = sem("values_product_in_sbuf")
        s_o_ps = sem("attention_transposed")
        s_o_used = sem("attention_used")
        s_hv = sem("hidden_share_ready")
        s_obank = sem("o_banks_cleared")
        s_zero = sem("zeros_made")
        s_fill = sem("sorted_rows_cleared")
        s_dw_small = sem("d_small_weights_landed")
        s_stg = [sem(f"weights_landed{i}") for i in range(2)]
        s_wscaled = sem("weights_scaled")
        s_whi = sem("weights_high")
        s_wlo = sem("weights_low")
        s_wlate_hi = sem("late_weights_high")
        s_wlate = sem("late_weights_low")
        s_dconst = sem("d_constants_made")
        s_rw = sem("router_weights_split")
        s_rwh = sem("router_weights_high")
        s_dhs = sem("d_ln_scaled")
        s_dhhi = sem("d_ln_high")
        s_dhl = sem("d_ln_split")
        s_dt_ps = sem("d_ln_transposed")
        s_dht = sem("d_ln_t_in_sbuf")
        s_r = sem("router_hidden_product")
        s_rg = sem("router_gelu")
        s_rhl = sem("router_hidden_split")
        s_dlg = sem("router_logits")
        s_dl = sem("router_logits_less_max")
        s_ex = sem("router_exponentials")
        s_m = sem("choice_masks")
        s_rank = sem("ranks_counted")
        s_slot = sem("slots_ready")
        s_eid = sem("tile_experts_ready")
        s_scat = sem("rows_scattered")
        s_gb = sem("gelu_of_b1")
        s_gbp = sem("gelu_of_b1_parts")
        s_gb16 = sem("gelu_of_b1_spread")
        s_ce = sem("idle_outputs_product")
        s_ce_sb = sem("idle_outputs_in_sbuf")
        s_coef = sem("coefficients_ready")
        s_cf_ps = sem("coefficients_transposed")
        s_cf = sem("coefficients_t_in_sbuf")
        s_base = sem("idle_share_product")
        s_base_used = sem("idle_share_added")
        s_xr = [sem(f"tile_rows_landed{i}") for i in range(2)]
        s_xt_ps = sem("tile_rows_transposed")
        s_xt = sem("tile_rows_t_in_sbuf")
        s_dup = sem("tile_up_product")
        s_dg = sem("tile_gelu")
        s_dgh = sem("tile_hidden_high")
        s_dgl = sem("tile_hidden_split")
        s_dd = sem("tile_down_product")
        s_ys = sem("tile_output_in_sbuf")
        s_yst = [sem(f"tile_output_stored{i}") for i in range(2)]
        s_yg = [sem(f"routed_rows_gathered{t}") for t in range(T)]
        s_x3_done = sem("x3_ready")
        s_xout = sem("out_tile_ready")
        s_out_ready = sem("out_ready")
        s_out = sem("out_stored")

        block = stack.enter_context(nc.Block())
        DOWN_BANKS = 4
        BLOCKS = 4 * E
        ORDER = ([("w1", e) for e in range(E - 1)] + [("w2", e) for e in range(E // 2, E)]
                 + [("w1", E - 1)] + [("w2", e) for e in range(E // 2)])
        EARLY, MIDDLE = 2 * (E - 1), 2 * (E - 1) + E

        def weight_block(i):
            (which, e), half = ORDER[i // 2], i % 2
            if which == "w1":
                return w1d[:, e, half], W1[:, e, 0, half], W1[:, e, 1, half]
            cs = slice(half * HC8 // 2, (half + 1) * HC8 // 2)
            flat = lambda a: a.rearrange("p c d -> p (c d)")
            return flat(w2d[:, e, cs]), flat(W2[:, e, 0, cs]), flat(W2[:, e, 1, cs])

        DOWNS = T * CA // 2

        @block.sync
        def _(sp):
            def load_weights(i):
                if i >= 2:
                    done_before = i - 1
                    if done_before <= MIDDLE:
                        sp.wait_ge(s_wlo, done_before)
                    else:
                        sp.wait_ge(s_wlate, done_before - MIDDLE)
                sp.dma_start(STG[:, i % 2], weight_block(i)[0]).then_inc(s_stg[i % 2], 16)

            for h in range(2):
                sp.dma_start(X[:, h * HT:(h + 1) * HT, :],
                             x[h * HT * P:(h + 1) * HT * P, :].rearrange("(t p) d -> p t d", p=P)
                             ).then_inc(s_x[h], 16)
            sp.dma_start(WRAW, w1a.rearrange("p c k h -> p (c k h)")).then_inc(s_wl0, 16)
            sp.dma_start(WRAW2, w2a.rearrange("p c d -> p (c d)")).then_inc(s_wl0, 16)
            sp.dma_start(B9[:, :], b2a).then_inc(s_wl0, 16)
            sp.dma_start(CN, ctx.rearrange("(t p) d -> p t d", p=P)).then_inc(s_ctx, 16)
            for i in range(2):
                load_weights(i)
            sp.wait_ge(s_zero, 1)
            sp.dma_start(sorted_rows.rearrange("(t p) d -> p t d", p=P),
                         HV[:, 0].bitcast(U32).unsqueeze(1).broadcast_to([P, TILES, D])).then_inc(s_fill, 16)
            sp.wait_ge(s_kparts, 3)
            for k in range(KC):
                sp.dma_start(k_parts[:, k * P:(k + 1) * P, :].rearrange("s p n -> p s n"),
                             KS[:, :, k]).then_inc(s_kparts_out, 16)
            for i in range(2, 6):
                load_weights(i)
            sp.wait_ge(s_kparts_out, 16 * KC)

            def load_k_stack(b):
                for r, s in enumerate(K_PART):
                    sp.dma_start(KST[b % 2][r * DH:(r + 1) * DH],
                                 k_parts[s, :, b * S:(b + 1) * S].rearrange("(h d) n -> d h n", d=DH)
                                 ).then_inc(s_kst[b % 2], 16)

            load_k_stack(0)
            for i in range(6, EARLY):
                load_weights(i)
            sp.wait_ge(s_down, DOWNS)
            load_k_stack(1)
            for i in range(EARLY, EARLY + 2):
                load_weights(i)
            for b in range(2, B):
                sp.wait_ge(s_p2, 12 * (b - 1))
                load_k_stack(b)
                for i in range(EARLY + 2 + 4 * (b - 2), min(EARLY + 6 + 4 * (b - 2), MIDDLE)):
                    load_weights(i)
            for i in range(MIDDLE, BLOCKS):
                load_weights(i)
            sp.wait_ge(s_scat, 16 * 2 * T)

            def load_tile(j, q, first=False):
                if not first:
                    sp.wait_ge(s_xt_ps, j - 1)
                sp.dma_start(XR[:, q].rearrange("p s d -> p (s d)").bitcast(U32),
                             sorted_rows[bass.ds(j * P, P), :]).then_inc(s_xr[q], 16)

            def store_tile(j, q):
                sp.wait_ge(s_ys, j + 1)
                sp.dma_start(routed_rows[bass.ds(j * P, P), :], YS[:, q]).then_inc(s_yst[q], 16)

            load_tile(0, 0, first=True)
            load_tile(1, 1, first=True)
            with sp.Fori(1, TILES // 2) as i:
                for q in range(2):
                    load_tile(2 * i + q, q)
                    store_tile(2 * i + q - 2, q)
            load_tile(TILES - 1, 0)
            for j in range(TILES - 3, TILES):
                store_tile(j, j % 2)
            for t in range(T):
                sp.wait_ge(s_xout, t + 1)
                sp.dma_start(out[t * P:(t + 1) * P, :], X[:, t, :]).then_inc(s_out, 16)
            sp.wait_ge(s_out, 16 * T)

        @block.gpsimd
        def _(pool):
            done = Count(s_pool)
            nc.gpsimd.memset(ident[:, :], 0.0).then_inc(s_pool, 1)
            nc.gpsimd.memset(neg_half[:, :], -0.5).then_inc(s_const, 1)
            nc.gpsimd.iota(iota_e[:, :], [[1, E]], base=0, channel_multiplier=0,
                           allow_small_or_imprecise_dtypes=True).then_inc(s_const, 1)
            pool.wait_ge(s_pool, 1)
            nc.gpsimd.affine_select(out=ident[:, :], in_=ident[:, :], compare_op=ALU.not_equal,
                                    fill=1.0, base=0, pattern=[[-1, P]],
                                    channel_multiplier=1).then_inc(s_const, 1)
            pool.wait_ge(s_const, 3)
            nc.gpsimd.tensor_copy(ident_h[:, :], ident[:, :]).then_inc(s_const, 1)
            nc.gpsimd.tensor_copy(ident_b[:, :], ident[:, :]).then_inc(s_const, 1)
            done.n = 1
            nc.gpsimd.memset(HV[:, 0], 0.0).then_inc(s_zero, 1)
            nc.gpsimd.memset(neg_mask[:, :], 0.0).then_inc(s_pool, 1)
            nc.gpsimd.memset(ones[:, :], 1.0).then_inc(s_pool, 1)
            nc.gpsimd.iota(hidden_n[:, :], [[-P, 2]], base=S - 1, channel_multiplier=-1,
                           allow_small_or_imprecise_dtypes=True).then_inc(s_masks, 1)
            nc.gpsimd.memset(floor[:, :], CAUSAL_FILL).then_inc(s_pool, 1)
            done.n = 4
            pool.wait_ge(s_pool, 4)
            nc.gpsimd.affine_select(out=neg_mask[:, :], in_=neg_mask[:, :], compare_op=ALU.is_ge, fill=NEVER,
                                    base=0, pattern=[[-1, P]], channel_multiplier=1).then_inc(s_masks, 1)
            nc.gpsimd.affine_select(out=after[:, :], in_=ones[:, :], compare_op=ALU.is_gt, fill=0.0,
                                    base=0, pattern=[[-1, P]], channel_multiplier=1).then_inc(s_masks, 1)
            nc.gpsimd.affine_select(out=floor[:, 1:2], in_=floor[:, 1:2], compare_op=ALU.not_equal, fill=-3e38,
                                    base=1 - P, pattern=[[0, 1]], channel_multiplier=1).then_inc(s_masks, 1)
            pool.wait_ge(s_camax, 1)
            nc.gpsimd.partition_all_reduce(camax_all[:, :, :].rearrange("p a b -> p (a b)"),
                                           camax[:, :, :].rearrange("p a b -> p (a b)"), P,
                                           bass.bass_isa.ReduceOp.max).then_inc(s_camax_all, 1)

            def hidden_share(b):
                pool.wait_ge(s_wm, b + 1)
                pool.wait_ge(s_suf, T // 2)
                if b:
                    pool.wait_ge(s_o_used, 2 * b)
                for i in range(2):
                    nc.gpsimd.tensor_tensor(
                        HV[:, i].rearrange("p (h d) -> p h d", h=HEADS),
                        SUFV[:, 2 * b + i].rearrange("p (h d) -> p h d", h=HEADS),
                        WM[:, b % 2, i].unsqueeze(2).broadcast_to([P, HEADS, DH]), ALU.mult).then_inc(s_hv, 1)

            def estimate_rstd(n, h):
                pool.wait_ge(s_ve, n + 1)
                ts = slice(h * HT, (h + 1) * HT)
                nc.gpsimd.tensor_tensor(rstd0[:, ts], ve[:, ts], neg_half[:, ts],
                                        ALU.pow).then_inc(s_rstd0, 1)

            for h in range(2):
                estimate_rstd(h, h)
            pool.wait_ge(s_ct, 16)
            nc.gpsimd.tensor_copy(KS[:, 0], CT).then_inc(s_kparts, 1)
            pool.wait_ge(s_kparts, 1)
            nc.gpsimd.tensor_tensor(KR, CT, KS[:, 0], ALU.subtract).then_inc(s_pool, 1)
            pool.wait_ge(s_pool, 5)
            nc.gpsimd.tensor_copy(KS[:, 1], KR).then_inc(s_kparts, 1)
            pool.wait_ge(s_kparts, 2)
            nc.gpsimd.tensor_tensor(KS[:, 2], KR, KS[:, 1], ALU.subtract).then_inc(s_kparts, 1)
            done.n = 5
            def weights_low(i):
                _, hi, lo = weight_block(i)
                pool.wait_ge(s_whi, i + 1)
                nc.gpsimd.tensor_tensor(lo, STG[:, i % 2], hi, ALU.subtract).then_inc(s_wlo, 1)

            for i in range(6):
                weights_low(i)
            for h in range(2):
                estimate_rstd(2 + h, h)
            pool.wait_ge(s_w0, 3)
            pool.wait_ge(s_ctx, 16)
            nc.gpsimd.memset(VA[:, :, :, DH:DH + 1], 1.0).then_inc(s_va, 1)
            nc.gpsimd.tensor_copy(VA[:, :, :, 0:DH], CN.rearrange("p t (h d) -> p t h d", h=HEADS)
                                  ).then_inc(s_va, 1)
            pool.wait_ge(s_kparts_out, 16 * KC)
            pool.wait_ge(s_va, 2)
            nc.gpsimd.memset(KST[0][ROWS:ROWS + 3], 1.0).then_inc(s_va, 1)
            pool.wait_ge(s_va, 3)
            for i in range(6, EARLY):
                weights_low(i)
            pool.wait_ge(s_down, DOWNS)
            pool.wait_ge(s_wlo, EARLY)
            nc.gpsimd.memset(KST[1][ROWS:ROWS + 3], 1.0).then_inc(s_va, 1)
            pool.wait_ge(s_va, 4)
            for b in range(B):
                pool.wait_ge(s_ve, 4 + b + 1)
                ts = slice(2 * b, 2 * b + 2)
                nc.gpsimd.tensor_tensor(rstd0[:, ts], ve[:, ts], neg_half[:, ts], ALU.pow).then_inc(s_rstd0, 1)
                if b:
                    hidden_share(b - 1)
                    for i in range(EARLY + 2 * b - 2, EARLY + 2 * b):
                        weights_low(i)
            hidden_share(B - 1)
            for i in range(MIDDLE - 2, MIDDLE):
                weights_low(i)
            pool.wait_ge(s_pool, 5)
            nc.gpsimd.iota(iota_tile[:, :], [[1, TILES]], base=0, channel_multiplier=0,
                           allow_small_or_imprecise_dtypes=True).then_inc(s_dconst, 1)
            nc.gpsimd.iota(iota_full[:, :], [[P, T]], base=0, channel_multiplier=0,
                           allow_small_or_imprecise_dtypes=True).then_inc(s_dconst, 1)
            nc.gpsimd.tensor_copy(ones_b[:, :], ones[:, :]).then_inc(s_dconst, 1)
            nc.gpsimd.affine_select(out=before_b[:, :], in_=ones[:, :], compare_op=ALU.is_gt, fill=0.0,
                                    base=0, pattern=[[1, P]], channel_multiplier=-1).then_inc(s_dconst, 1)
            for h in range(2):
                estimate_rstd(8 + h, h)
            pool.wait_ge(s_fill, 16)
            pool.wait_ge(s_slot, 1)
            pool.wait_ge(s_dhl, T)
            pool.wait_ge(s_dhhi, T)
            for t in range(T):
                for k in range(2):
                    pool.indirect_dma_start(sorted_rows[:, :],
                                            bass.IndirectOffsetOnAxis(ap=SLOT[:, k, t:t + 1], axis=0),
                                            DHL[:, t].rearrange("p s d -> p (s d)").bitcast(U32), None
                                            ).then_inc(s_scat, 16)
            for q in range(2):
                pool.wait_ge(s_yst[q], 16 * ((TILES + 1 - q) // 2))
            for t in range(T):
                for k in range(2):
                    pool.indirect_dma_start(YG[:, t, k], None, routed_rows[:, :],
                                            bass.IndirectOffsetOnAxis(ap=SLOT[:, k, t:t + 1], axis=0)
                                            ).then_inc(s_yg[t], 16)

        @block.scalar
        def _(act):
            done = Count(s_act)
            act.dma_start(CT, ctx_t).then_inc(s_ct, 16)
            act.dma_start(g_raw[:, :], gates2.partition_broadcast(P)).then_inc(s_g, 16)
            act.dma_start(GWR, gate_w).then_inc(s_wl0, 16)
            act.dma_start(B1A[:, :], b1a).then_inc(s_wl0, 16)
            act.wait_ge(s_g, 16)
            nc.scalar.activation(tg[:, :], g_raw[:, :], ACT.Tanh).then_inc(s_tg, 1)
            act.wait_ge(s_wl0, 80)
            for raw, dst in ((WRAW, W1A[:, 0].rearrange("p c k h -> p (c k h)")),
                             (WRAW2, W2A[:, 0].rearrange("p c d -> p (c d)")),
                             (GWR.rearrange("p k e -> p (k e)"), GWA[:, 0].rearrange("p k e -> p (k e)"))):
                nc.scalar.activation(dst, raw, ACT.Copy, scale=W_SCALE).then_inc(s_act, 1)
            done.n = 3
            def weights_high(i):
                _, hi, _ = weight_block(i)
                if i == 8:
                    act.wait_ge(s_va, 2)
                    act.wait_ge(s_suf_ps, T // 2)
                    act.wait_ge(s_kparts_out, 16 * KC)
                if i == EARLY:
                    act.wait_ge(s_down, DOWNS)
                act.wait_ge(s_stg[i % 2], 16 * (i // 2 + 1))
                nc.scalar.activation(STG[:, i % 2], STG[:, i % 2], ACT.Copy, scale=W_SCALE).then_inc(s_wscaled, 1)
                act.wait_ge(s_wscaled, i + 1)
                nc.scalar.activation(hi, STG[:, i % 2], ACT.Copy).then_inc(s_whi, 1)

            for i in range(3):
                weights_high(i)
            for h in range(2):
                act.wait_ge(s_xqt_ps, h + 1)
                nc.scalar.activation(XQT[:, h].rearrange("p k n -> p (k n)"), bank[h][:, :].bitcast(BF16),
                                     ACT.Copy).then_inc(s_xqt, 1)
            for i in range(3, 6):
                weights_high(i)
            act.wait_ge(s_w0, 3)
            for j in range(T // 2):
                act.wait_ge(s_suf_ps, j + 1)
                nc.scalar.activation(SUFV[:, 2 * j:2 * j + 2].rearrange("p t d -> p (t d)"), bank[4 + j][:, :],
                                     ACT.Copy).then_inc(s_suf, 1)
            for t in range(T):
                act.wait_ge(s_hs, t + 1)
                nc.scalar.activation(HHL[:, t, 0], HS[:, t], ACT.Copy).then_inc(s_hhi, 1)
                if t % 2:
                    j = t // 2
                    act.wait_ge(s_ht_ps, j + 1)
                    nc.scalar.activation(
                        HT_[:, :, :, j * 2 * P:(j + 1) * 2 * P].rearrange("p k s (t n) -> p t (k s) n", t=2),
                        bank[j][:, :].bitcast(F16).rearrange("p (t a n) -> p t a n", t=2, n=P),
                        ACT.Copy).then_inc(s_ht, 1)
            act.wait_ge(s_z12, 1)
            nc.scalar.activation(th[:, :], z12[:, :], ACT.Tanh,
                                 scale=0.5 / (X_SCALE * W_SCALE)).then_inc(s_th, 1)
            for i in range(2 * CA):
                c = i % CA
                act.wait_ge(s_up, i + 1)
                if i >= 2:
                    act.wait_ge(s_ghl, i - 1)
                nc.scalar.activation(G32[:, i % 2], bank[i % 4][:, :], ACT.Gelu, bias=B1A[:, c:c + 1],
                                     scale=1.0 / (X_SCALE * W_SCALE)).then_inc(s_gelu, 1)
                if i % 5 == 3:
                    weights_high(6 + i // 5)
            for i in range(10, EARLY):
                weights_high(i)
            def repeat_parts(b):
                for i in range(2):
                    act.wait_ge(s_q1, 2 * b + i + 1)
                    nc.scalar.activation(QTOK[:, i, :, 1:3], QTOK[:, i, :, 0:1].broadcast_to([P, HEADS, 2, DH]),
                                         ACT.Copy).then_inc(s_qtok, 1)
                    nc.scalar.activation(QTOK[:, i, :, 4:5], QTOK[:, i, :, 3:4], ACT.Copy).then_inc(s_qtok, 1)

            def store_q(b, j):
                if b >= 2 and j == 0:
                    act.wait_ge(s_p2, 12 * (b - 1))
                act.wait_ge(s_qt_ps, 4 * b + j + 1)
                i, h0 = j // 2, 8 * (j % 2)
                nc.scalar.activation(QST[b % 2][0:ROWS, h0:h0 + 8, i * P:(i + 1) * P],
                                     qt_bank[:, :].bitcast(BF16)[0:ROWS].rearrange("p (h n) -> p h n", h=8),
                                     ACT.Copy).then_inc(s_qst, 1)

            def store_minus_max(b):
                act.wait_ge(s_nm_ps, b + 1)
                if b:
                    act.wait_ge(s_nmrow, 48 * b)
                nc.scalar.activation(NMS[:, :], qt_bank[:, :].bitcast(BF16)[0:3 * HEADS, 0:S],
                                     ACT.Copy).then_inc(s_nms, 1)
                act.wait_ge(s_nms, b + 1)
                for s in range(3):
                    act.dma_start(QST[b % 2][ROWS + s:ROWS + s + 1], NMS[s * HEADS:(s + 1) * HEADS, :]
                                  ).then_inc(s_nmrow, 16)

            def hidden_weight(b):
                act.wait_ge(s_wz, b + 1)
                if b >= 2:
                    act.wait_ge(s_o_used, 2 * (b - 1))
                nc.scalar.activation(WM[:, b % 2].rearrange("p i h -> p (i h)"),
                                     WZ[:, b % 2].rearrange("p i h -> p (i h)"), ACT.Exp,
                                     scale=0.25).then_inc(s_wm, 1)

            def exponentials(b, u):
                n = 12 * b + u
                act.wait_ge(s_p2, n + 1)
                if n >= 6:
                    act.wait_ge(s_pv, (n - 6) // 3 + 1)
                nc.scalar.activation(PT[:, n % 6], s2_bank[n % 3][:, :], ACT.Exp, scale=0.25).then_inc(s_pt, 1)

            def store_o(b, j):
                act.wait_ge(s_pv, 4 * b + 2 * j + 2)
                if b:
                    act.wait_ge(s_o_ps, 2 * b)
                nc.scalar.activation(OT[:, j], o_bank[j][:, :], ACT.Copy).then_inc(s_ot, 1)

            repeat_parts(0)
            for j in range(4):
                store_q(0, j)
            store_minus_max(0)
            hidden_weight(0)
            for b in range(B):
                if b + 1 < B:
                    repeat_parts(b + 1)
                for u in range(12):
                    if b + 1 < B and u < 4:
                        store_q(b + 1, u)
                    exponentials(b, u)
                    if u == 8:
                        store_o(b, 0)
                    if u in (5, 10):
                        weights_high(EARLY + 2 * b + u // 10)
                store_o(b, 1)
                if b + 1 < B:
                    store_minus_max(b + 1)
                    hidden_weight(b + 1)
            for src, dst in ((rw1, RW1R), (rw2, RW2R[:, :]), (b1d, B1D[:, :, :]), (b2d, B24[2 * E:3 * E, :])):
                act.dma_start(dst, src).then_inc(s_dw_small, 16)
            for t in range(T):
                act.wait_ge(s_dhs, t + 1)
                nc.scalar.activation(DHL[:, t, 0], DHS[:, t], ACT.Copy).then_inc(s_dhhi, 1)
                if t % 2:
                    j = t // 2
                    act.wait_ge(s_dt_ps, j + 1)
                    nc.scalar.activation(
                        DHT[:, :, :, j * 2 * P:(j + 1) * 2 * P].rearrange("p k s (t n) -> p t (k s) n", t=2),
                        bank[j][:, :].bitcast(F16).rearrange("p (t a n) -> p t a n", t=2, n=P),
                        ACT.Copy).then_inc(s_dht, 1)
                if t == 0:
                    act.wait_ge(s_dw_small, 64)
                    nc.scalar.activation(RW1[:, 0].rearrange("p k h -> p (k h)"),
                                         RW1R.rearrange("p k h -> p (k h)"), ACT.Copy,
                                         scale=W_SCALE).then_inc(s_rwh, 1)
                    nc.scalar.activation(RW2[:, 0], RW2R[:, :], ACT.Copy, scale=W_SCALE).then_inc(s_rwh, 1)
            for h in range(2):
                act.wait_ge(s_r, h + 1)
                nc.scalar.activation(R32[:, h * 512:(h + 1) * 512], bank[4 + h][:, :], ACT.Gelu,
                                     scale=1.0 / (X_SCALE * W_SCALE)).then_inc(s_rg, 1)
            nc.scalar.activation(GB[:, :, :], B1D[:, :, :], ACT.Gelu).then_inc(s_gb, 1)
            act.wait_ge(s_dl, 1)
            nc.scalar.activation(PR[:, :, :], LG[:, :, :], ACT.Exp,
                                 scale=1.0 / (G_SCALE * W_SCALE)).then_inc(s_ex, 1)
            act.wait_ge(s_x3_done, 1)
            for i in range(MIDDLE, BLOCKS):
                _, hi, _ = weight_block(i)
                act.wait_ge(s_stg[i % 2], 16 * (i // 2 + 1))
                nc.scalar.activation(hi, STG[:, i % 2], ACT.Copy, scale=W_SCALE).then_inc(s_wlate_hi, 1)

            def tile_gelu(j, q, first=False):
                e = act.value_load(EID[0:1, bass.ds(j, 1)], min_val=0, max_val=E - 1)
                for hb in range(2):
                    act.wait_ge(s_dup, 2 * j + hb + 1)
                    if not first:
                        act.wait_ge(s_dgl, 2 * j + hb - 3)
                    for c in range(4 * hb, 4 * hb + 4):
                        ins = nc.scalar.activation(GD[:, q, c * P:(c + 1) * P],
                                                   up_bank[2 * q + hb][:, (c % 4) * P:(c % 4 + 1) * P], ACT.Gelu,
                                                   bias=B1D[:, e, c:c + 1], scale=1.0 / (X_SCALE * W_SCALE))
                    ins.then_inc(s_dg, 1)

            act.wait_ge(s_eid, 1)
            act.wait_ge(s_base_used, T)
            tile_gelu(0, 0, first=True)
            tile_gelu(1, 1, first=True)
            with act.Fori(1, TILES // 2) as i:
                for q in range(2):
                    tile_gelu(2 * i + q, q)
            tile_gelu(TILES - 1, 0)

        @block.tensor
        def _(pe):
            pe.wait_ge(s_const, 5)
            for h in range(2):
                pe.wait_ge(s_xq, h + 1)
                v = bank[h][:, :].bitcast(BF16).rearrange("p (k t n) -> p k t n", k=KC, t=HT)
                for t in range(HT):
                    for k in range(KC):
                        mm = nc.tensor.transpose(v[:, k, t], XQ[:, h * HT + t, k * P:(k + 1) * P], ident_b[:, :])
                mm.then_inc(s_xqt_ps, 1)
            for t in range(T):
                if t % HT == 0:
                    pe.wait_ge(s_xqt, t // HT + 1)
                if t == 0:
                    pe.wait_ge(s_cqt, 1)
                if t >= 4:
                    pe.wait_ge(s_da_used, t - 3)
                b = t // 2
                for k in range(KC):
                    mm = nc.tensor.matmul(bank[4 + t % 4][:, k * D:(k + 1) * D],
                                          XQT[:, t // HT, k, (t % HT) * P:(t % HT + 1) * P],
                                          CQT[:, k, b * S:(b + 1) * S], start=True, stop=True)
                mm.then_inc(s_da, 1)
            pe.wait_ge(s_da_used, T)
            pe.wait_ge(s_ctx, 16)
            pe.wait_ge(s_masks, 4)
            for t in range(T):
                o = bank[4 + t // 2][:, (t % 2) * D:(t % 2 + 1) * D]
                mm = nc.tensor.matmul(o, after[:, :], CN[:, t], start=True, stop=bool(t % 2))
                if t % 2 == 0:
                    nc.tensor.matmul(o, ones[:, :], CN[:, t + 1], start=False, stop=True)
                else:
                    mm.then_inc(s_suf_ps, 1)
            for t in range(T):
                pe.wait_ge(s_hhl, t + 1)
                pe.wait_ge(s_hhi, t + 1)
                v = bank[t // 2][:, :].bitcast(F16).rearrange("p (t k s n) -> p t k s n", t=2, k=KC, s=2)
                for k in range(KC):
                    for s in range(2):
                        mm = nc.tensor.transpose(v[:, t % 2, k, s], HHL[:, t, s, k * P:(k + 1) * P],
                                                 ident_h[:, :])
                if t % 2:
                    mm.then_inc(s_ht_ps, 1)
            pe.wait_ge(s_w0, 3)
            pe.wait_ge(s_act, 3)
            pe.wait_ge(s_suf, T // 2)
            passes = ((0, 0), (0, 1), (1, 0))
            for t in range(T):
                if t % 2 == 0:
                    pe.wait_ge(s_ht, t // 2 + 1)
                n = 0
                for a, b in passes:
                    for k in range(KC):
                        mm = nc.tensor.matmul(bank[4][:, t * E:(t + 1) * E], HT_[:, k, a, t * P:(t + 1) * P],
                                              GWA[:, b, k], start=(n == 0), stop=(n == 5))
                        n += 1
            mm.then_inc(s_lg, 1)
            for i in range(2 * CA):
                c, h = i % CA, i // CA
                if i >= 4:
                    pe.wait_ge(s_gelu, i - 3)
                n = 0
                for a, b in passes:
                    for k in range(KC):
                        mm = nc.tensor.matmul(bank[i % 4][:, :], W1A[:, b, c, k],
                                              HT_[:, k, a, h * 512:(h + 1) * 512],
                                              start=(n == 0), stop=(n == 5))
                        n += 1
                mm.then_inc(s_up, 1)
                if i == 12:
                    pe.wait_ge(s_gates, 1)
                    for t in range(T):
                        mm = nc.tensor.transpose(bank[5 + t // 4][0:E + 1, (t % 4) * P:(t % 4 + 1) * P],
                                                 gates[:, t], ident[:, :])
                    mm.then_inc(s_gt_ps, 1)
            pe.wait_ge(s_gt, 1)
            n = 0
            for t in range(T):
                if t % HT == 0:
                    pe.wait_ge(s_ghl, CA * (t // HT + 1))
                for c in range(0, CA, 2):
                    if n >= DOWN_BANKS:
                        pe.wait_ge(s_down_used, n - DOWN_BANKS + 1)
                    dst = bank[4 + n % DOWN_BANKS]
                    shared = c >= E
                    q = 0
                    for cc in (c, c + 1):
                        o = dst[:, 0:D] if shared else dst[:, (cc - c) * D:(cc - c + 1) * D]
                        for a, b in passes:
                            last = q == (6 if shared else 3) - 1
                            mm = nc.tensor.matmul(o, GHL[:, a, cc, t * P:(t + 1) * P], W2A[:, b, cc],
                                                  start=(q == 0), stop=(last and not shared))
                            q += 1
                        if not shared:
                            q = 0
                    if shared:
                        mm = nc.tensor.matmul(dst[:, 0:D], gates_t[:, t * P:(t + 1) * P], B9[:, :],
                                              start=False, stop=True)
                    mm.then_inc(s_down, 1)
                    n += 1

            def transpose_q(b, j):
                i, h0 = j // 2, 8 * (j % 2)
                if j % 2 == 0:
                    pe.wait_ge(s_qtok, 4 * b + 2 * i + 2)
                if b or j:
                    pe.wait_ge(s_qst, 4 * b + j)
                if b and j == 0:
                    pe.wait_ge(s_nms, b)
                    if b >= 2:
                        pe.wait_ge(s_o_used, 2 * (b - 1))
                v = qt_bank[:, :].bitcast(BF16).rearrange("p (h n) -> p h n", h=8)
                for h in range(8):
                    mm = nc.tensor.transpose(v[0:ROWS, h], QTOK[:, i, h0 + h].rearrange("p r d -> p (r d)"),
                                             ident_b[:, :])
                mm.then_inc(s_qt_ps, 1)

            def scores_for_max(b, u):
                n = 12 * b + u
                if u == 0:
                    pe.wait_ge(s_kst[b % 2], 96 * (b // 2 + 1))
                    pe.wait_ge(s_qst, 4 * b + 2)
                if u == 4:
                    pe.wait_ge(s_qst, 4 * b + 4)
                if n >= 2:
                    pe.wait_ge(s_mx, n - 1)
                i = 0 if u < 4 else 1
                nh, nk = (4, P) if i == 0 else (2, S)
                h0 = 4 * u if i == 0 else 2 * (u - 4)
                v = s1_bank[n % 2][:, :].rearrange("p (h n) -> p h n", h=nh)
                nc.tensor.matmul(v[:, :, nk - P:nk], ident_b[:, :],
                                 neg_mask[:, :].unsqueeze(1).broadcast_to([P, nh, P]),
                                 start=True, stop=False, skip_group_check=True)
                for h in range(nh):
                    mm = nc.tensor.matmul(v[:, h], QST[b % 2][0:ROWS, h0 + h, i * P:(i + 1) * P],
                                          KST[b % 2][0:ROWS, h0 + h, 0:nk], start=False, stop=h == nh - 1,
                                          skip_group_check=True)
                mm.then_inc(s_p1, 1)

            def transpose_minus_max(b):
                pe.wait_ge(s_nmp, b + 1)
                pe.wait_ge(s_qst, 4 * b + 4)
                v = qt_bank[:, :].bitcast(BF16)
                if b:
                    pe.wait_ge(s_o_used, 2 * b)
                for i in range(2):
                    mm = nc.tensor.transpose(v[0:3 * HEADS, i * P:(i + 1) * P],
                                             NMP[:, i].rearrange("p s h -> p (s h)"), ident_b[:, :])
                mm.then_inc(s_nm_ps, 1)

            def scores_by_key(b, u):
                n = 12 * b + u
                g, w = u // 3, u % 3
                if u == 0:
                    pe.wait_ge(s_nmrow, 48 * (b + 1))
                if n >= 3:
                    pe.wait_ge(s_pt, n - 2)
                k, nh, nq = (0, 2, S) if w < 2 else (1, 4, P)
                h0 = 4 * g + (2 * w if w < 2 else 0)
                v = s2_bank[n % 3][:, :].rearrange("p (h n) -> p h n", h=nh)
                nc.tensor.matmul(v[:, :, 0:P], neg_mask[:, :], ident_b[:, :].unsqueeze(1).broadcast_to([P, nh, P]),
                                 start=True, stop=False, skip_group_check=True)
                for h in range(nh):
                    mm = nc.tensor.matmul(v[:, h], KST[b % 2][0:ROWS + 3, h0 + h, k * P:(k + 1) * P],
                                          QST[b % 2][0:ROWS + 3, h0 + h, k * P:S], start=False, stop=h == nh - 1,
                                          skip_group_check=True)
                mm.then_inc(s_p2, 1)

            def weighted_values(b, g):
                n = 12 * b + 3 * g
                pe.wait_ge(s_pt, n + 3)
                if g % 2 == 0 and b:
                    pe.wait_ge(s_ot, 2 * (b - 1) + g // 2 + 1)
                c0 = (g % 2) * S
                ob = o_bank[g // 2]
                for j in range(4):
                    p = PT[:, (n + j // 2) % 6].rearrange("p (h n) -> p h n", h=2)[:, j % 2]
                    nc.tensor.matmul(ob[32 * j:32 * j + DH + 1, c0:c0 + S], VA[:, 2 * b, 4 * g + j], p,
                                     start=True, stop=False, skip_group_check=True)
                for j in range(4):
                    p = PT[:, (n + 2) % 6].rearrange("p (h n) -> p h n", h=4)[:, j]
                    mm = nc.tensor.matmul(ob[32 * j:32 * j + DH + 1, c0 + P:c0 + S], VA[:, 2 * b + 1, 4 * g + j],
                                          p, start=False, stop=True, skip_group_check=True)
                mm.then_inc(s_pv, 1)

            def transpose_o(b, i):
                pe.wait_ge(s_ot, 2 * b + 2)
                if i:
                    pe.wait_ge(s_o_used, 2 * b + i)
                elif b + 1 < B:
                    pe.wait_ge(s_qst, 4 * b + 8)
                else:
                    pe.wait_ge(s_nms, B)
                for g in range(4):
                    c0 = (g % 2) * S + i * P
                    mm = nc.tensor.transpose(qt_bank[:, g * P:(g + 1) * P], OT[:, g // 2, c0:c0 + P], ident[:, :])
                mm.then_inc(s_o_ps, 1)

            pe.wait_ge(s_down_used, DOWNS)
            pe.wait_ge(s_va, 4)
            pe.wait_ge(s_obank, 2)
            for j in range(4):
                transpose_q(0, j)
            for u in range(12):
                scores_for_max(0, u)
            transpose_minus_max(0)
            for b in range(B):
                for u in range(12):
                    if b + 1 < B and u < 4:
                        transpose_q(b + 1, u)
                    if b + 1 < B and u >= 4:
                        scores_for_max(b + 1, u - 4)
                    scores_by_key(b, u)
                    if u % 3 == 2 and u >= 5:
                        weighted_values(b, u // 3 - 1)
                if b + 1 < B:
                    for u in range(8, 12):
                        scores_for_max(b + 1, u)
                weighted_values(b, 3)
                for i in range(2):
                    transpose_o(b, i)
                if b + 1 < B:
                    transpose_minus_max(b + 1)
            pe.wait_ge(s_x3_done, 1)
            for t in range(T):
                pe.wait_ge(s_dhl, t + 1)
                pe.wait_ge(s_dhhi, t + 1)
                v = bank[t // 2][:, :].bitcast(F16).rearrange("p (t k s n) -> p t k s n", t=2, k=KC, s=2)
                for k in range(KC):
                    for s in range(2):
                        mm = nc.tensor.transpose(v[:, t % 2, k, s], DHL[:, t, s, k * P:(k + 1) * P],
                                                 ident_h[:, :])
                if t % 2:
                    mm.then_inc(s_dt_ps, 1)
            pe.wait_ge(s_rw, 2)
            for h in range(2):
                pe.wait_ge(s_dht, 2 * h + 2)
                n = 0
                for a, b in passes:
                    for k in range(KC):
                        mm = nc.tensor.matmul(bank[4 + h][:, :], RW1[:, b, k], DHT[:, k, a, h * 512:(h + 1) * 512],
                                              start=(n == 0), stop=(n == 5))
                        n += 1
                mm.then_inc(s_r, 1)
            for t in range(T):
                pe.wait_ge(s_rhl, t // HT + 1)
                for n, (a, b) in enumerate(passes):
                    mm = nc.tensor.matmul(bank[6][:, t * E:(t + 1) * E], RHL[:, a, t * P:(t + 1) * P], RW2[:, b],
                                          start=(n == 0), stop=(n == 2))
            mm.then_inc(s_dlg, 1)
            pe.wait_ge(s_m, 1)
            pe.wait_ge(s_dconst, 4)
            rank = bank[4][:, 0:T * E]
            nc.tensor.matmul(rank, before_b[:, :], MSB[:, :, :].rearrange("p t e -> p (t e)"),
                             start=True, stop=False, skip_group_check=True)
            for t in range(T - 1):
                nc.tensor.matmul(rank[:, (t + 1) * E:].rearrange("p (t e) -> p t e", e=E), ones_b[:, :],
                                 MSB[:, t:t + 1].broadcast_to([P, T - 1 - t, E]), start=False,
                                 stop=t == T - 2, skip_group_check=True)
            for t in range(T):
                mm = nc.tensor.matmul(bank[5][:, 0:2 * E], ones_b[:, :],
                                      M01B[:, t].rearrange("p k e -> p (k e)"), start=t == 0, stop=t == T - 1)
            mm.then_inc(s_rank, 1)
            pe.wait_ge(s_gb16, 2)
            experts = list(range(E // 2, E)) + list(range(E // 2))
            for n, e in enumerate(experts):
                if e < E // 2:
                    pe.wait_ge(s_wlate, 2 * (e + 2))
                for c in range(HC8):
                    for s in range(2):
                        mm = nc.tensor.matmul(bank[7][0:2 * E, 0:D], GB16[:, c, e], W2[:, e, s, c],
                                              start=(n == 0 and c == 0 and s == 0),
                                              stop=(n == E - 1 and c == HC8 - 1 and s == 1))
            mm.then_inc(s_ce, 1)
            pe.wait_ge(s_coef, 1)
            for t in range(T):
                mm = nc.tensor.transpose(bank[2 + t // 4][0:3 * E, (t % 4) * P:(t % 4 + 1) * P], COEF[:, t],
                                         ident[:, :])
            mm.then_inc(s_cf_ps, 1)
            pe.wait_ge(s_cf, 2)
            pe.wait_ge(s_ce_sb, 1)
            for t in range(T):
                if t >= 2:
                    pe.wait_ge(s_base_used, t - 1)
                nc.tensor.matmul(bank[4 + t % 2][:, 0:D], COEF_T[0:3 * E, t * P:(t + 1) * P], B24[0:3 * E, :],
                                 start=True, stop=True).then_inc(s_base, 1)

            def transpose_tile(j, q, m, first=False):
                pe.wait_ge(s_xr[q], 16 * m + 16)
                if not first:
                    pe.wait_ge(s_xt, j - 1)
                v = bank[q][:, :].bitcast(F16)[:, 0:4 * P].rearrange("p (k s n) -> p k s n", k=KC, s=2)
                for k in range(KC):
                    for s in range(2):
                        mm = nc.tensor.transpose(v[:, k, s], XR[:, q, s, k * P:(k + 1) * P], ident_h[:, :])
                mm.then_inc(s_xt_ps, 1)

            def expert_of(j):
                return pe.value_load(EID[0:1, bass.ds(j, 1)], min_val=0, max_val=E - 1)

            def tile_up(j, q, first=False):
                e = expert_of(j)
                pe.wait_ge(s_xt, j + 1)
                for hb in range(2):
                    if not first:
                        pe.wait_ge(s_dg, 2 * j + hb - 3)
                    for c in range(4 * hb, 4 * hb + 4):
                        n = 0
                        for a, b in passes:
                            for k in range(KC):
                                mm = nc.tensor.matmul(up_bank[2 * q + hb][:, (c % 4) * P:(c % 4 + 1) * P],
                                                      W1[:, e, b, k, c * P:(c + 1) * P], XT[:, q, k, a],
                                                      start=(n == 0), stop=(n == 5))
                                n += 1
                    mm.then_inc(s_dup, 1)

            def tile_down(j, q, first=False):
                e = expert_of(j)
                if not first:
                    pe.wait_ge(s_ys, j - 1)
                n = 0
                for hb in range(2):
                    pe.wait_ge(s_dgl, 2 * j + hb + 1)
                    for c in range(4 * hb, 4 * hb + 4):
                        for a, b in passes:
                            mm = nc.tensor.matmul(bank[6 + q][:, 0:D], GDL[:, q, a, c * P:(c + 1) * P],
                                                  W2[:, e, b, c], start=(n == 0), stop=(n == 3 * HC8 - 1))
                            n += 1
                mm.then_inc(s_dd, 1)

            pe.wait_ge(s_eid, 1)
            pe.wait_ge(s_wlate, BLOCKS - MIDDLE)
            pe.wait_ge(s_base_used, T)
            transpose_tile(0, 0, 0, first=True)
            tile_up(0, 0, first=True)
            transpose_tile(1, 1, 0, first=True)
            tile_up(1, 1, first=True)
            transpose_tile(2, 0, 1)
            tile_down(0, 0, first=True)
            for j in range(2, 4):
                tile_up(j, j % 2)
                transpose_tile(j + 1, 1 - j % 2, (j + 1) // 2)
                tile_down(j - 1, 1 - j % 2, first=j == 2)
            with pe.Fori(2, TILES // 2) as i:
                for q in range(2):
                    tile_up(2 * i + q, q)
                    transpose_tile(2 * i + q + 1, 1 - q, i + q)
                    tile_down(2 * i + q - 1, 1 - q)
            tile_up(TILES - 1, 0)
            tile_down(TILES - 2, 1)
            tile_down(TILES - 1, 0)

        @block.vector
        def _(dve):
            done = Count(s_dve)

            def step(instruction):
                dve.wait_ge(s_dve, done.on(instruction))

            def mark(instruction):
                return done.on(instruction)

            def here():
                dve.wait_ge(s_dve, done.n)

            v = nc.vector

            def ln_variance(h, n):
                ts = slice(h * HT, (h + 1) * HT)
                for t in range(h * HT, (h + 1) * HT):
                    mark(v.bn_stats(stats[:, t], X[:, t]))
                here()
                for t in range(h * HT, (h + 1) * HT):
                    mark(v.bn_aggr(mv[:, t], stats[:, t]))
                here()
                v.tensor_scalar(ve[:, ts], mv[:, ts, 1], EPS, None, ALU.add).then_inc(s_ve, 1)

            def ln_rstd(h, n, scale):
                ts = slice(h * HT, (h + 1) * HT)
                dve.wait_ge(s_rstd0, n + 1)
                dve.wait_ge(s_ve, n + 1)
                step(v.tensor_tensor(rt[:, ts], ve[:, ts], rstd0[:, ts], ALU.mult))
                step(v.tensor_tensor(rt[:, ts], rt[:, ts], rstd0[:, ts], ALU.mult))
                step(v.tensor_scalar(rt[:, ts], rt[:, ts], -0.5 * scale, 1.5 * scale, ALU.mult, ALU.add))
                step(v.tensor_tensor(rstd[:, ts], rt[:, ts], rstd0[:, ts], ALU.mult))

            def round_fp8(dst, val, tmp):
                step(v.tensor_scalar(tmp.bitcast(U32), val.bitcast(U32), 0x7F800000, None, ALU.bitwise_and))
                step(v.tensor_scalar(tmp, tmp, FP8_MIN_NORMAL, ROUND_FP8, ALU.max, ALU.mult))
                step(v.tensor_tensor(val, val, tmp, ALU.add))
                return v.tensor_tensor(dst, val, tmp, ALU.subtract)

            dve.wait_ge(s_ct, 16)
            v.tensor_reduce(camax[:, :, :], CT.rearrange("p k (t n) -> p k t n", t=T), AX.X, ALU.max,
                            apply_absolute_value=True).then_inc(s_camax, 1)
            for h in range(2):
                dve.wait_ge(s_x[h], 16)
                ln_variance(h, h)
            dve.wait_ge(s_camax_all, 1)
            step(v.tensor_scalar(sw[:, :, :], camax_all[:, :, :], 1e-6, None, ALU.max))
            step(v.reciprocal(rw[:, :, :], sw[:, :, :]))
            step(v.tensor_scalar(rw[:, :, :], rw[:, :, :], FP8_MAX, None, ALU.mult))
            dve.wait_ge(s_tg, 1)
            step(v.tensor_scalar(sw[:, :, :], sw[:, :, :], tg[:, 0:1], 1.0 / FP8_MAX, ALU.mult, ALU.mult))
            step(v.tensor_tensor(VC.rearrange("p k (t n) -> p (k t) n", t=T),
                                 CT.rearrange("p k (t n) -> p (k t) n", t=T),
                                 rw[:, :, :].rearrange("p k t -> p (k t)").unsqueeze(2).broadcast_to([P, KC * T, P]),
                                 ALU.mult))
            round_fp8(CQT, VC, C2).then_inc(s_cqt, 1)
            for h in range(2):
                ts = slice(h * HT, (h + 1) * HT)
                ln_rstd(h, h, 1.0)
                for t in range(h * HT, (h + 1) * HT):
                    mark(v.tensor_scalar(XC[:, t], X[:, t], mv[:, t, 0:1], rstd[:, t:t + 1],
                                         ALU.subtract, ALU.mult))
                here()
                xk = XC[:, ts].rearrange("p t (k n) -> p (t k) n", k=KC)
                vk = V[:, ts].rearrange("p t (k n) -> p (t k) n", k=KC)
                flat = lambda a: a[:, ts].rearrange("p t k -> p (t k)")
                step(v.tensor_reduce(flat(xamax), xk, AX.X, ALU.max, apply_absolute_value=True))
                step(v.tensor_scalar(flat(sx), flat(xamax), 1e-4, None, ALU.max))
                step(v.reciprocal(flat(rx), flat(sx)))
                step(v.tensor_scalar(flat(rx), flat(rx), FP8_MAX, None, ALU.mult))
                step(v.tensor_scalar(flat(sx), flat(sx), 1.0 / FP8_MAX, None, ALU.mult))
                step(v.tensor_tensor(vk, xk, flat(rx).unsqueeze(2).broadcast_to([P, HT * KC, P]), ALU.mult))
                round_fp8(XQ[:, ts], V[:, ts], C1[:, ts]).then_inc(s_xq, 1)
            for nb in range(2):
                for k in range(KC):
                    mark(v.tensor_tensor(
                        sxw[:, :, nb, k].rearrange("p (b i) -> p b i", i=2),
                        sx[:, :, k].rearrange("p (b i) -> p b i", i=2),
                        sw[:, k, :].rearrange("p (b n) -> p b n", n=2)[:, :, nb:nb + 1].broadcast_to([P, B, 2]),
                        ALU.mult))
            here()
            for t in range(T):
                dve.wait_ge(s_da, t + 1)
                for k in range(KC):
                    for nb in range(2):
                        ins = v.scalar_tensor_tensor(
                            out=X[:, t, nb * P:(nb + 1) * P], in0=bank[4 + t % 4][:, k * D + nb * P:k * D + (nb + 1) * P],
                            scalar=sxw[:, t, nb, k:k + 1], in1=X[:, t, nb * P:(nb + 1) * P],
                            op0=ALU.mult, op1=ALU.add)
                        if (k, nb) == (KC - 1, 1):
                            ins.then_inc(s_da_used, 1)
                        else:
                            mark(ins)
                            if nb:
                                here()
            dve.wait_ge(s_da_used, T)
            dve.wait_ge(s_act, 3)
            dve.wait_ge(s_wl0, 80)
            for raw, w in ((GWR.rearrange("p k e -> p (k e)"), GWA.rearrange("p s k e -> p s (k e)")),
                           (WRAW, W1A.rearrange("p s c k h -> p s (c k h)")),
                           (WRAW2, W2A.rearrange("p s c d -> p s (c d)"))):
                v.scalar_tensor_tensor(out=w[:, 1], in0=raw, scalar=W_SCALE, in1=w[:, 0],
                                       op0=ALU.mult, op1=ALU.subtract).then_inc(s_w0, 1)
            step(v.tensor_scalar(B9[:, :], B9[:, :], G_SCALE * W_SCALE, None, ALU.mult))
            for h in range(2):
                ln_variance(h, 2 + h)
            for h in range(2):
                ln_rstd(h, 2 + h, X_SCALE)
                for t in range(h * HT, (h + 1) * HT):
                    v.tensor_scalar(HS[:, t], X[:, t], mv[:, t, 0:1], rstd[:, t:t + 1],
                                    ALU.subtract, ALU.mult).then_inc(s_hs, 1)
                for t in range(h * HT, (h + 1) * HT):
                    dve.wait_ge(s_hhi, t + 1)
                    v.tensor_tensor(HHL[:, t, 1], HS[:, t], HHL[:, t, 0], ALU.subtract).then_inc(s_hhl, 1)
            dve.wait_ge(s_lg, 1)
            step(v.tensor_copy(logits[:, :, :].rearrange("p t e -> p (t e)"), bank[4][:, 0:T * E]))
            for t in range(T):
                mark(v.max(top[:, t], logits[:, t]))
            here()
            for t in range(T):
                mark(v.max_index(topi[:, t], top[:, t], logits[:, t]))
            v.tensor_tensor(z12[:, :], top[:, :, 0], top[:, :, 1], ALU.subtract).then_inc(s_z12, 1)
            here()
            step(v.tensor_copy(topf[:, :, :], topi[:, :, 0:2]))
            for k, m in enumerate((mask0, mask1)):
                mark(v.tensor_tensor(m[:, :, :], iota_e[:, :].unsqueeze(1).broadcast_to([P, T, E]),
                                     topf[:, :, k:k + 1].broadcast_to([P, T, E]), ALU.is_equal))
            dve.wait_ge(s_th, 1)
            mark(v.tensor_scalar(wk[:, 0], th[:, :], 0.5, 0.5, ALU.mult, ALU.add))
            mark(v.tensor_scalar(wk[:, 1], th[:, :], -0.5, 0.5, ALU.mult, ALU.add))
            mark(v.memset(gates[:, :, E:E + 1], 1.0))
            here()
            for k, m in enumerate((mask0, mask1)):
                mark(v.tensor_tensor(m[:, :, :], m[:, :, :], wk[:, k].unsqueeze(2).broadcast_to([P, T, E]), ALU.mult))
            here()
            v.tensor_tensor(gates[:, :, 0:E], mask0[:, :, :], mask1[:, :, :], ALU.add).then_inc(s_gates, 1)
            dve.wait_ge(s_gates, 1)
            step(v.tensor_scalar(gates_s[:, :, :].rearrange("p t e -> p (t e)"),
                                 gates[:, :, :].rearrange("p t e -> p (t e)"), tg[:, 2:3],
                                 1.0 / (G_SCALE * W_SCALE), ALU.mult, ALU.mult))
            for i in range(2 * CA):
                c, h = i % CA, i // CA
                dve.wait_ge(s_gelu, i + 1)
                hi, lo = (GHL[:, s, c, h * 512:(h + 1) * 512] for s in range(2))
                step(v.tensor_scalar(hi, G32[:, i % 2], G_SCALE, None, ALU.mult))
                v.scalar_tensor_tensor(out=lo, in0=G32[:, i % 2], scalar=G_SCALE, in1=hi,
                                       op0=ALU.mult, op1=ALU.subtract).then_inc(s_ghl, 1)
                if i == 14:
                    dve.wait_ge(s_gt_ps, 1)
                    step(v.tensor_copy(gates_t[:, 0:512], bank[5][0:E + 1, :]))
                    v.tensor_copy(gates_t[:, 512:1024], bank[6][0:E + 1, :]).then_inc(s_gt, 1)
            n = 0
            for t in range(T):
                for c in range(0, CA, 2):
                    dve.wait_ge(s_down, n + 1)
                    src = bank[4 + n % DOWN_BANKS]
                    if c < E:
                        step(v.scalar_tensor_tensor(out=X[:, t], in0=src[:, 0:D], scalar=gates_s[:, t, c:c + 1],
                                                    in1=X[:, t], op0=ALU.mult, op1=ALU.add))
                        lastcol = src[:, D:2 * D]
                    else:
                        lastcol = src[:, 0:D]
                    e = min(c + 1, E)
                    v.scalar_tensor_tensor(out=X[:, t], in0=lastcol, scalar=gates_s[:, t, e:e + 1],
                                           in1=X[:, t], op0=ALU.mult, op1=ALU.add).then_inc(s_down_used, 1)
                    n += 1
                    dve.wait_ge(s_down_used, n)
            for j in range(2):
                v.memset(o_bank[j][:, :], 0.0).then_inc(s_obank, 1)

            def attention_q(b):
                ts = slice(2 * b, 2 * b + 2)
                for t in range(2 * b, 2 * b + 2):
                    mark(v.bn_stats(stats[:, t], X[:, t]))
                here()
                for t in range(2 * b, 2 * b + 2):
                    mark(v.bn_aggr(mv[:, t], stats[:, t]))
                here()
                v.tensor_scalar(ve[:, ts], mv[:, ts, 1], EPS, None, ALU.add).then_inc(s_ve, 1)
                dve.wait_ge(s_rstd0, 4 + b + 1)
                dve.wait_ge(s_ve, 4 + b + 1)
                step(v.tensor_tensor(rt[:, ts], ve[:, ts], rstd0[:, ts], ALU.mult))
                step(v.tensor_tensor(rt[:, ts], rt[:, ts], rstd0[:, ts], ALU.mult))
                step(v.tensor_scalar(rt[:, ts], rt[:, ts], -0.5, 1.5, ALU.mult, ALU.add))
                step(v.tensor_tensor(rstd[:, ts], rt[:, ts], rstd0[:, ts], ALU.mult))
                if b:
                    dve.wait_ge(s_qt_ps, 4 * b)
                heads = lambda a: a.rearrange("p (h d) -> p h d", h=HEADS)
                for i in range(2):
                    t = 2 * b + i
                    step(v.tensor_scalar(HC[:, i], X[:, t], mv[:, t, 0:1], rstd[:, t:t + 1],
                                         ALU.subtract, ALU.mult))
                    step(v.tensor_copy(QTOK[:, i, :, 0], heads(HC[:, i])))
                    step(v.tensor_tensor(heads(RC[:, i]), heads(HC[:, i]), QTOK[:, i, :, 0], ALU.subtract))
                    step(v.tensor_copy(QTOK[:, i, :, 3], heads(RC[:, i])))
                    v.tensor_tensor(QTOK[:, i, :, 5], heads(RC[:, i]), QTOK[:, i, :, 3],
                                    ALU.subtract).then_inc(s_q1, 1)

            def maximum(b, u):
                n = 12 * b + u
                dve.wait_ge(s_p1, n + 1)
                i = 0 if u < 4 else 1
                nh = 4 if i == 0 else 2
                h0 = 4 * u if i == 0 else 2 * (u - 4)
                v.tensor_reduce(MX[:, b % 2, i, h0:h0 + nh], s1_bank[n % 2][:, :].rearrange("p (h n) -> p h n", h=nh),
                                AX.X, ALU.max).then_inc(s_mx, 1)

            def minus_maximum(b):
                dve.wait_ge(s_mx, 12 * (b + 1))
                p = b % 2
                step(v.tensor_tensor(NM[:, p], MX[:, p], floor[:, :].unsqueeze(2).broadcast_to([P, 2, HEADS]),
                                     ALU.max))
                mark(v.tensor_scalar(WZ[:, p], NM[:, p], -1.0, CAUSAL_FILL, ALU.mult, ALU.add))
                step(v.tensor_scalar(NMR[:, :, :], NM[:, p], -1.0, None, ALU.mult))
                v.tensor_scalar(WZ[:, p], WZ[:, p], 0.0, None, ALU.min).then_inc(s_wz, 1)
                if b:
                    dve.wait_ge(s_nm_ps, b)
                step(v.tensor_copy(NMP[:, :, 0], NMR[:, :, :]))
                step(v.tensor_tensor(NMR2[:, :, :], NMR[:, :, :], NMP[:, :, 0], ALU.subtract))
                step(v.tensor_copy(NMP[:, :, 1], NMR2[:, :, :]))
                v.tensor_tensor(NMP[:, :, 2], NMR2[:, :, :], NMP[:, :, 1], ALU.subtract).then_inc(s_nmp, 1)

            def attention_out(b, i):
                t = 2 * b + i
                dve.wait_ge(s_wm, b + 1)
                step(v.tensor_scalar(DENR[:, :], WM[:, b % 2, i], hidden_n[:, i:i + 1], None, ALU.mult))
                dve.wait_ge(s_o_ps, t + 1)
                o = qt_bank[:, :].rearrange("p (h c) -> p h c", c=32)
                step(v.tensor_tensor(DEN[:, :], o[:, :, DH], DENR[:, :], ALU.add))
                step(v.reciprocal(DENR[:, :], DEN[:, :]))
                dve.wait_ge(s_hv, t + 1)
                num = NUM[:, :].rearrange("p (h d) -> p h d", h=HEADS)
                v.tensor_tensor(num, o[:, :, 0:DH], HV[:, i].rearrange("p (h d) -> p h d", h=HEADS),
                                ALU.add).then_inc(s_o_used, 1)
                dve.wait_ge(s_o_used, t + 1)
                step(v.tensor_tensor(num, num, DENR[:, :].unsqueeze(2).broadcast_to([P, HEADS, DH]), ALU.mult))
                step(v.scalar_tensor_tensor(out=X[:, t], in0=NUM[:, :], scalar=tg[:, 1:2], in1=X[:, t],
                                            op0=ALU.mult, op1=ALU.add))

            dve.wait_ge(s_masks, 4)
            attention_q(0)
            for u in range(12):
                maximum(0, u)
            minus_maximum(0)
            for b in range(B):
                if b + 1 < B:
                    attention_q(b + 1)
                    for u in range(12):
                        maximum(b + 1, u)
                for i in range(2):
                    attention_out(b, i)
                if b + 1 < B:
                    minus_maximum(b + 1)
            v.memset(rt[:, 0:1], 0.0).then_inc(s_x3_done, 1)
            for h in range(2):
                ln_variance(h, 8 + h)
            for h in range(2):
                ln_rstd(h, 8 + h, X_SCALE)
                for t in range(h * HT, (h + 1) * HT):
                    v.tensor_scalar(DHS[:, t], X[:, t], mv[:, t, 0:1], rstd[:, t:t + 1],
                                    ALU.subtract, ALU.mult).then_inc(s_dhs, 1)
                for t in range(h * HT, (h + 1) * HT):
                    dve.wait_ge(s_dhhi, t + 1)
                    v.tensor_tensor(DHL[:, t, 1], DHS[:, t], DHL[:, t, 0], ALU.subtract).then_inc(s_dhl, 1)
            dve.wait_ge(s_rwh, 2)
            dve.wait_ge(s_dw_small, 64)
            v.scalar_tensor_tensor(out=RW1[:, 1].rearrange("p k h -> p (k h)"),
                                   in0=RW1R.rearrange("p k h -> p (k h)"), scalar=W_SCALE,
                                   in1=RW1[:, 0].rearrange("p k h -> p (k h)"),
                                   op0=ALU.mult, op1=ALU.subtract).then_inc(s_rw, 1)
            v.scalar_tensor_tensor(out=RW2[:, 1], in0=RW2R[:, :], scalar=W_SCALE, in1=RW2[:, 0],
                                   op0=ALU.mult, op1=ALU.subtract).then_inc(s_rw, 1)
            for h in range(2):
                dve.wait_ge(s_rg, h + 1)
                hi, lo = (RHL[:, s, h * 512:(h + 1) * 512] for s in range(2))
                src = R32[:, h * 512:(h + 1) * 512]
                step(v.tensor_scalar(hi, src, G_SCALE, None, ALU.mult))
                v.scalar_tensor_tensor(out=lo, in0=src, scalar=G_SCALE, in1=hi,
                                       op0=ALU.mult, op1=ALU.subtract).then_inc(s_rhl, 1)
            dve.wait_ge(s_dlg, 1)
            step(v.tensor_copy(LG[:, :, :].rearrange("p t e -> p (t e)"), bank[6][:, 0:T * E]))
            step(v.tensor_reduce(LM[:, :], LG[:, :, :], AX.X, ALU.max))
            v.tensor_tensor(LG[:, :, :], LG[:, :, :], LM[:, :].unsqueeze(2).broadcast_to([P, T, E]),
                            ALU.subtract).then_inc(s_dl, 1)
            dve.wait_ge(s_ex, 1)
            step(v.tensor_reduce(LM[:, :], PR[:, :, :], AX.X, ALU.add))
            step(v.reciprocal(LM[:, :], LM[:, :]))
            step(v.tensor_tensor(PR[:, :, :], PR[:, :, :], LM[:, :].unsqueeze(2).broadcast_to([P, T, E]), ALU.mult))
            for t in range(T):
                mark(v.max(DTOP[:, t], PR[:, t]))
            here()
            for t in range(T):
                mark(v.max_index(DTOPI[:, t], DTOP[:, t], PR[:, t]))
            here()
            step(v.tensor_copy(DTOPF[:, :, :], DTOPI[:, :, 0:2]))
            for k in range(2):
                mark(v.tensor_tensor(M01[:, :, k], iota_e[:, :].unsqueeze(1).broadcast_to([P, T, E]),
                                     DTOPF[:, :, k:k + 1].broadcast_to([P, T, E]), ALU.is_equal))
            here()
            mark(v.tensor_copy(M01B[:, :, :, :].rearrange("p t k e -> p (t k e)"),
                               M01[:, :, :, :].rearrange("p t k e -> p (t k e)")))
            v.tensor_tensor(MSB[:, :, :], M01[:, :, 0], M01[:, :, 1], ALU.add).then_inc(s_m, 1)
            here()
            for k in range(2):
                mark(v.tensor_scalar(WKD[:, k], DTOP[:, :, k], tg[:, 3:4], None, ALU.mult))
            dve.wait_ge(s_gb, 1)
            step(v.tensor_scalar(GBH[:, :, :], GB[:, :, :], G_SCALE, None, ALU.mult))
            step(v.scalar_tensor_tensor(out=GBL[:, :, :], in0=GB[:, :, :], scalar=G_SCALE, in1=GBH[:, :, :],
                                        op0=ALU.mult, op1=ALU.subtract))
            step(v.memset(GB16.rearrange("p c e x -> p (c e x)").bitcast(F32), 0.0))
            for s, part in enumerate((GBH, GBL)):
                spread = GB16.rearrange("p c e x -> p c (e x)")[:, :, s * E::2 * E + 1]
                v.tensor_copy(spread, part[:, :, :].rearrange("p e c -> p c e")).then_inc(s_gb16, 1)
            dve.wait_ge(s_rank, 1)
            step(v.tensor_copy(NE01[:, :, :].rearrange("p k e -> p (k e)"), bank[5][:, 0:2 * E]))
            step(v.tensor_tensor(NE[:, :], NE01[:, 0], NE01[:, 1], ALU.add))
            dve.wait_ge(s_dconst, 4)
            step(v.tensor_tensor(USED[:, :, :], NE[:, :].unsqueeze(2).broadcast_to([P, E, T]),
                                 iota_full[:, :].unsqueeze(1).broadcast_to([P, E, T]), ALU.is_gt))
            step(v.tensor_reduce(NT[:, :], USED[:, :, :], AX.X, ALU.add))
            step(v.tensor_tensor_scan(ENDT[:, :], ones[:, 0:E], NT[:, :], 0.0, ALU.mult, ALU.add))
            step(v.tensor_tensor(BASE[:, :], ENDT[:, :], NT[:, :], ALU.subtract))
            step(v.tensor_scalar(BASE[:, :], BASE[:, :], float(P), None, ALU.mult))
            step(v.tensor_tensor(SLOTQ[:, :, :], bank[4][:, 0:T * E].rearrange("p (t e) -> p t e", e=E),
                                 BASE[:, :].unsqueeze(1).broadcast_to([P, T, E]), ALU.add))
            for k in range(2):
                mark(v.tensor_tensor(SLOTM[:, k], M01[:, :, k], SLOTQ[:, :, :], ALU.mult))
            here()
            step(v.tensor_reduce(SLOTF[:, :, :], SLOTM[:, :, :, :], AX.X, ALU.add))
            v.tensor_copy(SLOT[:, :, :], SLOTF[:, :, :]).then_inc(s_slot, 1)
            step(v.tensor_tensor(EOF_[:, :, :], iota_tile[:, :].unsqueeze(2).broadcast_to([P, TILES, E]),
                                 ENDT[:, :].unsqueeze(1).broadcast_to([P, TILES, E]), ALU.is_ge))
            step(v.tensor_reduce(EIDF[:, :], EOF_[:, :, :], AX.X, ALU.add))
            step(v.tensor_scalar(EIDF[:, :], EIDF[:, :], float(E - 1), None, ALU.min))
            v.tensor_copy(EID[:, :], EIDF[:, :]).then_inc(s_eid, 1)
            step(v.tensor_scalar(ACTV[:, :, :], NE01[:, :, :], 0.0, None, ALU.is_gt))
            for k in range(2):
                step(v.tensor_scalar(CF[:, k], M01[:, :, k], -1.0, 1.0, ALU.mult, ALU.add))
                step(v.tensor_tensor(CF[:, k], CF[:, k], ACTV[:, k].unsqueeze(1).broadcast_to([P, T, E]), ALU.mult))
                step(v.tensor_tensor(CF[:, k], CF[:, k], DTOP[:, :, k:k + 1].broadcast_to([P, T, E]), ALU.mult))
                step(v.tensor_tensor(SLOTM[:, k], M01[:, :, k], DTOP[:, :, k:k + 1].broadcast_to([P, T, E]), ALU.mult))
            for r in range(2):
                mark(v.tensor_tensor(COEF[:, :, r * E:(r + 1) * E], CF[:, 0], CF[:, 1], ALU.add))
            step(v.tensor_tensor(SLOTQ[:, :, :], SLOTM[:, 0], SLOTM[:, 1], ALU.add))
            v.tensor_tensor(COEF[:, :, 2 * E:3 * E], COEF[:, :, 0:E], SLOTQ[:, :, :], ALU.add).then_inc(s_coef, 1)
            for i in range(MIDDLE, BLOCKS):
                _, hi, lo = weight_block(i)
                dve.wait_ge(s_wlate_hi, i - MIDDLE + 1)
                v.scalar_tensor_tensor(out=lo, in0=STG[:, i % 2], scalar=W_SCALE, in1=hi,
                                       op0=ALU.mult, op1=ALU.subtract).then_inc(s_wlate, 1)
            dve.wait_ge(s_cf_ps, 1)
            for h in range(2):
                v.tensor_copy(COEF_T[0:3 * E, h * 512:(h + 1) * 512], bank[2 + h][0:3 * E, :]).then_inc(s_cf, 1)
            dve.wait_ge(s_ce, 1)
            v.tensor_scalar(B24[0:2 * E, :], bank[7][0:2 * E, 0:D], 1.0 / (G_SCALE * W_SCALE), None,
                            ALU.mult).then_inc(s_ce_sb, 1)
            for t in range(T):
                dve.wait_ge(s_base, t + 1)
                v.scalar_tensor_tensor(out=X[:, t], in0=bank[4 + t % 2][:, 0:D], scalar=tg[:, 3:4], in1=X[:, t],
                                       op0=ALU.mult, op1=ALU.add).then_inc(s_base_used, 1)

            def rows_t(j, q, first=False):
                dve.wait_ge(s_xt_ps, j + 1)
                if not first:
                    dve.wait_ge(s_dup, 2 * j - 2)
                v.tensor_copy(XT[:, q].rearrange("p k s n -> p (k s n)"),
                              bank[q][:, :].bitcast(F16)[:, 0:4 * P]).then_inc(s_xt, 1)

            def split_hidden(j, q, hb, first=False):
                dve.wait_ge(s_dg, 2 * j + hb + 1)
                if not first:
                    dve.wait_ge(s_dd, j - 1)
                src = GD[:, q, hb * 512:(hb + 1) * 512]
                hi, lo = (GDL[:, q, s, hb * 512:(hb + 1) * 512] for s in range(2))
                v.tensor_scalar(hi, src, G_SCALE, None, ALU.mult).then_inc(s_dgh, 1)
                dve.wait_ge(s_dgh, 2 * j + hb + 1)
                v.scalar_tensor_tensor(out=lo, in0=src, scalar=G_SCALE, in1=hi,
                                       op0=ALU.mult, op1=ALU.subtract).then_inc(s_dgl, 1)

            def tile_out(j, q, m, first=False):
                dve.wait_ge(s_dd, j + 1)
                if not first:
                    dve.wait_ge(s_yst[q], 16 * m)
                v.tensor_scalar(YS[:, q], bank[6 + q][:, 0:D], 1.0 / (G_SCALE * W_SCALE), None,
                                ALU.mult).then_inc(s_ys, 1)

            rows_t(0, 0, first=True)
            split_hidden(0, 0, 0, first=True)
            rows_t(1, 1, first=True)
            split_hidden(0, 0, 1, first=True)
            split_hidden(1, 1, 0, first=True)
            rows_t(2, 0)
            split_hidden(1, 1, 1, first=True)
            tile_out(0, 0, 0, first=True)
            for j in range(2, 4):
                split_hidden(j, j % 2, 0)
                rows_t(j + 1, 1 - j % 2)
                split_hidden(j, j % 2, 1)
                tile_out(j - 1, 1 - j % 2, j // 2 - 1 + j % 2, first=j == 2)
            with dve.Fori(2, TILES // 2) as i:
                for q in range(2):
                    split_hidden(2 * i + q, q, 0)
                    rows_t(2 * i + q + 1, 1 - q)
                    split_hidden(2 * i + q, q, 1)
                    tile_out(2 * i + q - 1, 1 - q, i - 1 + q)
            for hb in range(2):
                split_hidden(TILES - 1, 0, hb)
            tile_out(TILES - 2, 1, TILES // 2 - 1)
            tile_out(TILES - 1, 0, TILES // 2)
            for t in range(T):
                dve.wait_ge(s_yg[t], 32)
                step(v.scalar_tensor_tensor(out=X[:, t], in0=YG[:, t, 0], scalar=WKD[:, 0, t:t + 1], in1=X[:, t],
                                            op0=ALU.mult, op1=ALU.add))
                v.scalar_tensor_tensor(out=X[:, t], in0=YG[:, t, 1], scalar=WKD[:, 1, t:t + 1], in1=X[:, t],
                                       op0=ALU.mult, op1=ALU.add).then_inc(s_xout, 1)


def lay_out(x, ctx_2048, g_xattn, g_ffn, L0_ffn_gate_w, L0_ffn_w1, L0_ffn_b1, L0_ffn_w2, L0_ffn_b2,
            L0_ffn_shared_w1, L0_ffn_shared_b1, L0_ffn_shared_w2, L0_ffn_shared_b2,
            L1_ffn_rw1, L1_ffn_rw2, L1_ffn_w1, L1_ffn_b1, L1_ffn_w2, L1_ffn_b2):
    tokens, d = x.shape[0] * x.shape[1], x.shape[2]
    k = d // P
    experts = L0_ffn_gate_w.shape[1]
    shared = L0_ffn_shared_w1.shape[1] // P
    hidden = L1_ffn_w1.shape[2]
    ctx = ctx_2048.reshape(tokens, d)
    return {
        "x": x.reshape(tokens, d),
        "ctx": ctx,
        "ctx_t": ctx.T.reshape(k, P, tokens).transpose(1, 0, 2),
        "gates": np.concatenate([g_xattn, g_ffn]),
        "gate_w": L0_ffn_gate_w.reshape(k, P, experts).transpose(1, 0, 2),
        "l0_w1": np.concatenate([L0_ffn_w1.reshape(experts, k, P, P).transpose(2, 0, 1, 3),
                                 L0_ffn_shared_w1.reshape(k, P, shared, P).transpose(1, 2, 0, 3)], 1),
        "l0_b1": np.concatenate([L0_ffn_b1, L0_ffn_shared_b1.reshape(shared, P)], 0).T,
        "l0_w2": np.concatenate([L0_ffn_w2.transpose(1, 0, 2),
                                 L0_ffn_shared_w2.reshape(shared, P, d).transpose(1, 0, 2)], 1),
        "l0_b2": np.concatenate([L0_ffn_b2, L0_ffn_shared_b2[None]], 0),
        "router_w1": L1_ffn_rw1.reshape(k, P, -1).transpose(1, 0, 2),
        "router_w2": L1_ffn_rw2,
        "l1_w1": L1_ffn_w1.reshape(experts, k, P, hidden).transpose(2, 0, 1, 3),
        "l1_b1": L1_ffn_b1.reshape(experts, hidden // P, P).transpose(2, 0, 1),
        "l1_w2": L1_ffn_w2.reshape(experts, hidden // P, P, d).transpose(2, 0, 1, 3),
        "l1_b2": L1_ffn_b2,
    }


def kernel(**inputs):
    import concourse.bacc as bacc
    from concourse.bass_utils import run_bass_kernel_spmd

    shape = inputs["x"].shape
    nc = bacc.Bacc("TRN2", target_bir_lowering=False, num_devices=1)
    arrays, args = {}, []
    for name, a in lay_out(**{n: np.asarray(a) for n, a in inputs.items()}).items():
        a = np.ascontiguousarray(a)
        arrays[f"in_{name}_dram"] = a
        args.append(nc.dram_tensor(f"in_{name}_dram", a.shape, mybir.dt.from_np(a.dtype),
                                   kind="ExternalInput").ap())
    args.append(nc.dram_tensor("out_dram", (shape[0] * shape[1], shape[2]), F32, kind="ExternalOutput").ap())
    flamingo(nc, *args)
    result = run_bass_kernel_spmd(nc, [arrays], core_ids=[0])
    return result.results[0]["out_dram"].reshape(shape)
```

```python
from contextlib import ExitStack

import numpy as np

import concourse.bass as bass
from concourse import mybir

F32 = mybir.dt.float32
BF16 = mybir.dt.bfloat16
F16 = mybir.dt.float16
I32 = mybir.dt.int32
U32 = mybir.dt.uint32
ALU = mybir.AluOpType
ACT = mybir.ActivationFunctionType
AX = mybir.AxisListType

P = 128
EPS = 1e-5
FP8_MAX = 448.0
ROUND_FP8 = 1.5 * 2.0 ** 20
FP8_MIN_NORMAL = 2.0 ** -6
X_SCALE = 256.0
W_SCALE = 64.0
G_SCALE = 16.0


class Count:

    def __init__(self, sem, step=1):
        self.sem, self.step, self.n = sem, step, 0

    def on(self, instruction):
        instruction.then_inc(self.sem, self.step)
        self.n += self.step
        return self.n


CAUSAL_FILL = -1e4 * 4.0
NEVER = -1e30
Q_PART = (0, 0, 0, 1, 1, 2)
K_PART = (0, 1, 2, 0, 1, 0)


def flamingo(nc, x, ctx, ctx_t, gates2, gate_w, w1a, b1a, w2a, b2a, rw1, rw2, w1d, b1d, w2d, b2d, out):
    N, D = x.shape
    T = N // P
    KC = D // P
    E = gate_w.shape[2]
    B = 4
    S = N // B
    HT = T // 2
    CA = w1a.shape[1]

    with ExitStack() as stack:
        def sb(name, shape, dt):
            return stack.enter_context(nc.sbuf_tensor(name, shape, dt))

        def sem(name):
            return stack.enter_context(nc.semaphore(name))

        HEADS = 16
        DH = D // HEADS
        ROWS = len(Q_PART) * DH
        HID = w1d.shape[3]
        HC8 = HID // P
        PAIRS = 2 * N
        TILES = PAIRS // P + E - 1
        HEAD, UNROLL = 3, 4
        LOOPS = (TILES - HEAD - 1) // UNROLL
        TAIL = HEAD + UNROLL * LOOPS
        sorted_rows = nc.dram_tensor("sorted_rows", [TILES * P, D], U32).ap()
        routed_rows = nc.dram_tensor("routed_rows", [TILES * P, D], F32).ap()
        k_parts = nc.dram_tensor("k_parts", [3, D, N], BF16).ap()

        W1_ = sb("W1", [P, 64 * 256], F32)
        arena = sb("arena", [P, 113 * 256], F32)

        def at(kb, shape, dt):
            size = 1
            for n in shape:
                size *= n
            words = size * mybir.dt.size(dt) // 4
            o = int(kb * 256)
            v = arena[:, o:o + words].bitcast(dt) if dt != F32 else arena[:, o:o + words]
            if len(shape) == 1:
                return v
            names = "abcd"[:len(shape)]
            return v.rearrange(f"p ({' '.join(names)}) -> p {' '.join(names)}",
                               **{c: n for c, n in zip(names, shape)})

        X = sb("X", [P, T, D], F32)
        ident = sb("ident", [P, P], F32)
        ident_h = sb("ident_h", [P, P], F16)
        ident_b = sb("ident_b", [P, P], BF16)
        iota_e = sb("iota_e", [P, E], F32)
        g_raw = sb("g_raw", [P, 4], F32)
        tg = sb("tg", [P, 4], F32)
        stats = sb("stats", [P, T, 6], F32)
        mv = sb("mv", [P, T, 2], F32)
        ve = sb("ve", [P, T], F32)
        rstd0 = sb("rstd0", [P, T], F32)
        rt = sb("rt", [P, T], F32)
        rstd = sb("rstd", [P, T], F32)
        neg_half = sb("neg_half", [P, T], F32)
        KS = W1_[:, 48 * 256:60 * 256].bitcast(BF16).rearrange("p (s k n) -> p s k n", s=3, k=KC)
        KR = W1_[:, 40 * 256:48 * 256].rearrange("p (k n) -> p k n", k=KC)
        CN = W1_[:, 32 * 256:40 * 256].rearrange("p (t d) -> p t d", t=T)
        KST = [W1_[:, 56 * 256:64 * 256].bitcast(BF16).rearrange("p (h n) -> p h n", h=HEADS),
               at(68, [HEADS, S], BF16)]
        QST = [at(0, [HEADS, S], BF16), at(8, [HEADS, S], BF16)]
        HC = at(16, [2, D], F32)
        RC = at(18, [2, D], F32)
        RC2 = at(20, [2, D], F32)
        QTOK = at(22, [2, HEADS, len(Q_PART), DH], BF16)
        OT = at(105.5, [2, 512], F32)
        PT = at(76, [6, 512], F32)
        VA = at(89, [T, HEADS, DH + 1], F32)
        SUFV = at(97.5, [T, D], F32)
        neg_mask = sb("neg_mask", [P, P], BF16)
        after = sb("after", [P, P], F32)
        ones = sb("ones", [P, P], F32)
        hidden_n = sb("hidden_n", [P, 2], F32)
        floor = sb("floor", [P, 2], F32)
        MX = sb("MX", [P, 2, 2, HEADS], F32)
        NM = sb("NM", [P, 2, 2, HEADS], F32)
        NMR = sb("NMR", [P, 2, HEADS], F32)
        NMR2 = sb("NMR2", [P, 2, HEADS], F32)
        NMP = sb("NMP", [P, 2, 3, HEADS], BF16)
        NMS = sb("NMS", [3 * HEADS, S], BF16)
        WZ = sb("WZ", [P, 2, 2, HEADS], F32)
        WM = sb("WM", [P, 2, 2, HEADS], F32)
        DEN = sb("DEN", [P, HEADS], F32)
        DENR = sb("DENR", [P, HEADS], F32)
        HV = sb("HV", [P, 2, D], F32)
        NUM = at(88, [D], F32)
        W1 = W1_[:, :].bitcast(F16).rearrange("p (e s k n) -> p e s k n", e=E, s=2, k=KC)
        W2 = at(0, [E, HC8, 2, D], F16)
        STG = sb("STG", [P, 2, HID], F32)
        DHS = at(24, [T, D], F32)
        DHL = at(64, [T, 2, D], F16)
        DHT = at(16, [KC, 2, N], F16)
        R32 = at(88, [N], F32)
        RHL = at(92, [2, N], F16)
        GB16 = at(96, [HC8, E, 2 * E], F16)
        COEF_T = at(98, [N], F32)
        B24 = at(102, [D], F32)
        XR = at(104, [2, 2, D], F16)
        XT = at(106, [2, KC, 2, P], F16)
        YS = at(108, [2, D], F32)
        GD = at(64, [2, HID], F32)
        GDL = at(88, [2, 2, HID], F16)
        YG = at(72, [T, 2, D], F32)
        RW1R = at(110, [KC, P], F32)
        RW1 = at(111, [2, KC, P], F16)
        RW2R = sb("RW2R", [P, E], F32)
        RW2 = sb("RW2", [P, 2, E], F16)
        B1D = sb("B1D", [P, E, HC8], F32)
        GB = sb("GB", [P, E, HC8], F32)
        GBH = sb("GBH", [P, E, HC8], F16)
        GBL = sb("GBL", [P, E, HC8], F16)
        before_b = sb("before_b", [P, P], BF16)
        ones_b = sb("ones_b", [P, P], BF16)
        iota_tile = sb("iota_tile", [P, TILES], F32)
        iota_full = sb("iota_full", [P, T], F32)
        LG = at(112, [T, E], F32)
        LM = sb("LM", [P, T], F32)
        PR = at(112.25, [T, E], F32)
        DTOP = sb("DTOP", [P, T, 8], F32)
        DTOPI = sb("DTOPI", [P, T, 8], U32)
        DTOPF = sb("DTOPF", [P, T, 2], F32)
        M01 = at(112.5, [T, 2, E], F32)
        M01B = sb("M01B", [P, T, 2, E], BF16)
        MSB = sb("MSB", [P, T, E], BF16)
        NE01 = sb("NE01", [P, 2, E], F32)
        NE = sb("NE", [P, E], F32)
        USED = sb("USED", [P, E, T], F32)
        NT = sb("NT", [P, E], F32)
        ENDT = sb("ENDT", [P, E], F32)
        BASE = sb("BASE", [P, E], F32)
        SLOTQ = sb("SLOTQ", [P, T, E], F32)
        SLOTM = sb("SLOTM", [P, 2, T, E], F32)
        SLOTF = sb("SLOTF", [P, 2, T], F32)
        SLOT = sb("SLOT", [P, 2, T], U32)
        EOF_ = sb("EOF", [P, TILES, E], F32)
        EIDF = sb("EIDF", [P, TILES], F32)
        EID = sb("EID", [P, TILES], I32)
        ACTV = sb("ACTV", [P, 2, E], F32)
        COEF = sb("COEF", [P, T, 3 * E], F32)
        CF = sb("CF", [P, 2, T, E], F32)
        WKD = sb("WKD", [P, 2, T], F32)
        CT = at(0, [KC, N], F32)
        XC = at(8, [T, D], F32)
        V = at(16, [T, D], F32)
        C1 = at(24, [T, D], F32)
        XQ = at(32, [T, D], BF16)
        XQT = at(36, [2, KC, HT * P], BF16)
        VC = at(40, [KC, N], F32)
        C2 = at(48, [KC, N], F32)
        CQT = at(56, [KC, N], BF16)
        HS = at(0, [T, D], F32)
        HHL = at(8, [T, 2, D], F16)
        HT_ = at(16, [KC, 2, N], F16)
        G32 = at(24, [2, 512], F32)
        GHL = at(28, [2, CA, N], F16)
        W1A = at(68, [2, CA, KC, P], F16)
        W2A = at(78, [2, CA, D], F16)
        GWA = at(88, [2, KC, E], F16)
        WRAW = at(89, [CA * D], F32)
        WRAW2 = at(99, [CA * D], F32)
        GWR = at(109, [KC, E], F32)
        B1A = sb("B1A", [P, CA], F32)
        B9 = at(110, [D], F32)[0:E + 1]
        camax = sb("camax", [P, KC, T], F32)
        camax_all = sb("camax_all", [P, KC, T], F32)
        xamax = sb("xamax", [P, T, KC], F32)
        sx = sb("sx", [P, T, KC], F32)
        rx = sb("rx", [P, T, KC], F32)
        sw = sb("sw", [P, KC, T], F32)
        rw = sb("rw", [P, KC, T], F32)
        sxw = sb("sxw", [P, T, 2, KC], F32)
        logits = LG
        top = DTOP
        topi = DTOPI
        topf = DTOPF
        mask0 = CF[:, 0]
        mask1 = CF[:, 1]
        z12 = sb("z12", [P, T], F32)
        th = sb("th", [P, T], F32)
        wk = WKD
        gates = sb("gates", [P, T, E + 1], F32)
        gates_s = sb("gates_s", [P, T, E + 1], F32)
        gates_t = at(0, [N], F32)[0:E + 1]

        bank = [stack.enter_context(nc.psum_tensor(f"bank{i}", [P, 512], F32)) for i in range(8)]

        s1_bank, s2_bank, ot_bank, o_bank, qt_bank = bank[0:2], bank[2:4], bank[4], bank[5:7], bank[7]
        up_bank = bank[2:6]

        s_x = [sem(f"x_landed{i}") for i in range(2)]
        s_ct = sem("ctx_t_landed")
        s_g = sem("layer_gates_landed")
        s_wl0 = sem("l0_weights_landed")
        s_const = sem("constants_made")
        s_dve = sem("dve_step")
        s_act = sem("act_step")
        s_pool = sem("pool_step")
        s_camax = sem("ctx_amax_local")
        s_camax_all = sem("ctx_amax_all")
        s_ve = sem("variance_ready")
        s_rstd0 = sem("rstd_estimated")
        s_tg = sem("tanh_gates_ready")
        s_xq = sem("x_quantised")
        s_xqt_ps = sem("xq_transposed")
        s_xqt = sem("xq_t_in_sbuf")
        s_cqt = sem("ctx_quantised")
        s_da = sem("stage_a_product")
        s_da_used = sem("stage_a_product_used")
        s_w0 = sem("l0_weights_split")
        s_hhl = sem("ln_split")
        s_hs = sem("ln_scaled")
        s_hhi = sem("ln_high")
        s_ht_ps = sem("ln_transposed")
        s_ht = sem("ln_t_in_sbuf")
        s_lg = sem("logits_product")
        s_z12 = sem("logit_gap")
        s_th = sem("tanh_gap")
        s_gates = sem("gates_ready")
        s_gt_ps = sem("gates_transposed")
        s_gt = sem("gates_t_in_sbuf")
        s_up = sem("up_product")
        s_gelu = sem("gelu_done")
        s_ghl = sem("hidden_split")
        s_down = sem("down_product")
        s_down_used = sem("down_product_used")
        s_ctx = sem("ctx_landed")
        s_kparts = sem("k_parts_split")
        s_kparts_out = sem("k_parts_stored")
        s_kst = [sem(f"k_stack_landed{i}") for i in range(2)]
        s_masks = sem("masks_made")
        s_va = sem("v_with_ones_ready")
        s_suf_ps = sem("suffix_sums_product")
        s_suf = sem("suffix_sums_ready")
        s_q1 = sem("q_parts_ready")
        s_qtok = sem("q_parts_repeated")
        s_qt_ps = sem("q_stack_transposed")
        s_qst = sem("q_stack_in_sbuf")
        s_p1 = sem("scores_for_maximum")
        s_mx = sem("maximum_taken")
        s_nmp = sem("minus_maximum_split")
        s_nm_ps = sem("minus_maximum_transposed")
        s_nms = sem("minus_maximum_in_sbuf")
        s_nmrow = sem("minus_maximum_rows_landed")
        s_wz = sem("hidden_exponent")
        s_wm = sem("hidden_weight")
        s_p2 = sem("scores_by_key")
        s_pt = sem("exponentials_ready")
        s_pv = sem("values_product")
        s_ot = sem("values_product_in_sbuf")
        s_o_ps = sem("attention_transposed")
        s_o_used = sem("attention_used")
        s_hv = sem("hidden_share_ready")
        s_obank = sem("o_banks_cleared")
        s_zero = sem("zeros_made")
        s_fill = sem("sorted_rows_cleared")
        s_dw_small = sem("d_small_weights_landed")
        s_stg = [sem(f"weights_landed{i}") for i in range(2)]
        s_wscaled = sem("weights_scaled")
        s_whi = sem("weights_high")
        s_wlo = sem("weights_low")
        s_wlate_hi = sem("late_weights_high")
        s_wlate = sem("late_weights_low")
        s_dconst = sem("d_constants_made")
        s_rw = sem("router_weights_split")
        s_rwh = sem("router_weights_high")
        s_dhs = sem("d_ln_scaled")
        s_dhhi = sem("d_ln_high")
        s_dhl = sem("d_ln_split")
        s_dt_ps = sem("d_ln_transposed")
        s_dht = sem("d_ln_t_in_sbuf")
        s_r = sem("router_hidden_product")
        s_rg = sem("router_gelu")
        s_rhl = sem("router_hidden_split")
        s_dlg = sem("router_logits")
        s_dl = sem("router_logits_less_max")
        s_ex = sem("router_exponentials")
        s_m = sem("choice_masks")
        s_rank = sem("ranks_counted")
        s_slot = sem("slots_ready")
        s_eid = sem("tile_experts_ready")
        s_scat = sem("rows_scattered")
        s_gb = sem("gelu_of_b1")
        s_gbp = sem("gelu_of_b1_parts")
        s_gb16 = sem("gelu_of_b1_spread")
        s_ce = sem("idle_outputs_product")
        s_ce_sb = sem("idle_outputs_in_sbuf")
        s_coef = sem("coefficients_ready")
        s_cf_ps = sem("coefficients_transposed")
        s_cf = sem("coefficients_t_in_sbuf")
        s_base = sem("idle_share_product")
        s_base_used = sem("idle_share_added")
        s_xr = [sem(f"tile_rows_landed{i}") for i in range(2)]
        s_xt_ps = sem("tile_rows_transposed")
        s_xt = sem("tile_rows_t_in_sbuf")
        s_dup = sem("tile_up_product")
        s_dg = sem("tile_gelu")
        s_dgh = sem("tile_hidden_high")
        s_dgl = sem("tile_hidden_split")
        s_dd = sem("tile_down_product")
        s_yh = sem("tile_output_half_in_sbuf")
        s_ys = sem("tile_output_in_sbuf")
        s_yst = [sem(f"tile_output_stored{i}") for i in range(2)]
        s_yg = [sem(f"routed_rows_gathered{t}") for t in range(T)]
        s_x3_done = sem("x3_ready")
        s_xout = sem("out_tile_ready")
        s_out_ready = sem("out_ready")
        s_out = sem("out_stored")

        block = stack.enter_context(nc.Block())
        DOWN_BANKS = 4
        BLOCKS = 4 * E
        ORDER = ([("w1", e) for e in range(E - 1)] + [("w2", e) for e in range(E // 2, E)]
                 + [("w1", E - 1), ("w2", 0), ("w2", 1), ("w2", 3), ("w2", 2)])
        EARLY, MIDDLE, LATE = 2 * (E - 1), 2 * (E - 1) + E, 2 * (E - 1) + E + 4

        C_BLOCKS = [range(EARLY, EARLY + 2), range(EARLY + 2, EARLY + 5), range(EARLY + 5, MIDDLE),
                    range(MIDDLE, MIDDLE + 4)]
        SPLIT_AT = (2, 5, 11, 8)
        D_BLOCKS = range(MIDDLE + 4, BLOCKS)

        def weight_block(i):
            (which, e), half = ORDER[i // 2], i % 2
            if which == "w1":
                return w1d[:, e, half], W1[:, e, 0, half], W1[:, e, 1, half]
            cs = slice(half * HC8 // 2, (half + 1) * HC8 // 2)
            flat = lambda a: a.rearrange("p c d -> p (c d)")
            return flat(w2d[:, e, cs]), W2[:, e, cs, 0], W2[:, e, cs, 1]

        DOWNS = T * CA // 2

        @block.sync
        def _(sp):
            def load_weights(i):
                if i >= 2:
                    sp.wait_ge(s_wlo, i - 1)
                sp.dma_start(STG[:, i % 2], weight_block(i)[0]).then_inc(s_stg[i % 2], 16)

            for h in range(2):
                sp.dma_start(X[:, h * HT:(h + 1) * HT, :],
                             x[h * HT * P:(h + 1) * HT * P, :].rearrange("(t p) d -> p t d", p=P)
                             ).then_inc(s_x[h], 16)
            sp.dma_start(WRAW, w1a.rearrange("p c k h -> p (c k h)")).then_inc(s_wl0, 16)
            sp.dma_start(WRAW2, w2a.rearrange("p c d -> p (c d)")).then_inc(s_wl0, 16)
            sp.dma_start(B9[:, :], b2a).then_inc(s_wl0, 16)
            sp.dma_start(CN, ctx.rearrange("(t p) d -> p t d", p=P)).then_inc(s_ctx, 16)
            for i in range(2):
                load_weights(i)
            sp.wait_ge(s_zero, 1)
            sp.dma_start(sorted_rows.rearrange("(t p) d -> p t d", p=P),
                         HV[:, 0].bitcast(U32).unsqueeze(1).broadcast_to([P, TILES, D])).then_inc(s_fill, 16)
            sp.wait_ge(s_kparts, 3)
            for k in range(KC):
                sp.dma_start(k_parts[:, k * P:(k + 1) * P, :].rearrange("s p n -> p s n"),
                             KS[:, :, k]).then_inc(s_kparts_out, 16)
            for i in range(2, 6):
                load_weights(i)
            sp.wait_ge(s_kparts_out, 16 * KC)

            def load_k_stack(b):
                for r, s in enumerate(K_PART):
                    sp.dma_start(KST[b % 2][r * DH:(r + 1) * DH],
                                 k_parts[s, :, b * S:(b + 1) * S].rearrange("(h d) n -> d h n", d=DH)
                                 ).then_inc(s_kst[b % 2], 16)

            load_k_stack(0)
            for i in range(6, EARLY):
                load_weights(i)
            sp.wait_ge(s_down, DOWNS)
            load_k_stack(1)
            for i in range(EARLY, EARLY + 2):
                load_weights(i)

            def load_minus_max(b):
                sp.wait_ge(s_nms, b + 1)
                for s in range(1, 3):
                    sp.dma_start(QST[b % 2][ROWS + s:ROWS + s + 1], NMS[s * HEADS:(s + 1) * HEADS, :]
                                 ).then_inc(s_nmrow, 16)

            load_minus_max(0)
            for i in range(EARLY + 2, EARLY + 4):
                load_weights(i)
            load_minus_max(1)
            for b in range(2, B):
                sp.wait_ge(s_p2, 12 * (b - 1))
                load_k_stack(b)
                for i in range(EARLY + 2 * b, EARLY + 2 * b + 2):
                    load_weights(i)
                load_minus_max(b)
            for i in range(MIDDLE, D_BLOCKS[0]):
                load_weights(i)
            for i in D_BLOCKS:
                load_weights(i)
            sp.wait_ge(s_scat, 16 * 2 * T)

            def load_tile(j, q, first=False):
                if not first:
                    sp.wait_ge(s_xt_ps, j - 1)
                sp.dma_start(XR[:, q].rearrange("p s d -> p (s d)").bitcast(U32),
                             sorted_rows[bass.ds(j * P, P), :]).then_inc(s_xr[q], 16)

            def store_tile(j, q):
                sp.wait_ge(s_ys, j + 1)
                sp.dma_start(routed_rows[bass.ds(j * P, P), :], YS[:, q]).then_inc(s_yst[q], 16)

            for j in range(4):
                load_tile(j, j % 2, first=j < 2)
            store_tile(0, 0)
            with sp.Fori(0, LOOPS) as i:
                for r in range(UNROLL):
                    load_tile(UNROLL * i + HEAD + r + 1, r % 2)
                    store_tile(UNROLL * i + HEAD + r - 2, (r + 1) % 2)
            for j in range(TAIL, TILES):
                if j + 1 < TILES:
                    load_tile(j + 1, (j + 1) % 2)
                store_tile(j - 2, j % 2)
            for j in range(TILES - 2, TILES):
                store_tile(j, j % 2)
            for t in range(T):
                sp.wait_ge(s_xout, t + 1)
                sp.dma_start(out[t * P:(t + 1) * P, :], X[:, t, :]).then_inc(s_out, 16)
            sp.wait_ge(s_out, 16 * T)

        @block.gpsimd
        def _(pool):
            done = Count(s_pool)
            nc.gpsimd.memset(ident[:, :], 0.0).then_inc(s_pool, 1)
            nc.gpsimd.memset(neg_half[:, :], -0.5).then_inc(s_const, 1)
            nc.gpsimd.iota(iota_e[:, :], [[1, E]], base=0, channel_multiplier=0,
                           allow_small_or_imprecise_dtypes=True).then_inc(s_const, 1)
            pool.wait_ge(s_pool, 1)
            nc.gpsimd.affine_select(out=ident[:, :], in_=ident[:, :], compare_op=ALU.not_equal,
                                    fill=1.0, base=0, pattern=[[-1, P]],
                                    channel_multiplier=1).then_inc(s_const, 1)
            pool.wait_ge(s_const, 3)
            nc.gpsimd.tensor_copy(ident_h[:, :], ident[:, :]).then_inc(s_const, 1)
            nc.gpsimd.tensor_copy(ident_b[:, :], ident[:, :]).then_inc(s_const, 1)
            done.n = 1
            nc.gpsimd.memset(HV[:, 0], 0.0).then_inc(s_zero, 1)
            nc.gpsimd.memset(neg_mask[:, :], 0.0).then_inc(s_pool, 1)
            nc.gpsimd.memset(ones[:, :], 1.0).then_inc(s_pool, 1)
            nc.gpsimd.iota(hidden_n[:, :], [[-P, 2]], base=S - 1, channel_multiplier=-1,
                           allow_small_or_imprecise_dtypes=True).then_inc(s_masks, 1)
            nc.gpsimd.memset(floor[:, :], CAUSAL_FILL).then_inc(s_pool, 1)
            done.n = 4
            pool.wait_ge(s_pool, 4)
            nc.gpsimd.affine_select(out=neg_mask[:, :], in_=neg_mask[:, :], compare_op=ALU.is_ge, fill=NEVER,
                                    base=0, pattern=[[-1, P]], channel_multiplier=1).then_inc(s_masks, 1)
            nc.gpsimd.affine_select(out=after[:, :], in_=ones[:, :], compare_op=ALU.is_gt, fill=0.0,
                                    base=0, pattern=[[-1, P]], channel_multiplier=1).then_inc(s_masks, 1)
            nc.gpsimd.affine_select(out=floor[:, 1:2], in_=floor[:, 1:2], compare_op=ALU.not_equal, fill=-3e38,
                                    base=1 - P, pattern=[[0, 1]], channel_multiplier=1).then_inc(s_masks, 1)
            pool.wait_ge(s_camax, 1)
            nc.gpsimd.partition_all_reduce(camax_all[:, :, :].rearrange("p a b -> p (a b)"),
                                           camax[:, :, :].rearrange("p a b -> p (a b)"), P,
                                           bass.bass_isa.ReduceOp.max).then_inc(s_camax_all, 1)

            def hidden_share(b):
                pool.wait_ge(s_wm, b + 1)
                pool.wait_ge(s_suf, T // 2)
                if b:
                    pool.wait_ge(s_o_used, 2 * b)
                for i in range(2):
                    nc.gpsimd.tensor_tensor(
                        HV[:, i].rearrange("p (h d) -> p h d", h=HEADS),
                        SUFV[:, 2 * b + i].rearrange("p (h d) -> p h d", h=HEADS),
                        WM[:, b % 2, i].unsqueeze(2).broadcast_to([P, HEADS, DH]), ALU.mult).then_inc(s_hv, 1)

            def estimate_rstd(n, h):
                pool.wait_ge(s_ve, n + 1)
                ts = slice(h * HT, (h + 1) * HT)
                nc.gpsimd.tensor_tensor(rstd0[:, ts], ve[:, ts], neg_half[:, ts],
                                        ALU.pow).then_inc(s_rstd0, 1)

            def estimate_rstd2(n, g):
                pool.wait_ge(s_ve, n + 1)
                ts = slice(2 * g, 2 * g + 2)
                nc.gpsimd.tensor_tensor(rstd0[:, ts], ve[:, ts], neg_half[:, ts],
                                        ALU.pow).then_inc(s_rstd0, 1)

            for h in range(2):
                estimate_rstd(h, h)
            pool.wait_ge(s_ct, 16)
            nc.gpsimd.tensor_copy(KS[:, 0], CT).then_inc(s_kparts, 1)
            pool.wait_ge(s_kparts, 1)
            nc.gpsimd.tensor_tensor(KR, CT, KS[:, 0], ALU.subtract).then_inc(s_pool, 1)
            pool.wait_ge(s_pool, 5)
            nc.gpsimd.tensor_copy(KS[:, 1], KR).then_inc(s_kparts, 1)
            pool.wait_ge(s_kparts, 2)
            nc.gpsimd.tensor_tensor(KS[:, 2], KR, KS[:, 1], ALU.subtract).then_inc(s_kparts, 1)
            done.n = 5
            def weights_low(i):
                _, hi, lo = weight_block(i)
                pool.wait_ge(s_whi, i + 1)
                src = STG[:, i % 2] if len(hi.shape) == 2 else STG[:, i % 2].rearrange("p (c d) -> p c d", d=D)
                nc.gpsimd.tensor_tensor(lo, src, hi, ALU.subtract).then_inc(s_wlo, 1)

            for i in range(6):
                weights_low(i)
            for h in range(2):
                estimate_rstd(2 + h, h)
            pool.wait_ge(s_w0, 3)
            pool.wait_ge(s_ctx, 16)
            nc.gpsimd.memset(VA[:, :, :, DH:DH + 1], 1.0).then_inc(s_va, 1)
            nc.gpsimd.tensor_copy(VA[:, :, :, 0:DH], CN.rearrange("p t (h d) -> p t h d", h=HEADS)
                                  ).then_inc(s_va, 1)
            pool.wait_ge(s_kparts_out, 16 * KC)
            pool.wait_ge(s_va, 2)
            nc.gpsimd.memset(KST[0][ROWS:ROWS + 3], 1.0).then_inc(s_va, 1)
            pool.wait_ge(s_va, 3)
            for i in range(6, EARLY):
                weights_low(i)
            pool.wait_ge(s_down, DOWNS)
            pool.wait_ge(s_wlo, EARLY)
            nc.gpsimd.memset(KST[1][ROWS:ROWS + 3], 1.0).then_inc(s_va, 1)
            pool.wait_ge(s_va, 4)
            for h in range(2):
                estimate_rstd(4 + h, h)
            for b in range(B):
                for i in C_BLOCKS[b]:
                    if i == C_BLOCKS[B - 1][1]:
                        estimate_rstd2(8, 2)
                    weights_low(i)
                if b == B - 2:
                    for g in range(2):
                        estimate_rstd2(6 + g, g)
                hidden_share(b)
            pool.wait_ge(s_pool, 5)
            nc.gpsimd.iota(iota_tile[:, :], [[1, TILES]], base=0, channel_multiplier=0,
                           allow_small_or_imprecise_dtypes=True).then_inc(s_dconst, 1)
            nc.gpsimd.iota(iota_full[:, :], [[P, T]], base=0, channel_multiplier=0,
                           allow_small_or_imprecise_dtypes=True).then_inc(s_dconst, 1)
            nc.gpsimd.tensor_copy(ones_b[:, :], ones[:, :]).then_inc(s_dconst, 1)
            nc.gpsimd.affine_select(out=before_b[:, :], in_=ones[:, :], compare_op=ALU.is_gt, fill=0.0,
                                    base=0, pattern=[[1, P]], channel_multiplier=-1).then_inc(s_dconst, 1)
            estimate_rstd2(9, 3)
            for i in D_BLOCKS:
                weights_low(i)
            pool.wait_ge(s_fill, 16)
            pool.wait_ge(s_slot, 1)
            pool.wait_ge(s_dhl, T)
            pool.wait_ge(s_dhhi, T)
            for t in range(T):
                for k in range(2):
                    pool.indirect_dma_start(sorted_rows[:, :],
                                            bass.IndirectOffsetOnAxis(ap=SLOT[:, k, t:t + 1], axis=0),
                                            DHL[:, t].rearrange("p s d -> p (s d)").bitcast(U32), None
                                            ).then_inc(s_scat, 16)
            for q in range(2):
                pool.wait_ge(s_yst[q], 16 * ((TILES + 1 - q) // 2))
            for t in range(T):
                for k in range(2):
                    pool.indirect_dma_start(YG[:, t, k], None, routed_rows[:, :],
                                            bass.IndirectOffsetOnAxis(ap=SLOT[:, k, t:t + 1], axis=0)
                                            ).then_inc(s_yg[t], 16)

        @block.scalar
        def _(act):
            done = Count(s_act)
            act.dma_start(CT, ctx_t).then_inc(s_ct, 16)
            act.dma_start(g_raw[:, :], gates2.partition_broadcast(P)).then_inc(s_g, 16)
            act.dma_start(GWR, gate_w).then_inc(s_wl0, 16)
            act.dma_start(B1A[:, :], b1a).then_inc(s_wl0, 16)
            act.wait_ge(s_g, 16)
            nc.scalar.activation(tg[:, :], g_raw[:, :], ACT.Tanh).then_inc(s_tg, 1)
            act.wait_ge(s_wl0, 80)
            for raw, dst in ((WRAW, W1A[:, 0].rearrange("p c k h -> p (c k h)")),
                             (WRAW2, W2A[:, 0].rearrange("p c d -> p (c d)")),
                             (GWR.rearrange("p k e -> p (k e)"), GWA[:, 0].rearrange("p k e -> p (k e)"))):
                nc.scalar.activation(dst, raw, ACT.Copy, scale=W_SCALE).then_inc(s_act, 1)
            done.n = 3
            def weights_high(i):
                _, hi, _ = weight_block(i)
                if i == 8:
                    act.wait_ge(s_va, 2)
                    act.wait_ge(s_suf_ps, T // 2)
                    act.wait_ge(s_kparts_out, 16 * KC)
                if i == EARLY:
                    act.wait_ge(s_down, DOWNS)
                if i == MIDDLE:
                    act.wait_ge(s_p2, 12 * (B - 1))
                if i == LATE:
                    act.wait_ge(s_p2, 12 * B)
                if i == LATE + 2:
                    act.wait_ge(s_dhl, T)
                if i == LATE + 4:
                    act.wait_ge(s_r, 2)
                act.wait_ge(s_stg[i % 2], 16 * (i // 2 + 1))
                nc.scalar.activation(STG[:, i % 2], STG[:, i % 2], ACT.Copy, scale=W_SCALE).then_inc(s_wscaled, 1)
                act.wait_ge(s_wscaled, i + 1)
                src = STG[:, i % 2] if len(hi.shape) == 2 else STG[:, i % 2].rearrange("p (c d) -> p c d", d=D)
                nc.scalar.activation(hi, src, ACT.Copy).then_inc(s_whi, 1)

            for i in range(3):
                weights_high(i)
            for h in range(2):
                act.wait_ge(s_xqt_ps, h + 1)
                nc.scalar.activation(XQT[:, h].rearrange("p k n -> p (k n)"), bank[h][:, :].bitcast(BF16),
                                     ACT.Copy).then_inc(s_xqt, 1)
            for i in range(3, 6):
                weights_high(i)
            act.wait_ge(s_w0, 3)
            for j in range(T // 2):
                act.wait_ge(s_suf_ps, j + 1)
                nc.scalar.activation(SUFV[:, 2 * j:2 * j + 2].rearrange("p t d -> p (t d)"), bank[4 + j][:, :],
                                     ACT.Copy).then_inc(s_suf, 1)
            for t in range(T):
                act.wait_ge(s_hs, t + 1)
                nc.scalar.activation(HHL[:, t, 0], HS[:, t], ACT.Copy).then_inc(s_hhi, 1)
                if t % 2:
                    j = t // 2
                    act.wait_ge(s_ht_ps, j + 1)
                    nc.scalar.activation(
                        HT_[:, :, :, j * 2 * P:(j + 1) * 2 * P].rearrange("p k s (t n) -> p t (k s) n", t=2),
                        bank[j][:, :].bitcast(F16).rearrange("p (t a n) -> p t a n", t=2, n=P),
                        ACT.Copy).then_inc(s_ht, 1)
            act.wait_ge(s_z12, 1)
            nc.scalar.activation(th[:, :], z12[:, :], ACT.Tanh,
                                 scale=0.5 / (X_SCALE * W_SCALE)).then_inc(s_th, 1)
            for i in range(2 * CA):
                c = i % CA
                act.wait_ge(s_up, i + 1)
                if i >= 2:
                    act.wait_ge(s_ghl, i - 1)
                nc.scalar.activation(G32[:, i % 2], bank[i % 4][:, :], ACT.Gelu, bias=B1A[:, c:c + 1],
                                     scale=1.0 / (X_SCALE * W_SCALE)).then_inc(s_gelu, 1)
                if i % 5 == 3:
                    weights_high(6 + i // 5)
            for i in range(10, EARLY):
                weights_high(i)
            def repeat_parts(b):
                for i in range(2):
                    act.wait_ge(s_q1, 2 * b + i + 1)
                    nc.scalar.activation(QTOK[:, i, :, 1:3], QTOK[:, i, :, 0:1].broadcast_to([P, HEADS, 2, DH]),
                                         ACT.Copy).then_inc(s_qtok, 1)
                    nc.scalar.activation(QTOK[:, i, :, 4:5], QTOK[:, i, :, 3:4], ACT.Copy).then_inc(s_qtok, 1)

            def store_q(b, j):
                if b and j == 0:
                    act.wait_ge(s_p2, 12 * (b - 1))
                act.wait_ge(s_qt_ps, 4 * b + j + 1)
                i, h0 = j // 2, 8 * (j % 2)
                nc.scalar.activation(QST[b % 2][0:ROWS, h0:h0 + 8, i * P:(i + 1) * P],
                                     qt_bank[:, :].bitcast(BF16)[0:ROWS].rearrange("p (h n) -> p h n", h=8),
                                     ACT.Copy).then_inc(s_qst, 1)

            def store_minus_max(b):
                act.wait_ge(s_nm_ps, b + 1)
                if b:
                    act.wait_ge(s_nmrow, 48 * b)
                nc.scalar.activation(NMS[:, :], qt_bank[:, :].bitcast(BF16)[0:3 * HEADS, 0:S],
                                     ACT.Copy).then_inc(s_nms, 1)
                act.wait_ge(s_nms, b + 1)
                act.dma_start(QST[b % 2][ROWS:ROWS + 1], NMS[0:HEADS, :]).then_inc(s_nmrow, 16)

            def hidden_weight(b):
                act.wait_ge(s_wz, b + 1)
                if b >= 2:
                    act.wait_ge(s_o_used, 2 * (b - 1))
                nc.scalar.activation(WM[:, b % 2].rearrange("p i h -> p (i h)"),
                                     WZ[:, b % 2].rearrange("p i h -> p (i h)"), ACT.Exp,
                                     scale=0.25).then_inc(s_wm, 1)

            def exponentials(b, u):
                n = 12 * b + u
                act.wait_ge(s_p2, n + 1)
                if n >= 6:
                    act.wait_ge(s_pv, (n - 6) // 3 + 1)
                nc.scalar.activation(PT[:, n % 6], s2_bank[n % 2][:, :], ACT.Exp, scale=0.25).then_inc(s_pt, 1)

            def store_o(b, j):
                act.wait_ge(s_pv, 4 * b + 2 * j + 2)
                if b:
                    act.wait_ge(s_o_ps, 2 * b)
                nc.scalar.activation(OT[:, j], o_bank[j][:, :], ACT.Copy).then_inc(s_ot, 1)

            def row_high(t):
                act.wait_ge(s_dhs, t + 1)
                nc.scalar.activation(DHL[:, t, 0], DHS[:, t], ACT.Copy).then_inc(s_dhhi, 1)

            def rows_t_out(j):
                act.wait_ge(s_dt_ps, j + 1)
                nc.scalar.activation(
                    DHT[:, :, :, j * 2 * P:(j + 1) * 2 * P].rearrange("p k s (t n) -> p t (k s) n", t=2),
                    bank[j % 2][:, :].bitcast(F16).rearrange("p (t a n) -> p t a n", t=2, n=P),
                    ACT.Copy).then_inc(s_dht, 1)

            repeat_parts(0)
            for j in range(4):
                store_q(0, j)
            repeat_parts(1)
            store_minus_max(0)
            hidden_weight(0)
            act.dma_start(B1D[:, :, :], b1d).then_inc(s_dw_small, 16)
            act.dma_start(RW2R[:, :], rw2).then_inc(s_dw_small, 16)
            for b in range(B):
                blocks = list(C_BLOCKS[b])
                for u in range(12):
                    if b + 1 < B and u < 4:
                        store_q(b + 1, u)
                    exponentials(b, u)
                    if b == B - 1 and u < HT:
                        row_high(u)
                    if b == B - 1 and u in (7, 10):
                        rows_t_out(u // 10)
                    if u == 8:
                        store_o(b, 0)
                    if blocks and (u in SPLIT_AT[:3] or (b == B - 1 and u == SPLIT_AT[3])):
                        weights_high(blocks.pop(0))
                    if u == 10 and b + 1 < B:
                        store_minus_max(b + 1)
                        hidden_weight(b + 1)
                store_o(b, 1)
                if b + 2 < B:
                    repeat_parts(b + 2)
            act.dma_start(RW1R, rw1).then_inc(s_dw_small, 16)
            act.wait_ge(s_hv, T)
            act.dma_start(B24[2 * E:3 * E, :], b2d).then_inc(s_dw_small, 16)
            for t in range(HT, T):
                if t == HT + 2:
                    for i in D_BLOCKS[:2]:
                        weights_high(i)
                row_high(t)
                if t == HT:
                    for src, dst in ((RW1R.rearrange("p k h -> p (k h)"), RW1[:, 0].rearrange("p k h -> p (k h)")),
                                     (RW2R[:, :], RW2[:, 0])):
                        act.wait_ge(s_dw_small, 64)
                        nc.scalar.activation(dst, src, ACT.Copy, scale=W_SCALE).then_inc(s_rwh, 1)
            weights_high(D_BLOCKS[2])
            for j in range(2, 4):
                rows_t_out(j)
            for h in range(2):
                act.wait_ge(s_r, h + 1)
                nc.scalar.activation(R32[:, h * 512:(h + 1) * 512], bank[4 + h][:, :], ACT.Gelu,
                                     scale=1.0 / (X_SCALE * W_SCALE)).then_inc(s_rg, 1)
            nc.scalar.activation(GB[:, :, :], B1D[:, :, :], ACT.Gelu).then_inc(s_gb, 1)
            act.wait_ge(s_dl, 1)
            nc.scalar.activation(PR[:, :, :], LG[:, :, :], ACT.Exp,
                                 scale=1.0 / (G_SCALE * W_SCALE)).then_inc(s_ex, 1)
            for i in D_BLOCKS[3:]:
                weights_high(i)

            def tile_gelu(j, q, first=False):
                e = act.value_load(EID[0:1, bass.ds(j, 1)], min_val=0, max_val=E - 1)
                for hb in range(2):
                    act.wait_ge(s_dup, 2 * j + hb + 1)
                    if not first:
                        act.wait_ge(s_dgl, 2 * j + hb - 3)
                    for c in range(4 * hb, 4 * hb + 4):
                        ins = nc.scalar.activation(GD[:, q, c * P:(c + 1) * P],
                                                   up_bank[2 * q + hb][:, (c % 4) * P:(c % 4 + 1) * P], ACT.Gelu,
                                                   bias=B1D[:, e, c:c + 1], scale=1.0 / (X_SCALE * W_SCALE))
                    ins.then_inc(s_dg, 1)

            act.wait_ge(s_eid, 1)
            act.wait_ge(s_base_used, T)
            for j in range(HEAD):
                tile_gelu(j, j % 2, first=j < 2)
            with act.Fori(0, LOOPS) as i:
                for r in range(UNROLL):
                    tile_gelu(UNROLL * i + HEAD + r, (HEAD + r) % 2)
            for j in range(TAIL, TILES):
                tile_gelu(j, j % 2)

        @block.tensor
        def _(pe):
            pe.wait_ge(s_const, 5)
            for h in range(2):
                pe.wait_ge(s_xq, h + 1)
                v = bank[h][:, :].bitcast(BF16).rearrange("p (k t n) -> p k t n", k=KC, t=HT)
                for t in range(HT):
                    for k in range(KC):
                        mm = nc.tensor.transpose(v[:, k, t], XQ[:, h * HT + t, k * P:(k + 1) * P], ident_b[:, :])
                mm.then_inc(s_xqt_ps, 1)
            for t in range(T):
                if t % HT == 0:
                    pe.wait_ge(s_xqt, t // HT + 1)
                if t == 0:
                    pe.wait_ge(s_cqt, 1)
                if t >= 4:
                    pe.wait_ge(s_da_used, t - 3)
                b = t // 2
                for k in range(KC):
                    mm = nc.tensor.matmul(bank[4 + t % 4][:, k * D:(k + 1) * D],
                                          XQT[:, t // HT, k, (t % HT) * P:(t % HT + 1) * P],
                                          CQT[:, k, b * S:(b + 1) * S], start=True, stop=True)
                mm.then_inc(s_da, 1)
            pe.wait_ge(s_da_used, T)
            pe.wait_ge(s_ctx, 16)
            pe.wait_ge(s_masks, 4)
            for t in range(T):
                o = bank[4 + t // 2][:, (t % 2) * D:(t % 2 + 1) * D]
                mm = nc.tensor.matmul(o, after[:, :], CN[:, t], start=True, stop=bool(t % 2))
                if t % 2 == 0:
                    nc.tensor.matmul(o, ones[:, :], CN[:, t + 1], start=False, stop=True)
                else:
                    mm.then_inc(s_suf_ps, 1)
            for t in range(T):
                pe.wait_ge(s_hhl, t + 1)
                pe.wait_ge(s_hhi, t + 1)
                v = bank[t // 2][:, :].bitcast(F16).rearrange("p (t k s n) -> p t k s n", t=2, k=KC, s=2)
                for k in range(KC):
                    for s in range(2):
                        mm = nc.tensor.transpose(v[:, t % 2, k, s], HHL[:, t, s, k * P:(k + 1) * P],
                                                 ident_h[:, :])
                if t % 2:
                    mm.then_inc(s_ht_ps, 1)
            pe.wait_ge(s_w0, 3)
            pe.wait_ge(s_act, 3)
            pe.wait_ge(s_suf, T // 2)
            passes = ((0, 0), (0, 1), (1, 0))
            for t in range(T):
                if t % 2 == 0:
                    pe.wait_ge(s_ht, t // 2 + 1)
                n = 0
                for a, b in passes:
                    for k in range(KC):
                        mm = nc.tensor.matmul(bank[4][:, t * E:(t + 1) * E], HT_[:, k, a, t * P:(t + 1) * P],
                                              GWA[:, b, k], start=(n == 0), stop=(n == 5))
                        n += 1
            mm.then_inc(s_lg, 1)
            for i in range(2 * CA):
                c, h = i % CA, i // CA
                if i >= 4:
                    pe.wait_ge(s_gelu, i - 3)
                n = 0
                for a, b in passes:
                    for k in range(KC):
                        mm = nc.tensor.matmul(bank[i % 4][:, :], W1A[:, b, c, k],
                                              HT_[:, k, a, h * 512:(h + 1) * 512],
                                              start=(n == 0), stop=(n == 5))
                        n += 1
                mm.then_inc(s_up, 1)
                if i == 12:
                    pe.wait_ge(s_gates, 1)
                    for t in range(T):
                        mm = nc.tensor.transpose(bank[5 + t // 4][0:E + 1, (t % 4) * P:(t % 4 + 1) * P],
                                                 gates[:, t], ident[:, :])
                    mm.then_inc(s_gt_ps, 1)
            pe.wait_ge(s_gt, 1)
            n = 0
            for t in range(T):
                if t % HT == 0:
                    pe.wait_ge(s_ghl, CA * (t // HT + 1))
                for c in range(0, CA, 2):
                    if n >= DOWN_BANKS:
                        pe.wait_ge(s_down_used, n - DOWN_BANKS + 1)
                    dst = bank[4 + n % DOWN_BANKS]
                    shared = c >= E
                    q = 0
                    for cc in (c, c + 1):
                        o = dst[:, 0:D] if shared else dst[:, (cc - c) * D:(cc - c + 1) * D]
                        for a, b in passes:
                            last = q == (6 if shared else 3) - 1
                            mm = nc.tensor.matmul(o, GHL[:, a, cc, t * P:(t + 1) * P], W2A[:, b, cc],
                                                  start=(q == 0), stop=(last and not shared))
                            q += 1
                        if not shared:
                            q = 0
                    if shared:
                        mm = nc.tensor.matmul(dst[:, 0:D], gates_t[:, t * P:(t + 1) * P], B9[:, :],
                                              start=False, stop=True)
                    mm.then_inc(s_down, 1)
                    n += 1

            def transpose_q(b, j):
                i, h0 = j // 2, 8 * (j % 2)
                if j % 2 == 0:
                    pe.wait_ge(s_qtok, 4 * b + 2 * i + 2)
                if b or j:
                    pe.wait_ge(s_qst, 4 * b + j)
                if b and j == 0:
                    pe.wait_ge(s_nms, b)
                v = qt_bank[:, :].bitcast(BF16).rearrange("p (h n) -> p h n", h=8)
                for h in range(8):
                    mm = nc.tensor.transpose(v[0:ROWS, h], QTOK[:, i, h0 + h].rearrange("p r d -> p (r d)"),
                                             ident_b[:, :])
                mm.then_inc(s_qt_ps, 1)

            def scores_for_max(b, u):
                n = 12 * b + u
                if u == 0:
                    pe.wait_ge(s_kst[b % 2], 96 * (b // 2 + 1))
                    pe.wait_ge(s_qst, 4 * b + 2)
                if u == 4:
                    pe.wait_ge(s_qst, 4 * b + 4)
                if n >= 2:
                    pe.wait_ge(s_mx, n - 1)
                i = 0 if u < 4 else 1
                nh, nk = (4, P) if i == 0 else (2, S)
                h0 = 4 * u if i == 0 else 2 * (u - 4)
                v = s1_bank[n % 2][:, :].rearrange("p (h n) -> p h n", h=nh)
                nc.tensor.matmul(v[:, :, nk - P:nk], ident_b[:, :],
                                 neg_mask[:, :].unsqueeze(1).broadcast_to([P, nh, P]),
                                 start=True, stop=False, skip_group_check=True)
                for h in range(nh):
                    mm = nc.tensor.matmul(v[:, h], QST[b % 2][0:ROWS, h0 + h, i * P:(i + 1) * P],
                                          KST[b % 2][0:ROWS, h0 + h, 0:nk], start=False, stop=h == nh - 1,
                                          skip_group_check=True)
                mm.then_inc(s_p1, 1)

            def transpose_minus_max(b):
                pe.wait_ge(s_nmp, b + 1)
                pe.wait_ge(s_qst, 4 * b + 4)
                v = qt_bank[:, :].bitcast(BF16)
                for i in range(2):
                    mm = nc.tensor.transpose(v[0:3 * HEADS, i * P:(i + 1) * P],
                                             NMP[:, i].rearrange("p s h -> p (s h)"), ident_b[:, :])
                mm.then_inc(s_nm_ps, 1)

            def scores_by_key(b, u):
                n = 12 * b + u
                g, w = u // 3, u % 3
                if u == 0:
                    pe.wait_ge(s_nmrow, 48 * (b + 1))
                if n >= 2:
                    pe.wait_ge(s_pt, n - 1)
                k, nh, nq = (0, 2, S) if w < 2 else (1, 4, P)
                h0 = 4 * g + (2 * w if w < 2 else 0)
                v = s2_bank[n % 2][:, :].rearrange("p (h n) -> p h n", h=nh)
                nc.tensor.matmul(v[:, :, 0:P], neg_mask[:, :], ident_b[:, :].unsqueeze(1).broadcast_to([P, nh, P]),
                                 start=True, stop=False, skip_group_check=True)
                for h in range(nh):
                    mm = nc.tensor.matmul(v[:, h], KST[b % 2][0:ROWS + 3, h0 + h, k * P:(k + 1) * P],
                                          QST[b % 2][0:ROWS + 3, h0 + h, k * P:S], start=False, stop=h == nh - 1,
                                          skip_group_check=True)
                mm.then_inc(s_p2, 1)

            def weighted_values(b, g):
                n = 12 * b + 3 * g
                pe.wait_ge(s_pt, n + 3)
                if g % 2 == 0 and b:
                    pe.wait_ge(s_ot, 2 * (b - 1) + g // 2 + 1)
                c0 = (g % 2) * S
                ob = o_bank[g // 2]
                for j in range(4):
                    p = PT[:, (n + j // 2) % 6].rearrange("p (h n) -> p h n", h=2)[:, j % 2]
                    nc.tensor.matmul(ob[32 * j:32 * j + DH + 1, c0:c0 + S], VA[:, 2 * b, 4 * g + j], p,
                                     start=True, stop=False, skip_group_check=True)
                for j in range(4):
                    p = PT[:, (n + 2) % 6].rearrange("p (h n) -> p h n", h=4)[:, j]
                    mm = nc.tensor.matmul(ob[32 * j:32 * j + DH + 1, c0 + P:c0 + S], VA[:, 2 * b + 1, 4 * g + j],
                                          p, start=False, stop=True, skip_group_check=True)
                mm.then_inc(s_pv, 1)

            def transpose_o(b, i):
                pe.wait_ge(s_ot, 2 * b + 2)
                if b or i:
                    pe.wait_ge(s_o_used, 2 * b + i)
                for g in range(4):
                    c0 = (g % 2) * S + i * P
                    mm = nc.tensor.transpose(ot_bank[:, g * P:(g + 1) * P], OT[:, g // 2, c0:c0 + P], ident[:, :])
                mm.then_inc(s_o_ps, 1)

            def transpose_rows(j):
                if j >= 2:
                    pe.wait_ge(s_dht, j - 1)
                v = bank[j % 2][:, :].bitcast(F16).rearrange("p (t k s n) -> p t k s n", t=2, k=KC, s=2)
                for i in range(2):
                    pe.wait_ge(s_dhl, 2 * j + i + 1)
                    for k in range(KC):
                        for s in range(2):
                            mm = nc.tensor.transpose(v[:, i, k, s], DHL[:, 2 * j + i, s, k * P:(k + 1) * P],
                                                     ident_h[:, :])
                mm.then_inc(s_dt_ps, 1)

            pe.wait_ge(s_down_used, DOWNS)
            pe.wait_ge(s_va, 4)
            pe.wait_ge(s_obank, 2)
            for j in range(4):
                transpose_q(0, j)
            for u in range(12):
                scores_for_max(0, u)
            transpose_minus_max(0)
            for b in range(B):
                for u in range(12):
                    if b + 1 < B and u < 4:
                        transpose_q(b + 1, u)
                    if b and u in (0, 2):
                        transpose_o(b - 1, u // 2)
                    if b + 1 < B and 3 <= u < 9:
                        for m in (2 * u - 6, 2 * u - 5):
                            scores_for_max(b + 1, m)
                    if b + 1 < B and u == 11:
                        transpose_minus_max(b + 1)
                    if b == B - 1 and u in (6, 9):
                        transpose_rows(u // 9)
                    scores_by_key(b, u)
                    if u % 3 == 2 and u >= 5:
                        weighted_values(b, u // 3 - 1)
                weighted_values(b, 3)
            for i in range(2):
                transpose_o(B - 1, i)
            for j in range(2, 4):
                transpose_rows(j)
            pe.wait_ge(s_rw, 2)
            for h in range(2):
                pe.wait_ge(s_dht, 2 * h + 2)
                n = 0
                for a, b in passes:
                    for k in range(KC):
                        mm = nc.tensor.matmul(bank[4 + h][:, :], RW1[:, b, k], DHT[:, k, a, h * 512:(h + 1) * 512],
                                              start=(n == 0), stop=(n == 5))
                        n += 1
                mm.then_inc(s_r, 1)
            for t in range(T):
                pe.wait_ge(s_rhl, t // HT + 1)
                for n, (a, b) in enumerate(passes):
                    mm = nc.tensor.matmul(bank[6][:, t * E:(t + 1) * E], RHL[:, a, t * P:(t + 1) * P], RW2[:, b],
                                          start=(n == 0), stop=(n == 2))
            mm.then_inc(s_dlg, 1)
            pe.wait_ge(s_m, 1)
            pe.wait_ge(s_dconst, 4)
            rank = bank[4][:, 0:T * E]
            nc.tensor.matmul(rank, before_b[:, :], MSB[:, :, :].rearrange("p t e -> p (t e)"),
                             start=True, stop=False, skip_group_check=True)
            for t in range(T - 1):
                nc.tensor.matmul(rank[:, (t + 1) * E:].rearrange("p (t e) -> p t e", e=E), ones_b[:, :],
                                 MSB[:, t:t + 1].broadcast_to([P, T - 1 - t, E]), start=False,
                                 stop=t == T - 2, skip_group_check=True)
            for t in range(T):
                mm = nc.tensor.matmul(bank[5][:, 0:2 * E], ones_b[:, :],
                                      M01B[:, t].rearrange("p k e -> p (k e)"), start=t == 0, stop=t == T - 1)
            mm.then_inc(s_rank, 1)
            pe.wait_ge(s_gb16, 2)
            experts = list(range(E // 2, E)) + list(range(E // 2))
            for n, e in enumerate(experts):
                if n == E // 2:
                    pe.wait_ge(s_wlo, BLOCKS)
                for c in range(HC8):
                    for s in range(2):
                        mm = nc.tensor.matmul(bank[7][0:2 * E, 0:D], GB16[:, c, e], W2[:, e, c, s],
                                              start=(n == 0 and c == 0 and s == 0),
                                              stop=(n == E - 1 and c == HC8 - 1 and s == 1))
            mm.then_inc(s_ce, 1)
            pe.wait_ge(s_coef, 1)
            for t in range(T):
                mm = nc.tensor.transpose(bank[2 + t // 4][0:3 * E, (t % 4) * P:(t % 4 + 1) * P], COEF[:, t],
                                         ident[:, :])
            mm.then_inc(s_cf_ps, 1)
            pe.wait_ge(s_cf, 2)
            pe.wait_ge(s_ce_sb, 1)
            for t in range(T):
                if t >= 2:
                    pe.wait_ge(s_base_used, t - 1)
                nc.tensor.matmul(bank[4 + t % 2][:, 0:D], COEF_T[0:3 * E, t * P:(t + 1) * P], B24[0:3 * E, :],
                                 start=True, stop=True).then_inc(s_base, 1)

            def transpose_tile(j, q, m, first=False):
                pe.wait_ge(s_xr[q], 16 * m + 16)
                if not first:
                    pe.wait_ge(s_xt, j - 1)
                v = bank[q][:, :].bitcast(F16)[:, 0:4 * P].rearrange("p (k s n) -> p k s n", k=KC, s=2)
                for k in range(KC):
                    for s in range(2):
                        mm = nc.tensor.transpose(v[:, k, s], XR[:, q, s, k * P:(k + 1) * P], ident_h[:, :])
                mm.then_inc(s_xt_ps, 1)

            def expert_of(j):
                return pe.value_load(EID[0:1, bass.ds(j, 1)], min_val=0, max_val=E - 1)

            def tile_up(j, q, e, first=False):
                pe.wait_ge(s_xt, j + 1)
                for hb in range(2):
                    if not first:
                        pe.wait_ge(s_dg, 2 * j + hb - 3)
                    for c in range(4 * hb, 4 * hb + 4):
                        n = 0
                        for a, b in passes:
                            for k in range(KC):
                                mm = nc.tensor.matmul(up_bank[2 * q + hb][:, (c % 4) * P:(c % 4 + 1) * P],
                                                      W1[:, e, b, k, c * P:(c + 1) * P], XT[:, q, k, a],
                                                      start=(n == 0), stop=(n == 5))
                                n += 1
                    mm.then_inc(s_dup, 1)

            def tile_down(j, q, e, first=False):
                if not first:
                    pe.wait_ge(s_ys, j - 1)
                for hb in range(2):
                    pe.wait_ge(s_dgl, 2 * j + hb + 1)
                    for c in range(4 * hb, 4 * hb + 4):
                        nc.tensor.matmul(bank[6 + q][:, :], GDL[:, q, 0, c * P:(c + 1) * P],
                                         W2[:, e, c].rearrange("p s d -> p (s d)"), start=(c == 0), stop=False,
                                         skip_group_check=True)
                        mm = nc.tensor.matmul(bank[6 + q][:, 0:D], GDL[:, q, 1, c * P:(c + 1) * P],
                                              W2[:, e, c, 0], start=False, stop=(c == HC8 - 1),
                                              skip_group_check=True)
                mm.then_inc(s_dd, 1)

            pe.wait_ge(s_eid, 1)
            pe.wait_ge(s_base_used, T)
            transpose_tile(0, 0, 0, first=True)
            for j in range(HEAD):
                e = expert_of(j)
                tile_up(j, j % 2, e, first=j < 2)
                transpose_tile(j + 1, (j + 1) % 2, (j + 1) // 2, first=j == 0)
                if j:
                    tile_down(j - 1, (j - 1) % 2, e_before, first=True)
                e_before = e
            with pe.Fori(0, LOOPS) as i:
                e_before = expert_of(UNROLL * i + HEAD - 1)
                for r in range(UNROLL):
                    j, q = UNROLL * i + HEAD + r, (HEAD + r) % 2
                    e = expert_of(j)
                    tile_up(j, q, e)
                    transpose_tile(j + 1, 1 - q, UNROLL // 2 * i + (HEAD + r + 1) // 2)
                    tile_down(j - 1, 1 - q, e_before)
                    e_before = e
            e_before = expert_of(TAIL - 1)
            for j in range(TAIL, TILES):
                e = expert_of(j)
                tile_up(j, j % 2, e)
                if j + 1 < TILES:
                    transpose_tile(j + 1, (j + 1) % 2, (j + 1) // 2)
                tile_down(j - 1, (j - 1) % 2, e_before)
                e_before = e
            tile_down(TILES - 1, (TILES - 1) % 2, e_before)

        @block.vector
        def _(dve):
            done = Count(s_dve)

            def step(instruction):
                dve.wait_ge(s_dve, done.on(instruction))

            def mark(instruction):
                return done.on(instruction)

            def here():
                dve.wait_ge(s_dve, done.n)

            v = nc.vector

            def ln_variance(h, n, size=HT):
                ts = slice(h * size, (h + 1) * size)
                for t in range(h * size, (h + 1) * size):
                    mark(v.bn_stats(stats[:, t], X[:, t]))
                here()
                for t in range(h * size, (h + 1) * size):
                    mark(v.bn_aggr(mv[:, t], stats[:, t]))
                here()
                v.tensor_scalar(ve[:, ts], mv[:, ts, 1], EPS, None, ALU.add).then_inc(s_ve, 1)

            def ln_rstd(h, n, scale, size=HT):
                ts = slice(h * size, (h + 1) * size)
                dve.wait_ge(s_rstd0, n + 1)
                dve.wait_ge(s_ve, n + 1)
                step(v.tensor_tensor(rt[:, ts], ve[:, ts], rstd0[:, ts], ALU.mult))
                step(v.tensor_tensor(rt[:, ts], rt[:, ts], rstd0[:, ts], ALU.mult))
                step(v.tensor_scalar(rt[:, ts], rt[:, ts], -0.5 * scale, 1.5 * scale, ALU.mult, ALU.add))
                step(v.tensor_tensor(rstd[:, ts], rt[:, ts], rstd0[:, ts], ALU.mult))

            def round_fp8(dst, val, tmp):
                step(v.tensor_scalar(tmp.bitcast(U32), val.bitcast(U32), 0x7F800000, None, ALU.bitwise_and))
                step(v.tensor_scalar(tmp, tmp, FP8_MIN_NORMAL, ROUND_FP8, ALU.max, ALU.mult))
                step(v.tensor_tensor(val, val, tmp, ALU.add))
                return v.tensor_tensor(dst, val, tmp, ALU.subtract)

            dve.wait_ge(s_ct, 16)
            v.tensor_reduce(camax[:, :, :], CT.rearrange("p k (t n) -> p k t n", t=T), AX.X, ALU.max,
                            apply_absolute_value=True).then_inc(s_camax, 1)
            for h in range(2):
                dve.wait_ge(s_x[h], 16)
                ln_variance(h, h)
            dve.wait_ge(s_camax_all, 1)
            step(v.tensor_scalar(sw[:, :, :], camax_all[:, :, :], 1e-6, None, ALU.max))
            step(v.reciprocal(rw[:, :, :], sw[:, :, :]))
            step(v.tensor_scalar(rw[:, :, :], rw[:, :, :], FP8_MAX, None, ALU.mult))
            dve.wait_ge(s_tg, 1)
            step(v.tensor_scalar(sw[:, :, :], sw[:, :, :], tg[:, 0:1], 1.0 / FP8_MAX, ALU.mult, ALU.mult))
            step(v.tensor_tensor(VC.rearrange("p k (t n) -> p (k t) n", t=T),
                                 CT.rearrange("p k (t n) -> p (k t) n", t=T),
                                 rw[:, :, :].rearrange("p k t -> p (k t)").unsqueeze(2).broadcast_to([P, KC * T, P]),
                                 ALU.mult))
            round_fp8(CQT, VC, C2).then_inc(s_cqt, 1)
            for h in range(2):
                ts = slice(h * HT, (h + 1) * HT)
                ln_rstd(h, h, 1.0)
                for t in range(h * HT, (h + 1) * HT):
                    mark(v.tensor_scalar(XC[:, t], X[:, t], mv[:, t, 0:1], rstd[:, t:t + 1],
                                         ALU.subtract, ALU.mult))
                here()
                xk = XC[:, ts].rearrange("p t (k n) -> p (t k) n", k=KC)
                vk = V[:, ts].rearrange("p t (k n) -> p (t k) n", k=KC)
                flat = lambda a: a[:, ts].rearrange("p t k -> p (t k)")
                step(v.tensor_reduce(flat(xamax), xk, AX.X, ALU.max, apply_absolute_value=True))
                step(v.tensor_scalar(flat(sx), flat(xamax), 1e-4, None, ALU.max))
                step(v.reciprocal(flat(rx), flat(sx)))
                step(v.tensor_scalar(flat(rx), flat(rx), FP8_MAX, None, ALU.mult))
                step(v.tensor_scalar(flat(sx), flat(sx), 1.0 / FP8_MAX, None, ALU.mult))
                step(v.tensor_tensor(vk, xk, flat(rx).unsqueeze(2).broadcast_to([P, HT * KC, P]), ALU.mult))
                round_fp8(XQ[:, ts], V[:, ts], C1[:, ts]).then_inc(s_xq, 1)
            for nb in range(2):
                for k in range(KC):
                    mark(v.tensor_tensor(
                        sxw[:, :, nb, k].rearrange("p (b i) -> p b i", i=2),
                        sx[:, :, k].rearrange("p (b i) -> p b i", i=2),
                        sw[:, k, :].rearrange("p (b n) -> p b n", n=2)[:, :, nb:nb + 1].broadcast_to([P, B, 2]),
                        ALU.mult))
            here()
            for t in range(T):
                dve.wait_ge(s_da, t + 1)
                for k in range(KC):
                    for nb in range(2):
                        ins = v.scalar_tensor_tensor(
                            out=X[:, t, nb * P:(nb + 1) * P], in0=bank[4 + t % 4][:, k * D + nb * P:k * D + (nb + 1) * P],
                            scalar=sxw[:, t, nb, k:k + 1], in1=X[:, t, nb * P:(nb + 1) * P],
                            op0=ALU.mult, op1=ALU.add)
                        if (k, nb) == (KC - 1, 1):
                            ins.then_inc(s_da_used, 1)
                        else:
                            mark(ins)
                            if nb:
                                here()
            dve.wait_ge(s_da_used, T)
            dve.wait_ge(s_act, 3)
            dve.wait_ge(s_wl0, 80)
            for raw, w in ((GWR.rearrange("p k e -> p (k e)"), GWA.rearrange("p s k e -> p s (k e)")),
                           (WRAW, W1A.rearrange("p s c k h -> p s (c k h)")),
                           (WRAW2, W2A.rearrange("p s c d -> p s (c d)"))):
                v.scalar_tensor_tensor(out=w[:, 1], in0=raw, scalar=W_SCALE, in1=w[:, 0],
                                       op0=ALU.mult, op1=ALU.subtract).then_inc(s_w0, 1)
            step(v.tensor_scalar(B9[:, :], B9[:, :], G_SCALE * W_SCALE, None, ALU.mult))
            for h in range(2):
                ln_variance(h, 2 + h)
            for h in range(2):
                ln_rstd(h, 2 + h, X_SCALE)
                for t in range(h * HT, (h + 1) * HT):
                    v.tensor_scalar(HS[:, t], X[:, t], mv[:, t, 0:1], rstd[:, t:t + 1],
                                    ALU.subtract, ALU.mult).then_inc(s_hs, 1)
                for t in range(h * HT, (h + 1) * HT):
                    dve.wait_ge(s_hhi, t + 1)
                    v.tensor_tensor(HHL[:, t, 1], HS[:, t], HHL[:, t, 0], ALU.subtract).then_inc(s_hhl, 1)
            dve.wait_ge(s_lg, 1)
            step(v.tensor_copy(logits[:, :, :].rearrange("p t e -> p (t e)"), bank[4][:, 0:T * E]))
            for t in range(T):
                mark(v.max(top[:, t], logits[:, t]))
            here()
            for t in range(T):
                mark(v.max_index(topi[:, t], top[:, t], logits[:, t]))
            v.tensor_tensor(z12[:, :], top[:, :, 0], top[:, :, 1], ALU.subtract).then_inc(s_z12, 1)
            here()
            step(v.tensor_copy(topf[:, :, :], topi[:, :, 0:2]))
            for k, m in enumerate((mask0, mask1)):
                mark(v.tensor_tensor(m[:, :, :], iota_e[:, :].unsqueeze(1).broadcast_to([P, T, E]),
                                     topf[:, :, k:k + 1].broadcast_to([P, T, E]), ALU.is_equal))
            dve.wait_ge(s_th, 1)
            mark(v.tensor_scalar(wk[:, 0], th[:, :], 0.5, 0.5, ALU.mult, ALU.add))
            mark(v.tensor_scalar(wk[:, 1], th[:, :], -0.5, 0.5, ALU.mult, ALU.add))
            mark(v.memset(gates[:, :, E:E + 1], 1.0))
            here()
            for k, m in enumerate((mask0, mask1)):
                mark(v.tensor_tensor(m[:, :, :], m[:, :, :], wk[:, k].unsqueeze(2).broadcast_to([P, T, E]), ALU.mult))
            here()
            v.tensor_tensor(gates[:, :, 0:E], mask0[:, :, :], mask1[:, :, :], ALU.add).then_inc(s_gates, 1)
            dve.wait_ge(s_gates, 1)
            step(v.tensor_scalar(gates_s[:, :, :].rearrange("p t e -> p (t e)"),
                                 gates[:, :, :].rearrange("p t e -> p (t e)"), tg[:, 2:3],
                                 1.0 / (G_SCALE * W_SCALE), ALU.mult, ALU.mult))
            for i in range(2 * CA):
                c, h = i % CA, i // CA
                dve.wait_ge(s_gelu, i + 1)
                hi, lo = (GHL[:, s, c, h * 512:(h + 1) * 512] for s in range(2))
                step(v.tensor_scalar(hi, G32[:, i % 2], G_SCALE, None, ALU.mult))
                v.scalar_tensor_tensor(out=lo, in0=G32[:, i % 2], scalar=G_SCALE, in1=hi,
                                       op0=ALU.mult, op1=ALU.subtract).then_inc(s_ghl, 1)
                if i == 14:
                    dve.wait_ge(s_gt_ps, 1)
                    step(v.tensor_copy(gates_t[:, 0:512], bank[5][0:E + 1, :]))
                    v.tensor_copy(gates_t[:, 512:1024], bank[6][0:E + 1, :]).then_inc(s_gt, 1)
            n = 0
            for t in range(T):
                for c in range(0, CA, 2):
                    dve.wait_ge(s_down, n + 1)
                    src = bank[4 + n % DOWN_BANKS]
                    if c < E:
                        step(v.scalar_tensor_tensor(out=X[:, t], in0=src[:, 0:D], scalar=gates_s[:, t, c:c + 1],
                                                    in1=X[:, t], op0=ALU.mult, op1=ALU.add))
                        lastcol = src[:, D:2 * D]
                    else:
                        lastcol = src[:, 0:D]
                    e = min(c + 1, E)
                    v.scalar_tensor_tensor(out=X[:, t], in0=lastcol, scalar=gates_s[:, t, e:e + 1],
                                           in1=X[:, t], op0=ALU.mult, op1=ALU.add).then_inc(s_down_used, 1)
                    n += 1
                    dve.wait_ge(s_down_used, n)
            for j in range(2):
                v.memset(o_bank[j][:, :], 0.0).then_inc(s_obank, 1)

            def attention_q(b):
                if b:
                    dve.wait_ge(s_qt_ps, 4 * b)
                heads = lambda a: a.rearrange("p (h d) -> p h d", h=HEADS)
                for i in range(2):
                    t = 2 * b + i
                    step(v.tensor_scalar(HC[:, i], X[:, t], mv[:, t, 0:1], rstd[:, t:t + 1],
                                         ALU.subtract, ALU.mult))
                    step(v.tensor_copy(QTOK[:, i, :, 0], heads(HC[:, i])))
                    step(v.tensor_tensor(heads(RC[:, i]), heads(HC[:, i]), QTOK[:, i, :, 0], ALU.subtract))
                    step(v.tensor_copy(QTOK[:, i, :, 3], heads(RC[:, i])))
                    v.tensor_tensor(QTOK[:, i, :, 5], heads(RC[:, i]), QTOK[:, i, :, 3],
                                    ALU.subtract).then_inc(s_q1, 1)

            def maximum(b, u):
                n = 12 * b + u
                dve.wait_ge(s_p1, n + 1)
                i = 0 if u < 4 else 1
                nh = 4 if i == 0 else 2
                h0 = 4 * u if i == 0 else 2 * (u - 4)
                v.tensor_reduce(MX[:, b % 2, i, h0:h0 + nh], s1_bank[n % 2][:, :].rearrange("p (h n) -> p h n", h=nh),
                                AX.X, ALU.max).then_inc(s_mx, 1)

            def minus_maximum(b):
                dve.wait_ge(s_mx, 12 * (b + 1))
                p = b % 2
                step(v.tensor_tensor(NM[:, p], MX[:, p], floor[:, :].unsqueeze(2).broadcast_to([P, 2, HEADS]),
                                     ALU.max))
                mark(v.tensor_scalar(WZ[:, p], NM[:, p], -1.0, CAUSAL_FILL, ALU.mult, ALU.add))
                step(v.tensor_scalar(NMR[:, :, :], NM[:, p], -1.0, None, ALU.mult))
                v.tensor_scalar(WZ[:, p], WZ[:, p], 0.0, None, ALU.min).then_inc(s_wz, 1)
                if b:
                    dve.wait_ge(s_nm_ps, b)
                step(v.tensor_copy(NMP[:, :, 0], NMR[:, :, :]))
                step(v.tensor_tensor(NMR2[:, :, :], NMR[:, :, :], NMP[:, :, 0], ALU.subtract))
                step(v.tensor_copy(NMP[:, :, 1], NMR2[:, :, :]))
                v.tensor_tensor(NMP[:, :, 2], NMR2[:, :, :], NMP[:, :, 1], ALU.subtract).then_inc(s_nmp, 1)

            def attention_out(b, i):
                t = 2 * b + i
                dve.wait_ge(s_wm, b + 1)
                step(v.tensor_scalar(DENR[:, :], WM[:, b % 2, i], hidden_n[:, i:i + 1], None, ALU.mult))
                dve.wait_ge(s_o_ps, t + 1)
                o = ot_bank[:, :].rearrange("p (h c) -> p h c", c=32)
                step(v.tensor_tensor(DEN[:, :], o[:, :, DH], DENR[:, :], ALU.add))
                step(v.reciprocal(DENR[:, :], DEN[:, :]))
                dve.wait_ge(s_hv, t + 1)
                num = NUM[:, :].rearrange("p (h d) -> p h d", h=HEADS)
                v.tensor_tensor(num, o[:, :, 0:DH], HV[:, i].rearrange("p (h d) -> p h d", h=HEADS),
                                ALU.add).then_inc(s_o_used, 1)
                dve.wait_ge(s_o_used, t + 1)
                step(v.tensor_tensor(num, num, DENR[:, :].unsqueeze(2).broadcast_to([P, HEADS, DH]), ALU.mult))
                step(v.scalar_tensor_tensor(out=X[:, t], in0=NUM[:, :], scalar=tg[:, 1:2], in1=X[:, t],
                                            op0=ALU.mult, op1=ALU.add))

            dve.wait_ge(s_masks, 4)
            def scaled_rows(g):
                ln_rstd(g, 6 + g, X_SCALE, 2)
                for t in (2 * g, 2 * g + 1):
                    v.tensor_scalar(DHS[:, t], X[:, t], mv[:, t, 0:1], rstd[:, t:t + 1],
                                    ALU.subtract, ALU.mult).then_inc(s_dhs, 1)

            def row_low(t):
                dve.wait_ge(s_dhhi, t + 1)
                v.tensor_tensor(DHL[:, t, 1], DHS[:, t], DHL[:, t, 0], ALU.subtract).then_inc(s_dhl, 1)

            for h in range(2):
                ln_variance(h, 4 + h)
            ln_rstd(0, 4, 1.0)
            attention_q(0)
            ln_rstd(1, 5, 1.0)
            for u in range(4):
                maximum(0, u)
            attention_q(1)
            for u in range(4, 12):
                maximum(0, u)
            minus_maximum(0)
            for b in range(B):
                if b:
                    for i in range(2):
                        attention_out(b - 1, i)
                if b + 1 < B:
                    for u in range(12):
                        maximum(b + 1, u)
                    minus_maximum(b + 1)
                if b + 2 < B:
                    attention_q(b + 2)
                if b == B - 2:
                    for g in range(2):
                        ln_variance(g, 6 + g, 2)
                    dve.wait_ge(s_qt_ps, 4 * B)
                    for g in range(2):
                        scaled_rows(g)
                if b == B - 1:
                    ln_variance(2, 8, 2)
                    for t in range(HT):
                        row_low(t)
                    scaled_rows(2)
            for i in range(2):
                attention_out(B - 1, i)
            v.memset(rt[:, 0:1], 0.0).then_inc(s_x3_done, 1)
            ln_variance(3, 9, 2)
            scaled_rows(3)
            for t in range(HT, T):
                row_low(t)
            dve.wait_ge(s_rwh, 2)
            dve.wait_ge(s_dw_small, 64)
            v.scalar_tensor_tensor(out=RW1[:, 1].rearrange("p k h -> p (k h)"),
                                   in0=RW1R.rearrange("p k h -> p (k h)"), scalar=W_SCALE,
                                   in1=RW1[:, 0].rearrange("p k h -> p (k h)"),
                                   op0=ALU.mult, op1=ALU.subtract).then_inc(s_rw, 1)
            v.scalar_tensor_tensor(out=RW2[:, 1], in0=RW2R[:, :], scalar=W_SCALE, in1=RW2[:, 0],
                                   op0=ALU.mult, op1=ALU.subtract).then_inc(s_rw, 1)
            for h in range(2):
                dve.wait_ge(s_rg, h + 1)
                hi, lo = (RHL[:, s, h * 512:(h + 1) * 512] for s in range(2))
                src = R32[:, h * 512:(h + 1) * 512]
                step(v.tensor_scalar(hi, src, G_SCALE, None, ALU.mult))
                v.scalar_tensor_tensor(out=lo, in0=src, scalar=G_SCALE, in1=hi,
                                       op0=ALU.mult, op1=ALU.subtract).then_inc(s_rhl, 1)
            dve.wait_ge(s_dlg, 1)
            step(v.tensor_copy(LG[:, :, :].rearrange("p t e -> p (t e)"), bank[6][:, 0:T * E]))
            step(v.tensor_reduce(LM[:, :], LG[:, :, :], AX.X, ALU.max))
            v.tensor_tensor(LG[:, :, :], LG[:, :, :], LM[:, :].unsqueeze(2).broadcast_to([P, T, E]),
                            ALU.subtract).then_inc(s_dl, 1)
            dve.wait_ge(s_ex, 1)
            step(v.tensor_reduce(LM[:, :], PR[:, :, :], AX.X, ALU.add))
            step(v.reciprocal(LM[:, :], LM[:, :]))
            step(v.tensor_tensor(PR[:, :, :], PR[:, :, :], LM[:, :].unsqueeze(2).broadcast_to([P, T, E]), ALU.mult))
            for t in range(T):
                mark(v.max(DTOP[:, t], PR[:, t]))
            here()
            for t in range(T):
                mark(v.max_index(DTOPI[:, t], DTOP[:, t], PR[:, t]))
            here()
            step(v.tensor_copy(DTOPF[:, :, :], DTOPI[:, :, 0:2]))
            for k in range(2):
                mark(v.tensor_tensor(M01[:, :, k], iota_e[:, :].unsqueeze(1).broadcast_to([P, T, E]),
                                     DTOPF[:, :, k:k + 1].broadcast_to([P, T, E]), ALU.is_equal))
            here()
            mark(v.tensor_copy(M01B[:, :, :, :].rearrange("p t k e -> p (t k e)"),
                               M01[:, :, :, :].rearrange("p t k e -> p (t k e)")))
            v.tensor_tensor(MSB[:, :, :], M01[:, :, 0], M01[:, :, 1], ALU.add).then_inc(s_m, 1)
            here()
            dve.wait_ge(s_rank, 1)
            step(v.tensor_copy(NE01[:, :, :].rearrange("p k e -> p (k e)"), bank[5][:, 0:2 * E]))
            step(v.tensor_tensor(NE[:, :], NE01[:, 0], NE01[:, 1], ALU.add))
            dve.wait_ge(s_dconst, 4)
            step(v.tensor_tensor(USED[:, :, :], NE[:, :].unsqueeze(2).broadcast_to([P, E, T]),
                                 iota_full[:, :].unsqueeze(1).broadcast_to([P, E, T]), ALU.is_gt))
            step(v.tensor_reduce(NT[:, :], USED[:, :, :], AX.X, ALU.add))
            step(v.tensor_tensor_scan(ENDT[:, :], ones[:, 0:E], NT[:, :], 0.0, ALU.mult, ALU.add))
            step(v.tensor_tensor(BASE[:, :], ENDT[:, :], NT[:, :], ALU.subtract))
            step(v.tensor_scalar(BASE[:, :], BASE[:, :], float(P), None, ALU.mult))
            step(v.tensor_tensor(SLOTQ[:, :, :], bank[4][:, 0:T * E].rearrange("p (t e) -> p t e", e=E),
                                 BASE[:, :].unsqueeze(1).broadcast_to([P, T, E]), ALU.add))
            for k in range(2):
                mark(v.tensor_tensor(SLOTM[:, k], M01[:, :, k], SLOTQ[:, :, :], ALU.mult))
            here()
            step(v.tensor_reduce(SLOTF[:, :, :], SLOTM[:, :, :, :], AX.X, ALU.add))
            v.tensor_copy(SLOT[:, :, :], SLOTF[:, :, :]).then_inc(s_slot, 1)
            step(v.tensor_tensor(EOF_[:, :, :], iota_tile[:, :].unsqueeze(2).broadcast_to([P, TILES, E]),
                                 ENDT[:, :].unsqueeze(1).broadcast_to([P, TILES, E]), ALU.is_ge))
            step(v.tensor_reduce(EIDF[:, :], EOF_[:, :, :], AX.X, ALU.add))
            step(v.tensor_scalar(EIDF[:, :], EIDF[:, :], float(E - 1), None, ALU.min))
            v.tensor_copy(EID[:, :], EIDF[:, :]).then_inc(s_eid, 1)
            dve.wait_ge(s_gb, 1)
            step(v.tensor_scalar(GBH[:, :, :], GB[:, :, :], G_SCALE, None, ALU.mult))
            step(v.scalar_tensor_tensor(out=GBL[:, :, :], in0=GB[:, :, :], scalar=G_SCALE, in1=GBH[:, :, :],
                                        op0=ALU.mult, op1=ALU.subtract))
            step(v.memset(GB16.rearrange("p c e x -> p (c e x)").bitcast(F32), 0.0))
            for s, part in enumerate((GBH, GBL)):
                spread = GB16.rearrange("p c e x -> p c (e x)")[:, :, s * E::2 * E + 1]
                v.tensor_copy(spread, part[:, :, :].rearrange("p e c -> p c e")).then_inc(s_gb16, 1)
            for k in range(2):
                mark(v.tensor_scalar(WKD[:, k], DTOP[:, :, k], tg[:, 3:4], 1.0 / (G_SCALE * W_SCALE),
                                     ALU.mult, ALU.mult))
            step(v.tensor_scalar(ACTV[:, :, :], NE01[:, :, :], 0.0, None, ALU.is_gt))
            for k in range(2):
                step(v.tensor_scalar(CF[:, k], M01[:, :, k], -1.0, 1.0, ALU.mult, ALU.add))
                step(v.tensor_tensor(CF[:, k], CF[:, k], ACTV[:, k].unsqueeze(1).broadcast_to([P, T, E]), ALU.mult))
                step(v.tensor_tensor(CF[:, k], CF[:, k], DTOP[:, :, k:k + 1].broadcast_to([P, T, E]), ALU.mult))
                step(v.tensor_tensor(SLOTM[:, k], M01[:, :, k], DTOP[:, :, k:k + 1].broadcast_to([P, T, E]), ALU.mult))
            for r in range(2):
                mark(v.tensor_tensor(COEF[:, :, r * E:(r + 1) * E], CF[:, 0], CF[:, 1], ALU.add))
            step(v.tensor_tensor(SLOTQ[:, :, :], SLOTM[:, 0], SLOTM[:, 1], ALU.add))
            v.tensor_tensor(COEF[:, :, 2 * E:3 * E], COEF[:, :, 0:E], SLOTQ[:, :, :], ALU.add).then_inc(s_coef, 1)
            dve.wait_ge(s_cf_ps, 1)
            for h in range(2):
                v.tensor_copy(COEF_T[0:3 * E, h * 512:(h + 1) * 512], bank[2 + h][0:3 * E, :]).then_inc(s_cf, 1)
            dve.wait_ge(s_ce, 1)
            v.tensor_scalar(B24[0:2 * E, :], bank[7][0:2 * E, 0:D], 1.0 / (G_SCALE * W_SCALE), None,
                            ALU.mult).then_inc(s_ce_sb, 1)
            for t in range(T):
                dve.wait_ge(s_base, t + 1)
                v.scalar_tensor_tensor(out=X[:, t], in0=bank[4 + t % 2][:, 0:D], scalar=tg[:, 3:4], in1=X[:, t],
                                       op0=ALU.mult, op1=ALU.add).then_inc(s_base_used, 1)

            def rows_t(j, q, first=False):
                dve.wait_ge(s_xt_ps, j + 1)
                if not first:
                    dve.wait_ge(s_dup, 2 * j - 2)
                v.tensor_copy(XT[:, q].rearrange("p k s n -> p (k s n)"),
                              bank[q][:, :].bitcast(F16)[:, 0:4 * P]).then_inc(s_xt, 1)

            def split_hidden(j, q, hb, first=False):
                dve.wait_ge(s_dg, 2 * j + hb + 1)
                if not first:
                    dve.wait_ge(s_dd, j - 1)
                src = GD[:, q, hb * 512:(hb + 1) * 512]
                hi, lo = (GDL[:, q, s, hb * 512:(hb + 1) * 512] for s in range(2))
                v.tensor_scalar(hi, src, G_SCALE, None, ALU.mult).then_inc(s_dgh, 1)
                dve.wait_ge(s_dgh, 2 * j + hb + 1)
                v.scalar_tensor_tensor(out=lo, in0=src, scalar=G_SCALE, in1=hi,
                                       op0=ALU.mult, op1=ALU.subtract).then_inc(s_dgl, 1)

            def tile_out(j, q, m, first=False):
                dve.wait_ge(s_dd, j + 1)
                if not first:
                    dve.wait_ge(s_yst[q], 16 * m)
                v.tensor_copy(YS[:, q], bank[6 + q][:, 0:D]).then_inc(s_yh, 1)
                dve.wait_ge(s_yh, j + 1)
                v.tensor_tensor(YS[:, q], YS[:, q], bank[6 + q][:, D:2 * D], ALU.add).then_inc(s_ys, 1)

            rows_t(0, 0, first=True)
            for j in range(HEAD):
                split_hidden(j, j % 2, 0, first=j < 2)
                rows_t(j + 1, (j + 1) % 2, first=j == 0)
                split_hidden(j, j % 2, 1, first=j < 2)
                if j:
                    tile_out(j - 1, (j - 1) % 2, 0, first=True)
            with dve.Fori(0, LOOPS) as i:
                for r in range(UNROLL):
                    j, q = UNROLL * i + HEAD + r, (HEAD + r) % 2
                    split_hidden(j, q, 0)
                    rows_t(j + 1, 1 - q)
                    split_hidden(j, q, 1)
                    tile_out(j - 1, 1 - q, UNROLL // 2 * i + (HEAD + r - 1) // 2)
            for j in range(TAIL, TILES):
                split_hidden(j, j % 2, 0)
                if j + 1 < TILES:
                    rows_t(j + 1, (j + 1) % 2)
                split_hidden(j, j % 2, 1)
                tile_out(j - 1, (j - 1) % 2, (j - 1) // 2)
            tile_out(TILES - 1, (TILES - 1) % 2, (TILES - 1) // 2)
            for t in range(T):
                dve.wait_ge(s_yg[t], 32)
                step(v.scalar_tensor_tensor(out=X[:, t], in0=YG[:, t, 0], scalar=WKD[:, 0, t:t + 1], in1=X[:, t],
                                            op0=ALU.mult, op1=ALU.add))
                v.scalar_tensor_tensor(out=X[:, t], in0=YG[:, t, 1], scalar=WKD[:, 1, t:t + 1], in1=X[:, t],
                                       op0=ALU.mult, op1=ALU.add).then_inc(s_xout, 1)


def lay_out(x, ctx_2048, g_xattn, g_ffn, L0_ffn_gate_w, L0_ffn_w1, L0_ffn_b1, L0_ffn_w2, L0_ffn_b2,
            L0_ffn_shared_w1, L0_ffn_shared_b1, L0_ffn_shared_w2, L0_ffn_shared_b2,
            L1_ffn_rw1, L1_ffn_rw2, L1_ffn_w1, L1_ffn_b1, L1_ffn_w2, L1_ffn_b2):
    tokens, d = x.shape[0] * x.shape[1], x.shape[2]
    k = d // P
    experts = L0_ffn_gate_w.shape[1]
    shared = L0_ffn_shared_w1.shape[1] // P
    hidden = L1_ffn_w1.shape[2]
    ctx = ctx_2048.reshape(tokens, d)
    return {
        "x": x.reshape(tokens, d),
        "ctx": ctx,
        "ctx_t": ctx.T.reshape(k, P, tokens).transpose(1, 0, 2),
        "gates": np.concatenate([g_xattn, g_ffn]),
        "gate_w": L0_ffn_gate_w.reshape(k, P, experts).transpose(1, 0, 2),
        "l0_w1": np.concatenate([L0_ffn_w1.reshape(experts, k, P, P).transpose(2, 0, 1, 3),
                                 L0_ffn_shared_w1.reshape(k, P, shared, P).transpose(1, 2, 0, 3)], 1),
        "l0_b1": np.concatenate([L0_ffn_b1, L0_ffn_shared_b1.reshape(shared, P)], 0).T,
        "l0_w2": np.concatenate([L0_ffn_w2.transpose(1, 0, 2),
                                 L0_ffn_shared_w2.reshape(shared, P, d).transpose(1, 0, 2)], 1),
        "l0_b2": np.concatenate([L0_ffn_b2, L0_ffn_shared_b2[None]], 0),
        "router_w1": L1_ffn_rw1.reshape(k, P, -1).transpose(1, 0, 2),
        "router_w2": L1_ffn_rw2,
        "l1_w1": L1_ffn_w1.reshape(experts, k, P, hidden).transpose(2, 0, 1, 3),
        "l1_b1": L1_ffn_b1.reshape(experts, hidden // P, P).transpose(2, 0, 1),
        "l1_w2": L1_ffn_w2.reshape(experts, hidden // P, P, d).transpose(2, 0, 1, 3),
        "l1_b2": L1_ffn_b2,
    }


def kernel(**inputs):
    import concourse.bacc as bacc
    from concourse.bass_utils import run_bass_kernel_spmd

    shape = inputs["x"].shape
    nc = bacc.Bacc("TRN2", target_bir_lowering=False, num_devices=1)
    arrays, args = {}, []
    for name, a in lay_out(**{n: np.asarray(a) for n, a in inputs.items()}).items():
        a = np.ascontiguousarray(a)
        arrays[f"in_{name}_dram"] = a
        args.append(nc.dram_tensor(f"in_{name}_dram", a.shape, mybir.dt.from_np(a.dtype),
                                   kind="ExternalInput").ap())
    args.append(nc.dram_tensor("out_dram", (shape[0] * shape[1], shape[2]), F32, kind="ExternalOutput").ap())
    flamingo(nc, *args)
    result = run_bass_kernel_spmd(nc, [arrays], core_ids=[0])
    return result.results[0]["out_dram"].reshape(shape)
```

```python
from contextlib import ExitStack

import numpy as np

import concourse.bass as bass
from concourse import mybir

F32 = mybir.dt.float32
BF16 = mybir.dt.bfloat16
F16 = mybir.dt.float16
I32 = mybir.dt.int32
U32 = mybir.dt.uint32
ALU = mybir.AluOpType
ACT = mybir.ActivationFunctionType
AX = mybir.AxisListType

P = 128
EPS = 1e-5
FP8_MAX = 448.0
ROUND_FP8 = 1.5 * 2.0 ** 20
FP8_MIN_NORMAL = 2.0 ** -6
X_SCALE = 256.0
W_SCALE = 64.0
G_SCALE = 16.0
CAUSAL_FILL = -1e4 * 4.0
NEVER = -1e30
Q_PART = (0, 0, 0, 1, 1, 2)
K_PART = (0, 1, 2, 0, 1, 0)


class Count:

    def __init__(self, sem, step=1):
        self.sem, self.step, self.n = sem, step, 0

    def on(self, instruction):
        instruction.then_inc(self.sem, self.step)
        self.n += self.step
        return self.n


def flamingo(nc, x, ctx, ctx_t, gates2, gate_w, w1a, b1a, w2a, b2a, rw1, rw2, w1d, b1d, w2d, b2d, out):
    N, D = x.shape
    T = N // P
    KC = D // P
    E = gate_w.shape[2]
    B = 4
    S = N // B
    HT = T // 2
    CA = w1a.shape[1]

    with ExitStack() as stack:
        def sb(name, shape, dt):
            return stack.enter_context(nc.sbuf_tensor(name, shape, dt))

        def sem(name):
            return stack.enter_context(nc.semaphore(name))

        HEADS = 16
        DH = D // HEADS
        ROWS = len(Q_PART) * DH
        HID = w1d.shape[3]
        HC8 = HID // P
        PAIRS = 2 * N
        TILES = PAIRS // P + E - 1
        HEAD, UNROLL = 3, 4
        LOOPS = (TILES - HEAD - 1) // UNROLL
        TAIL = HEAD + UNROLL * LOOPS
        sorted_rows = nc.dram_tensor("sorted_rows", [TILES * P, D], U32).ap()
        routed_rows = nc.dram_tensor("routed_rows", [TILES * P, D], F32).ap()
        k_parts = nc.dram_tensor("k_parts", [3, D, N], BF16).ap()

        W1_ = sb("W1", [P, 64 * 256], F32)
        arena = sb("arena", [P, 113 * 256], F32)

        def at(kb, shape, dt):
            size = 1
            for n in shape:
                size *= n
            words = size * mybir.dt.size(dt) // 4
            o = int(kb * 256)
            v = arena[:, o:o + words].bitcast(dt) if dt != F32 else arena[:, o:o + words]
            if len(shape) == 1:
                return v
            names = "abcd"[:len(shape)]
            return v.rearrange(f"p ({' '.join(names)}) -> p {' '.join(names)}",
                               **{c: n for c, n in zip(names, shape)})

        X = sb("X", [P, T, D], F32)
        ident = sb("ident", [P, P], F32)
        ident_h = sb("ident_h", [P, P], F16)
        ident_b = sb("ident_b", [P, P], BF16)
        iota_e = sb("iota_e", [P, E], F32)
        g_raw = sb("g_raw", [P, 4], F32)
        tg = sb("tg", [P, 4], F32)
        stats = sb("stats", [P, T, 6], F32)
        mv = sb("mv", [P, T, 2], F32)
        ve = sb("ve", [P, T], F32)
        rstd0 = sb("rstd0", [P, T], F32)
        rt = sb("rt", [P, T], F32)
        rstd = sb("rstd", [P, T], F32)
        neg_half = sb("neg_half", [P, T], F32)
        KS = W1_[:, 48 * 256:60 * 256].bitcast(BF16).rearrange("p (s k n) -> p s k n", s=3, k=KC)
        KR = W1_[:, 40 * 256:48 * 256].rearrange("p (k n) -> p k n", k=KC)
        CN = W1_[:, 32 * 256:40 * 256].rearrange("p (t d) -> p t d", t=T)
        KST = [W1_[:, 56 * 256:64 * 256].bitcast(BF16).rearrange("p (h n) -> p h n", h=HEADS),
               at(68, [HEADS, S], BF16)]
        QST = [at(0, [HEADS, S], BF16), at(8, [HEADS, S], BF16)]
        HC = at(16, [2, D], F32)
        RC = at(18, [2, D], F32)
        QTOK = at(22, [2, HEADS, len(Q_PART), DH], BF16)
        OT = at(107, [2, 512], F32)
        PT = at(76, [6, 512], F32)
        VA = at(89, [T, HEADS, DH + 1], F32)
        SUFV = at(99, [T, D], F32)
        neg_mask = sb("neg_mask", [P, P], BF16)
        after = sb("after", [P, P], F32)
        ones = sb("ones", [P, P], F32)
        hidden_n = sb("hidden_n", [P, 2], F32)
        floor = sb("floor", [P, 2], F32)
        MX = sb("MX", [P, 2, 2, HEADS], F32)
        NM = sb("NM", [P, 2, 2, HEADS], F32)
        NMR = sb("NMR", [P, 2, HEADS], F32)
        NMR2 = sb("NMR2", [P, 2, HEADS], F32)
        NMP = sb("NMP", [P, 2, 3, HEADS], BF16)
        NMS = sb("NMS", [3 * HEADS, S], BF16)
        WZ = sb("WZ", [P, 2, 2, HEADS], F32)
        WM = sb("WM", [P, 2, 2, HEADS], F32)
        DEN = sb("DEN", [P, HEADS], F32)
        DENR = sb("DENR", [P, HEADS], F32)
        HV = sb("HV", [P, 2, D], F32)
        NUM = at(88, [D], F32)
        W1 = W1_[:, :].bitcast(F16).rearrange("p (e s k n) -> p e s k n", e=E, s=2, k=KC)
        W2 = at(0, [E, HC8, 2, D], F16)
        STG = sb("STG", [P, 2, HID], F32)
        DHS = at(24, [T, D], F32)
        DHL = at(64, [T, 2, D], F16)
        DHT = at(16, [KC, 2, N], F16)
        R32 = at(88, [N], F32)
        RHL = at(92, [2, N], F16)
        GB16 = at(96, [HC8, E, 2 * E], F16)
        COEF_T = at(98, [N], F32)
        B24 = at(102, [D], F32)
        XR = at(104, [2, 2, D], F16)
        XT = at(106, [2, KC, 2, P], F16)
        YS = at(108, [2, D], F32)
        GD = at(64, [2, HID], F32)
        GDL = at(88, [2, 2, HID], F16)
        YG = at(72, [T, 2, D], F32)
        RW1R = at(97.5, [KC, P], F32)
        RW1 = at(111, [2, KC, P], F16)
        RW2R = sb("RW2R", [P, E], F32)
        RW2 = sb("RW2", [P, 2, E], F16)
        B1D = sb("B1D", [P, E, HC8], F32)
        GB = sb("GB", [P, E, HC8], F32)
        GBH = sb("GBH", [P, E, HC8], F16)
        GBL = sb("GBL", [P, E, HC8], F16)
        before_b = sb("before_b", [P, P], BF16)
        ones_b = sb("ones_b", [P, P], BF16)
        iota_tile = sb("iota_tile", [P, TILES], F32)
        iota_full = sb("iota_full", [P, T], F32)
        LG = at(112, [T, E], F32)
        LM = sb("LM", [P, T], F32)
        PR = at(112.25, [T, E], F32)
        DTOP = sb("DTOP", [P, T, 8], F32)
        DTOPI = sb("DTOPI", [P, T, 8], U32)
        DTOPF = sb("DTOPF", [P, T, 2], F32)
        M01 = at(112.5, [T, 2, E], F32)
        M01B = sb("M01B", [P, T, 2, E], BF16)
        MSB = sb("MSB", [P, T, E], BF16)
        NE01 = sb("NE01", [P, 2, E], F32)
        NE = sb("NE", [P, E], F32)
        USED = sb("USED", [P, E, T], F32)
        NT = sb("NT", [P, E], F32)
        ENDT = sb("ENDT", [P, E], F32)
        BASE = sb("BASE", [P, E], F32)
        SLOTQ = sb("SLOTQ", [P, T, E], F32)
        SLOTM = sb("SLOTM", [P, 2, T, E], F32)
        SLOTF = sb("SLOTF", [P, 2, T], F32)
        SLOT = sb("SLOT", [P, 2, T], U32)
        EOF_ = sb("EOF", [P, TILES, E], F32)
        EIDF = sb("EIDF", [P, TILES], F32)
        EID = sb("EID", [P, TILES], I32)
        ACTV = sb("ACTV", [P, 2, E], F32)
        COEF = sb("COEF", [P, T, 3 * E], F32)
        CF = sb("CF", [P, 2, T, E], F32)
        WKD = sb("WKD", [P, 2, T], F32)
        CT = W1_[:, 24 * 256:32 * 256].rearrange("p (k n) -> p k n", k=KC)
        XC = at(8, [T, D], F32)
        V = at(16, [T, D], F32)
        C1 = at(24, [T, D], F32)
        XQ = at(32, [T, D], BF16)
        XQT = at(36, [2, KC, HT * P], BF16)
        VC = at(40, [KC, N], F32)
        C2 = at(48, [KC, N], F32)
        CQT = at(56, [KC, N], BF16)
        HS = at(0, [T, D], F32)
        HHL = at(8, [T, 2, D], F16)
        HT_ = at(16, [KC, 2, N], F16)
        G32 = at(24, [2, 512], F32)
        GHL = at(28, [2, CA, N], F16)
        W1A = at(68, [2, CA, KC, P], F16)
        W2A = at(78, [2, CA, D], F16)
        GWA = at(88, [2, KC, E], F16)
        WRAW = at(89, [CA * D], F32)
        WRAW2 = at(99, [CA * D], F32)
        GWR = at(109, [KC, E], F32)
        B1A = sb("B1A", [P, CA], F32)
        B9 = at(111, [D], F32)[0:E + 1]
        camax = sb("camax", [P, KC, T], F32)
        camax_all = sb("camax_all", [P, KC, T], F32)
        xamax = sb("xamax", [P, T, KC], F32)
        sx = sb("sx", [P, T, KC], F32)
        rx = sb("rx", [P, T, KC], F32)
        sw = sb("sw", [P, KC, T], F32)
        rw = sb("rw", [P, KC, T], F32)
        sxw = sb("sxw", [P, T, 2, KC], F32)
        logits = LG
        top = DTOP
        topi = DTOPI
        topf = DTOPF
        mask0 = CF[:, 0]
        mask1 = CF[:, 1]
        z12 = sb("z12", [P, T], F32)
        th = sb("th", [P, T], F32)
        wk = WKD
        gates = sb("gates", [P, T, E + 1], F32)
        tgs = sb("tgs", [P, 1], F32)
        gates_t = at(107, [N], F32)[0:E + 1]
        gates3 = sb("gates3", [P, T, 3, E + 1], BF16)
        gates3_t = at(4, [N], BF16)[0:3 * (E + 1)]
        select = sb("select", [3 * (E + 1), E + 1], BF16)
        GG = at(0, [2, 512], F32)

        bank = [stack.enter_context(nc.psum_tensor(f"bank{i}", [P, 512], F32)) for i in range(8)]

        s1_bank, s2_bank, ot_bank, o_bank, qt_bank = bank[0:2], bank[2:4], bank[4], bank[5:7], bank[7]
        T_BANK = (qt_bank, s1_bank[0], s1_bank[1], qt_bank)
        up_bank = bank[2:6]
        UP_BANKS = len(up_bank)

        s_x = [sem(f"x_landed{i}") for i in range(2)]
        s_ct = sem("ctx_t_landed")
        s_g = sem("layer_gates_landed")
        s_wl0 = sem("l0_weights_landed")
        s_const = sem("constants_made")
        s_dve = sem("dve_step")
        s_act = sem("act_step")
        s_pool = sem("pool_step")
        s_camax = sem("ctx_amax_local")
        s_camax_all = sem("ctx_amax_all")
        s_ve = sem("variance_ready")
        s_rstd0 = sem("rstd_estimated")
        s_tg = sem("tanh_gates_ready")
        s_xq = sem("x_quantised")
        s_xqt_ps = sem("xq_transposed")
        s_xqt = sem("xq_t_in_sbuf")
        s_rw8 = sem("ctx_inverse_scales_ready")
        s_vc = sem("ctx_scaled_to_fp8_range")
        s_c2 = sem("ctx_rounding_constants_ready")
        s_cadd = sem("ctx_rounding_constants_added")
        s_cqt = sem("ctx_quantised")
        s_da = sem("stage_a_product")
        s_da_used = sem("stage_a_product_used")
        s_w0 = sem("l0_first_weights_split")
        s_w2low = sem("l0_second_weights_split")
        s_hhl = sem("ln_split")
        s_hs = sem("ln_scaled")
        s_hhi = sem("ln_high")
        s_ht_ps = sem("ln_transposed")
        s_ht = sem("ln_t_in_sbuf")
        s_lg = sem("logits_product")
        s_z12 = sem("logit_gap")
        s_th = sem("tanh_gap")
        s_gates = sem("gates_ready")
        s_gt_ps = sem("gates_transposed")
        s_gt = sem("gates_t_in_sbuf")
        s_gt3 = sem("gate_parts_t_in_sbuf")
        s_up = sem("up_product")
        s_gelu = sem("gelu_done")
        s_ghl = sem("hidden_split")
        s_sel = sem("selector_made")
        s_bc = sem("gate_rows_broadcast")
        s_gg = sem("hidden_gated")
        s_ghi = sem("hidden_high")
        s_down = sem("down_product")
        s_down_used = sem("down_product_used")
        s_ctx = sem("ctx_landed")
        s_khi = sem("k_high_part")
        s_kr = sem("k_remainder")
        s_kparts = sem("k_parts_split")
        s_kparts_out = sem("k_parts_stored")
        s_kst = [sem(f"k_stack_landed{i}") for i in range(2)]
        s_masks = sem("masks_made")
        s_va = sem("v_with_ones_ready")
        s_suf_ps = sem("suffix_sums_product")
        s_suf = sem("suffix_sums_ready")
        s_q1 = sem("q_parts_ready")
        s_qtok = sem("q_parts_repeated")
        s_qt_ps = sem("q_stack_transposed")
        s_qst = sem("q_stack_in_sbuf")
        s_p1 = sem("scores_for_maximum")
        s_mx = sem("maximum_taken")
        s_nmp = sem("minus_maximum_split")
        s_nm_ps = sem("minus_maximum_transposed")
        s_nms = sem("minus_maximum_in_sbuf")
        s_nmrow = sem("minus_maximum_rows_landed")
        s_wz = sem("hidden_exponent")
        s_wm = sem("hidden_weight")
        s_p2 = sem("scores_by_key")
        s_pt = sem("exponentials_ready")
        s_pv = sem("values_product")
        s_ot = sem("values_product_in_sbuf")
        s_o_ps = sem("attention_transposed")
        s_o_used = sem("attention_used")
        s_hv = sem("hidden_share_ready")
        s_obank = sem("o_banks_cleared")
        s_zero = sem("zeros_made")
        s_fill = sem("sorted_rows_cleared")
        s_dw_small = sem("d_small_weights_landed")
        s_stg = [sem(f"weights_landed{i}") for i in range(2)]
        s_wscaled = sem("weights_scaled")
        s_whi = sem("weights_high")
        s_wlo = sem("weights_low")
        s_wlate = sem("late_weights_low")
        s_dconst = sem("d_constants_made")
        s_rw = sem("router_weights_split")
        s_rwh = sem("router_weights_high")
        s_dhs = sem("d_ln_scaled")
        s_dhhi = sem("d_ln_high")
        s_dhl = sem("d_ln_split")
        s_dt_ps = sem("d_ln_transposed")
        s_dht = sem("d_ln_t_in_sbuf")
        s_r = sem("router_hidden_product")
        s_rg = sem("router_gelu")
        s_rhl = sem("router_hidden_split")
        s_dlg = sem("router_logits")
        s_dl = sem("router_logits_less_max")
        s_ex = sem("router_exponentials")
        s_m = sem("choice_masks")
        s_rank = sem("ranks_counted")
        s_slot = sem("slots_ready")
        s_eid = sem("tile_experts_ready")
        s_scat = sem("rows_scattered")
        s_gb = sem("gelu_of_b1")
        s_gb16 = sem("gelu_of_b1_spread")
        s_ce = sem("idle_outputs_product")
        s_ce_sb = sem("idle_outputs_in_sbuf")
        s_coef = sem("coefficients_ready")
        s_cf_ps = sem("coefficients_transposed")
        s_cf = sem("coefficients_t_in_sbuf")
        s_base = sem("idle_share_product")
        s_base_used = sem("idle_share_added")
        s_xr = [sem(f"tile_rows_landed{i}") for i in range(2)]
        s_xt_ps = sem("tile_rows_transposed")
        s_xt = sem("tile_rows_t_in_sbuf")
        s_dup = sem("tile_up_product")
        s_dadd = sem("tile_up_in_sbuf")
        s_dg = sem("tile_gelu")
        s_dgh = sem("tile_hidden_high")
        s_dgl = sem("tile_hidden_split")
        s_dd = sem("tile_down_product")
        s_ys = sem("tile_output_in_sbuf")
        s_yst = [sem(f"tile_output_stored{i}") for i in range(2)]
        s_yg = [sem(f"routed_rows_gathered{t}") for t in range(T)]
        s_xout = sem("out_tile_ready")
        s_out_ready = sem("out_ready")
        s_out = sem("out_stored")

        block = stack.enter_context(nc.Block())
        UNITS = [(h, c) for h in range(2) for c in [*range(E, CA), *range(E)]]
        ROUTED = [sum(c < E for _, c in UNITS[:n + 1]) for n in range(2 * CA)]
        SPLIT_AFTER = (5, 8, 11, 13, 15, 17)
        DOWN_AFTER = {CA + 3: 0, CA + 5: 1, CA + 7: 2, CA + 9: 3}
        DOWN_BANK = (4, 7, 4, 7, 5, 6, 4, 5)
        BLOCKS = 4 * E
        ORDER = ([("w1", e) for e in range(E - 1)] + [("w2", e) for e in range(E // 2, E)]
                 + [("w1", E - 1), ("w2", 0), ("w2", 1), ("w2", 3), ("w2", 2)])
        EARLY, MIDDLE, LATE = 2 * (E - 1), 2 * (E - 1) + E, 2 * (E - 1) + E + 4

        C_BLOCKS = [range(EARLY - 3, EARLY + 2), range(EARLY + 2, EARLY + 5), range(EARLY + 5, MIDDLE),
                    range(MIDDLE, MIDDLE + 4)]
        SPLIT_FROM = (2, 2, 2, 4)
        D_BLOCKS = range(MIDDLE + 4, BLOCKS)

        def weight_block(i):
            (which, e), half = ORDER[i // 2], i % 2
            if which == "w1":
                return w1d[:, e, half], W1[:, e, 0, half], W1[:, e, 1, half]
            cs = slice(half * HC8 // 2, (half + 1) * HC8 // 2)
            flat = lambda a: a.rearrange("p c d -> p (c d)")
            return flat(w2d[:, e, cs]), W2[:, e, cs, 0], W2[:, e, cs, 1]

        @block.sync
        def _(sp):
            def load_weights(i):
                if i >= 2:
                    sp.wait_ge(s_wlo, i - 1)
                sp.dma_start(STG[:, i % 2], weight_block(i)[0]).then_inc(s_stg[i % 2], 16)

            for h in range(2):
                sp.dma_start(X[:, h * HT:(h + 1) * HT, :],
                             x[h * HT * P:(h + 1) * HT * P, :].rearrange("(t p) d -> p t d", p=P)
                             ).then_inc(s_x[h], 16)
            sp.dma_start(WRAW, w1a.rearrange("p c k h -> p (c k h)")).then_inc(s_wl0, 16)
            sp.dma_start(WRAW2, w2a.rearrange("p c d -> p (c d)")).then_inc(s_wl0, 16)
            sp.dma_start(B9[:, :], b2a).then_inc(s_wl0, 16)
            sp.dma_start(CN, ctx.rearrange("(t p) d -> p t d", p=P)).then_inc(s_ctx, 16)
            for i in range(2):
                load_weights(i)
            sp.wait_ge(s_zero, 1)
            sp.dma_start(sorted_rows.rearrange("(t p) d -> p t d", p=P),
                         HV[:, 0].bitcast(U32).unsqueeze(1).broadcast_to([P, TILES, D])).then_inc(s_fill, 16)
            sp.wait_ge(s_kparts, 1)
            for k in range(KC):
                sp.dma_start(k_parts[:, k * P:(k + 1) * P, :].rearrange("s p n -> p s n"),
                             KS[:, :, k]).then_inc(s_kparts_out, 16)
            sp.wait_ge(s_kparts_out, 16 * KC)

            def load_k_stack(b):
                for r, s in enumerate(K_PART):
                    sp.dma_start(KST[b % 2][r * DH:(r + 1) * DH],
                                 k_parts[s, :, b * S:(b + 1) * S].rearrange("(h d) n -> d h n", d=DH)
                                 ).then_inc(s_kst[b % 2], 16)

            load_k_stack(0)
            for i in range(2, 10):
                load_weights(i)
            sp.wait_ge(s_up, 2 * CA)
            load_k_stack(1)
            for i in range(10, 12):
                load_weights(i)

            def load_minus_max(b):
                sp.wait_ge(s_nms, b + 1)
                for s in range(1, 3):
                    sp.dma_start(QST[b % 2][ROWS + s:ROWS + s + 1], NMS[s * HEADS:(s + 1) * HEADS, :]
                                 ).then_inc(s_nmrow, 16)

            load_minus_max(0)
            for i in range(12, EARLY + 2):
                load_weights(i)
            load_minus_max(1)
            for i in range(EARLY + 2, EARLY + 4):
                load_weights(i)
            for b in range(2, B):
                sp.wait_ge(s_p2, 12 * (b - 1))
                load_k_stack(b)
                for i in range(EARLY + 2 * b, EARLY + 2 * b + 2):
                    load_weights(i)
                load_minus_max(b)
            for i in range(MIDDLE, D_BLOCKS[0]):
                load_weights(i)
            for i in D_BLOCKS:
                load_weights(i)
            sp.wait_ge(s_scat, 16 * 2 * T)

            def load_tile(j, q, first=False):
                if not first:
                    sp.wait_ge(s_xt_ps, j - 1)
                sp.dma_start(XR[:, q].rearrange("p s d -> p (s d)").bitcast(U32),
                             sorted_rows[bass.ds(j * P, P), :]).then_inc(s_xr[q], 16)

            def store_tile(j, q):
                sp.wait_ge(s_ys, j + 1)
                sp.dma_start(routed_rows[bass.ds(j * P, P), :], YS[:, q]).then_inc(s_yst[q], 16)

            for j in range(4):
                load_tile(j, j % 2, first=j < 2)
            store_tile(0, 0)
            with sp.Fori(0, LOOPS) as i:
                for r in range(UNROLL):
                    load_tile(UNROLL * i + HEAD + r + 1, r % 2)
                    store_tile(UNROLL * i + HEAD + r - 2, (r + 1) % 2)
            for j in range(TAIL, TILES):
                if j + 1 < TILES:
                    load_tile(j + 1, (j + 1) % 2)
                store_tile(j - 2, j % 2)
            for j in range(TILES - 2, TILES):
                store_tile(j, j % 2)
            for t in range(T):
                sp.wait_ge(s_xout, t + 1)
                sp.dma_start(out[t * P:(t + 1) * P, :], X[:, t, :]).then_inc(s_out, 16)
            sp.wait_ge(s_out, 16 * T)

        @block.gpsimd
        def _(pool):
            nc.gpsimd.memset(ident[:, :], 0.0).then_inc(s_pool, 1)
            nc.gpsimd.memset(neg_half[:, :], -0.5).then_inc(s_const, 1)
            nc.gpsimd.iota(iota_e[:, :], [[1, E]], base=0, channel_multiplier=0,
                           allow_small_or_imprecise_dtypes=True).then_inc(s_const, 1)
            pool.wait_ge(s_pool, 1)
            nc.gpsimd.affine_select(out=ident[:, :], in_=ident[:, :], compare_op=ALU.not_equal,
                                    fill=1.0, base=0, pattern=[[-1, P]],
                                    channel_multiplier=1).then_inc(s_const, 1)
            pool.wait_ge(s_const, 3)
            nc.gpsimd.tensor_copy(ident_h[:, :], ident[:, :]).then_inc(s_const, 1)
            nc.gpsimd.tensor_copy(ident_b[:, :], ident[:, :]).then_inc(s_const, 1)
            nc.gpsimd.memset(HV[:, 0], 0.0).then_inc(s_zero, 1)
            nc.gpsimd.memset(neg_mask[:, :], 0.0).then_inc(s_pool, 1)
            nc.gpsimd.memset(ones[:, :], 1.0).then_inc(s_pool, 1)
            nc.gpsimd.iota(hidden_n[:, :], [[-P, 2]], base=S - 1, channel_multiplier=-1,
                           allow_small_or_imprecise_dtypes=True).then_inc(s_masks, 1)
            nc.gpsimd.memset(floor[:, :], CAUSAL_FILL).then_inc(s_pool, 1)
            pool.wait_ge(s_pool, 4)
            nc.gpsimd.affine_select(out=neg_mask[:, :], in_=neg_mask[:, :], compare_op=ALU.is_ge, fill=NEVER,
                                    base=0, pattern=[[-1, P]], channel_multiplier=1).then_inc(s_masks, 1)
            nc.gpsimd.affine_select(out=after[:, :], in_=ones[:, :], compare_op=ALU.is_gt, fill=0.0,
                                    base=0, pattern=[[-1, P]], channel_multiplier=1).then_inc(s_masks, 1)
            nc.gpsimd.affine_select(out=floor[:, 1:2], in_=floor[:, 1:2], compare_op=ALU.not_equal, fill=-3e38,
                                    base=1 - P, pattern=[[0, 1]], channel_multiplier=1).then_inc(s_masks, 1)
            pool.wait_ge(s_camax, 1)
            nc.gpsimd.partition_all_reduce(camax_all[:, :, :].rearrange("p a b -> p (a b)"),
                                           camax[:, :, :].rearrange("p a b -> p (a b)"), P,
                                           bass.bass_isa.ReduceOp.max).then_inc(s_camax_all, 1)

            def hidden_share(b):
                pool.wait_ge(s_wm, b + 1)
                pool.wait_ge(s_suf, T // 2)
                if b:
                    pool.wait_ge(s_o_used, 2 * b)
                for i in range(2):
                    nc.gpsimd.tensor_tensor(
                        HV[:, i].rearrange("p (h d) -> p h d", h=HEADS),
                        SUFV[:, 2 * b + i].rearrange("p (h d) -> p h d", h=HEADS),
                        WM[:, b % 2, i].unsqueeze(2).broadcast_to([P, HEADS, DH]), ALU.mult).then_inc(s_hv, 1)

            def estimate_rstd(n, h, size=HT):
                pool.wait_ge(s_ve, n + 1)
                ts = slice(h * size, (h + 1) * size)
                nc.gpsimd.tensor_tensor(rstd0[:, ts], ve[:, ts], neg_half[:, ts],
                                        ALU.pow).then_inc(s_rstd0, 1)

            estimate_rstd(0, 0)
            estimate_rstd(1, 1)
            pool.wait_ge(s_ct, 16)
            pool.wait_ge(s_rw8, 1)
            nc.gpsimd.tensor_tensor(VC.rearrange("p k (t n) -> p (k t) n", t=T),
                                    CT.rearrange("p k (t n) -> p (k t) n", t=T),
                                    rw[:, :, :].rearrange("p k t -> p (k t)").unsqueeze(2).broadcast_to([P, KC * T, P]),
                                    ALU.mult).then_inc(s_vc, 1)
            pool.wait_ge(s_khi, 1)
            nc.gpsimd.tensor_tensor(KR, CT, KS[:, 0], ALU.subtract).then_inc(s_kr, 1)
            pool.wait_ge(s_c2, 1)
            nc.gpsimd.tensor_tensor(VC, VC, C2, ALU.add).then_inc(s_cadd, 1)
            pool.wait_ge(s_cadd, 1)
            nc.gpsimd.tensor_tensor(CQT, VC, C2, ALU.subtract).then_inc(s_cqt, 1)
            pool.wait_ge(s_khi, 2)
            pool.wait_ge(s_kr, 1)
            nc.gpsimd.tensor_tensor(KS[:, 2], KR, KS[:, 1], ALU.subtract).then_inc(s_kparts, 1)
            def weights_low(i):
                _, hi, lo = weight_block(i)
                pool.wait_ge(s_whi, i + 1)
                src = STG[:, i % 2] if len(hi.shape) == 2 else STG[:, i % 2].rearrange("p (c d) -> p c d", d=D)
                nc.gpsimd.tensor_tensor(lo, src, hi, ALU.subtract).then_inc(s_wlo, 1)

            pool.wait_ge(s_act, 4)
            nc.gpsimd.tensor_tensor(W2A[:, 1].rearrange("p c d -> p (c d)"), WRAW2,
                                    W2A[:, 0].rearrange("p c d -> p (c d)"), ALU.subtract).then_inc(s_w2low, 1)
            for i in range(3):
                weights_low(i)
            for h in range(2):
                estimate_rstd(2 + h, h)
            pool.wait_ge(s_w0, 2)
            pool.wait_ge(s_ctx, 16)
            nc.gpsimd.memset(VA[:, :, :, DH:DH + 1], 1.0).then_inc(s_va, 1)
            nc.gpsimd.tensor_copy(VA[:, :, :, 0:DH], CN.rearrange("p t (h d) -> p t h d", h=HEADS)
                                  ).then_inc(s_va, 1)
            pool.wait_ge(s_kparts_out, 16 * KC)
            pool.wait_ge(s_va, 2)
            nc.gpsimd.memset(KST[0][ROWS:ROWS + 3], 1.0).then_inc(s_va, 1)
            pool.wait_ge(s_va, 3)
            for i in range(3, 9):
                weights_low(i)
            for g in range(2):
                estimate_rstd(4 + g, g, 2)
            pool.wait_ge(s_up, 2 * CA)
            pool.wait_ge(s_rstd0, 6)
            nc.gpsimd.memset(KST[1][ROWS:ROWS + 3], 1.0).then_inc(s_va, 1)
            pool.wait_ge(s_va, 4)
            for i in range(9, 11):
                weights_low(i)
            for g in range(2, 4):
                estimate_rstd(4 + g, g, 2)
            for b in range(B):
                if b:
                    hidden_share(b)
                if b == B - 1:
                    estimate_rstd(10, 2, 2)
                for i in C_BLOCKS[b]:
                    if b == B - 2 and i == C_BLOCKS[b][-1]:
                        for g in range(2):
                            estimate_rstd(8 + g, g, 2)
                    weights_low(i)
                if b == 0:
                    hidden_share(b)
            nc.gpsimd.iota(iota_tile[:, :], [[1, TILES]], base=0, channel_multiplier=0,
                           allow_small_or_imprecise_dtypes=True).then_inc(s_dconst, 1)
            nc.gpsimd.iota(iota_full[:, :], [[P, T]], base=0, channel_multiplier=0,
                           allow_small_or_imprecise_dtypes=True).then_inc(s_dconst, 1)
            nc.gpsimd.tensor_copy(ones_b[:, :], ones[:, :]).then_inc(s_dconst, 1)
            nc.gpsimd.affine_select(out=before_b[:, :], in_=ones[:, :], compare_op=ALU.is_gt, fill=0.0,
                                    base=0, pattern=[[1, P]], channel_multiplier=-1).then_inc(s_dconst, 1)
            estimate_rstd(11, 3, 2)
            for i in D_BLOCKS[:-2]:
                weights_low(i)
            pool.wait_ge(s_fill, 16)
            pool.wait_ge(s_slot, 1)
            pool.wait_ge(s_dhl, T)
            pool.wait_ge(s_dhhi, T)
            for t in range(T):
                for k in range(2):
                    pool.indirect_dma_start(sorted_rows[:, :],
                                            bass.IndirectOffsetOnAxis(ap=SLOT[:, k, t:t + 1], axis=0),
                                            DHL[:, t].rearrange("p s d -> p (s d)").bitcast(U32), None
                                            ).then_inc(s_scat, 16)
            for q in range(2):
                pool.wait_ge(s_yst[q], 16 * ((TILES + 1 - q) // 2))
            for t in range(T):
                for k in range(2):
                    pool.indirect_dma_start(YG[:, t, k], None, routed_rows[:, :],
                                            bass.IndirectOffsetOnAxis(ap=SLOT[:, k, t:t + 1], axis=0)
                                            ).then_inc(s_yg[t], 16)

        @block.scalar
        def _(act):
            act.dma_start(CT, ctx_t).then_inc(s_ct, 16)
            act.dma_start(g_raw[:, :], gates2.partition_broadcast(P)).then_inc(s_g, 16)
            act.dma_start(GWR, gate_w).then_inc(s_wl0, 16)
            act.dma_start(B1A[:, :], b1a).then_inc(s_wl0, 16)
            act.wait_ge(s_ct, 16)
            nc.scalar.activation(KS[:, 0], CT, ACT.Copy).then_inc(s_khi, 1)
            act.wait_ge(s_g, 16)
            nc.scalar.activation(tg[:, :], g_raw[:, :], ACT.Tanh).then_inc(s_tg, 1)
            act.wait_ge(s_wl0, 80)
            for raw, dst in ((WRAW, W1A[:, 0].rearrange("p c k h -> p (c k h)")),
                             (GWR.rearrange("p k e -> p (k e)"), GWA[:, 0].rearrange("p k e -> p (k e)")),
                             (WRAW2, WRAW2)):
                nc.scalar.activation(dst, raw, ACT.Copy, scale=W_SCALE).then_inc(s_act, 1)
            act.wait_ge(s_act, 3)
            nc.scalar.activation(W2A[:, 0].rearrange("p c d -> p (c d)"), WRAW2, ACT.Copy).then_inc(s_act, 1)
            def weights_scale(i):
                if i == 6:
                    act.wait_ge(s_kparts, 1)
                if i == 8:
                    act.wait_ge(s_va, 2)
                    act.wait_ge(s_suf_ps, T // 2)
                    act.wait_ge(s_kparts_out, 16 * KC)
                if i == EARLY:
                    act.wait_ge(s_down, T)
                if i == MIDDLE:
                    act.wait_ge(s_p2, 12 * (B - 1))
                if i == LATE:
                    act.wait_ge(s_p2, 12 * B)
                if i == LATE + 2:
                    act.wait_ge(s_dhl, T)
                if i == LATE + 4:
                    act.wait_ge(s_r, 2)
                act.wait_ge(s_stg[i % 2], 16 * (i // 2 + 1))
                nc.scalar.activation(STG[:, i % 2], STG[:, i % 2], ACT.Copy, scale=W_SCALE).then_inc(s_wscaled, 1)

            def weights_high(i):
                _, hi, _ = weight_block(i)
                act.wait_ge(s_wscaled, i + 1)
                src = STG[:, i % 2] if len(hi.shape) == 2 else STG[:, i % 2].rearrange("p (c d) -> p c d", d=D)
                nc.scalar.activation(hi, src, ACT.Copy).then_inc(s_whi, 1)

            def weights_split(i):
                weights_scale(i)
                weights_high(i)

            act.wait_ge(s_kr, 1)
            nc.scalar.activation(KS[:, 1], KR, ACT.Copy).then_inc(s_khi, 1)
            for i in range(2):
                weights_split(i)
            for h in range(2):
                act.wait_ge(s_xqt_ps, h + 1)
                nc.scalar.activation(XQT[:, h].rearrange("p k n -> p (k n)"), bank[h][:, :].bitcast(BF16),
                                     ACT.Copy).then_inc(s_xqt, 1)
            weights_split(2)
            act.wait_ge(s_w2low, 1)
            for j in range(T // 2):
                act.wait_ge(s_suf_ps, j + 1)
                nc.scalar.activation(SUFV[:, 2 * j:2 * j + 2].rearrange("p t d -> p (t d)"), bank[4 + j][:, :],
                                     ACT.Copy).then_inc(s_suf, 1)
            def row_high_b(t):
                act.wait_ge(s_hs, t + 1)
                nc.scalar.activation(HHL[:, t, 0], HS[:, t], ACT.Copy).then_inc(s_hhi, 1)

            for t in range(2):
                row_high_b(t)
            for j in range(T // 2):
                for t in range(2 * j + 2, min(2 * j + 4, T)):
                    row_high_b(t)
                act.wait_ge(s_ht_ps, j + 1)
                nc.scalar.activation(
                    HT_[:, :, :, j * 2 * P:(j + 1) * 2 * P].rearrange("p k s (t n) -> p t (k s) n", t=2),
                    bank[j][:, :].bitcast(F16).rearrange("p (t a n) -> p t a n", t=2, n=P),
                    ACT.Copy).then_inc(s_ht, 1)
            act.wait_ge(s_z12, 1)
            nc.scalar.activation(th[:, :], z12[:, :], ACT.Tanh,
                                 scale=0.5 / (X_SCALE * W_SCALE)).then_inc(s_th, 1)
            def hidden_high(n):
                h, c = UNITS[n]
                hi = GHL[:, 0, c, h * 512:(h + 1) * 512]
                if c < E:
                    act.wait_ge(s_gg, ROUTED[n])
                    nc.scalar.activation(hi, GG[:, n % 2], ACT.Copy).then_inc(s_ghi, 1)
                else:
                    act.wait_ge(s_gelu, n + 1)
                    nc.scalar.activation(hi, G32[:, n % 2], ACT.Copy, scale=G_SCALE).then_inc(s_ghi, 1)

            for n, (h, c) in enumerate(UNITS):
                act.wait_ge(s_up, n + 1)
                if n >= 2:
                    if UNITS[n - 2][1] < E:
                        act.wait_ge(s_gg, ROUTED[n - 2])
                    else:
                        act.wait_ge(s_ghl, n - 1)
                nc.scalar.activation(G32[:, n % 2], bank[n % 4][:, :], ACT.Gelu, bias=B1A[:, c:c + 1],
                                     scale=1.0 / (X_SCALE * W_SCALE)).then_inc(s_gelu, 1)
                if n:
                    hidden_high(n - 1)
                if n == 4:
                    act.wait_ge(s_gt_ps, 1)
                    nc.scalar.activation(gates_t[:, 0:512], bank[7][0:E + 1, :], ACT.Copy).then_inc(s_gt, 1)
                    nc.scalar.activation(gates_t[:, 512:1024], bank[4][0:E + 1, :], ACT.Copy).then_inc(s_gt, 1)
                if n in SPLIT_AFTER:
                    weights_split(3 + SPLIT_AFTER.index(n))
            hidden_high(2 * CA - 1)
            def repeat_parts(b):
                for i in range(2):
                    act.wait_ge(s_q1, 2 * b + i + 1)
                    nc.scalar.activation(QTOK[:, i, :, 1:3], QTOK[:, i, :, 0:1].broadcast_to([P, HEADS, 2, DH]),
                                         ACT.Copy).then_inc(s_qtok, 1)
                    nc.scalar.activation(QTOK[:, i, :, 4:5], QTOK[:, i, :, 3:4], ACT.Copy).then_inc(s_qtok, 1)

            def store_q(b, j):
                if b >= 2 and j == 0:
                    act.wait_ge(s_p2, 12 * (b - 1))
                act.wait_ge(s_qt_ps, 4 * b + j + 1)
                i, h0 = j // 2, 8 * (j % 2)
                nc.scalar.activation(QST[b % 2][0:ROWS, h0:h0 + 8, i * P:(i + 1) * P],
                                     T_BANK[j][:, :].bitcast(BF16)[0:ROWS].rearrange("p (h n) -> p h n", h=8),
                                     ACT.Copy).then_inc(s_qst, 1)

            def store_minus_max(b):
                act.wait_ge(s_nm_ps, b + 1)
                if b:
                    act.wait_ge(s_nmrow, 48 * b)
                nc.scalar.activation(NMS[:, :], qt_bank[:, :].bitcast(BF16)[0:3 * HEADS, 0:S],
                                     ACT.Copy).then_inc(s_nms, 1)
                act.wait_ge(s_nms, b + 1)
                act.dma_start(QST[b % 2][ROWS:ROWS + 1], NMS[0:HEADS, :]).then_inc(s_nmrow, 16)

            def hidden_weight(b):
                act.wait_ge(s_wz, b + 1)
                if b >= 2:
                    act.wait_ge(s_o_used, 2 * (b - 1))
                nc.scalar.activation(WM[:, b % 2].rearrange("p i h -> p (i h)"),
                                     WZ[:, b % 2].rearrange("p i h -> p (i h)"), ACT.Exp,
                                     scale=0.25).then_inc(s_wm, 1)

            def exponentials(b, u):
                n = 12 * b + u
                act.wait_ge(s_p2, n + 1)
                if n >= 6:
                    act.wait_ge(s_pv, (n - 6) // 3 + 1)
                nc.scalar.activation(PT[:, n % 6], s2_bank[n % 2][:, :], ACT.Exp, scale=0.25).then_inc(s_pt, 1)

            def store_o(b, j):
                act.wait_ge(s_pv, 4 * b + 2 * j + 2)
                if b:
                    act.wait_ge(s_o_ps, 2 * b)
                nc.scalar.activation(OT[:, j], o_bank[j][:, :], ACT.Copy).then_inc(s_ot, 1)

            def row_high(t):
                act.wait_ge(s_dhs, t + 1)
                nc.scalar.activation(DHL[:, t, 0], DHS[:, t], ACT.Copy).then_inc(s_dhhi, 1)

            def rows_t_out(j):
                act.wait_ge(s_dt_ps, j + 1)
                nc.scalar.activation(
                    DHT[:, :, :, j * 2 * P:(j + 1) * 2 * P].rearrange("p k s (t n) -> p t (k s) n", t=2),
                    bank[j % 2][:, :].bitcast(F16).rearrange("p (t a n) -> p t a n", t=2, n=P),
                    ACT.Copy).then_inc(s_dht, 1)

            repeat_parts(0)
            for j in range(4):
                store_q(0, j)
            for i in range(9, 11):
                weights_split(i)
            store_minus_max(0)
            hidden_weight(0)
            repeat_parts(1)
            act.dma_start(B1D[:, :, :], b1d).then_inc(s_dw_small, 16)
            act.dma_start(RW2R[:, :], rw2).then_inc(s_dw_small, 16)
            for b in range(B):
                steps = [(f, i) for i in C_BLOCKS[b] for f in (weights_scale, weights_high)]
                for u in range(12):
                    if b + 1 < B and 1 <= u < 5:
                        store_q(b + 1, u - 1)
                    exponentials(b, u)
                    if b == B - 1 and u < HT:
                        row_high(u)
                    if b == B - 1 and u in (7, 10):
                        rows_t_out(u // 10)
                    if u == 8:
                        store_o(b, 0)
                    if u == 10 and b + 1 < B:
                        store_minus_max(b + 1)
                        hidden_weight(b + 1)
                    if steps and u >= SPLIT_FROM[b]:
                        f, i = steps.pop(0)
                        f(i)
                store_o(b, 1)
                if b + 2 < B:
                    repeat_parts(b + 2)
            act.dma_start(RW1R, rw1).then_inc(s_dw_small, 16)
            act.wait_ge(s_hv, T)
            act.dma_start(B24[2 * E:3 * E, :], b2d).then_inc(s_dw_small, 16)
            for t in range(HT, T):
                if t == HT + 2:
                    for i in D_BLOCKS[:2]:
                        weights_split(i)
                row_high(t)
                if t == HT:
                    for src, dst in ((RW1R.rearrange("p k h -> p (k h)"), RW1[:, 0].rearrange("p k h -> p (k h)")),
                                     (RW2R[:, :], RW2[:, 0])):
                        act.wait_ge(s_dw_small, 64)
                        nc.scalar.activation(dst, src, ACT.Copy, scale=W_SCALE).then_inc(s_rwh, 1)
            for j in range(2, 4):
                rows_t_out(j)
            for h in range(2):
                act.wait_ge(s_r, h + 1)
                nc.scalar.activation(R32[:, h * 512:(h + 1) * 512], bank[4 + h][:, :], ACT.Gelu,
                                     scale=1.0 / (X_SCALE * W_SCALE)).then_inc(s_rg, 1)
            nc.scalar.activation(GB[:, :, :], B1D[:, :, :], ACT.Gelu).then_inc(s_gb, 1)
            weights_split(D_BLOCKS[2])
            act.wait_ge(s_dl, 1)
            nc.scalar.activation(PR[:, :, :], LG[:, :, :], ACT.Exp,
                                 scale=1.0 / (G_SCALE * W_SCALE)).then_inc(s_ex, 1)
            for i in D_BLOCKS[3:]:
                weights_split(i)

            def tile_gelu(j, q, first=False):
                e = act.value_load(EID[0:1, bass.ds(j, 1)], min_val=0, max_val=E - 1)
                for hb in range(2):
                    for c in range(4 * hb, 4 * hb + 4):
                        if c % 2 == 0:
                            act.wait_ge(s_dadd, UP_BANKS * j + c // 2 + 1)
                        x = GD[:, q, c * P:(c + 1) * P]
                        ins = nc.scalar.activation(x, x, ACT.Gelu, bias=B1D[:, e, c:c + 1],
                                                   scale=1.0 / (X_SCALE * W_SCALE))
                    ins.then_inc(s_dg, 1)
                for hb in range(2):
                    act.wait_ge(s_dg, 2 * j + hb + 1)
                    if not first:
                        act.wait_ge(s_dd, j - 1)
                    nc.scalar.activation(GDL[:, q, 0, hb * 512:(hb + 1) * 512], GD[:, q, hb * 512:(hb + 1) * 512],
                                         ACT.Copy, scale=G_SCALE).then_inc(s_dgh, 1)

            act.wait_ge(s_eid, 1)
            for j in range(HEAD):
                tile_gelu(j, j % 2, first=j < 2)
            with act.Fori(0, LOOPS) as i:
                for r in range(UNROLL):
                    tile_gelu(UNROLL * i + HEAD + r, (HEAD + r) % 2)
            for j in range(TAIL, TILES):
                tile_gelu(j, j % 2)

        @block.tensor
        def _(pe):
            pe.wait_ge(s_const, 5)
            for h in range(2):
                pe.wait_ge(s_xq, h + 1)
                v = bank[h][:, :].bitcast(BF16).rearrange("p (k t n) -> p k t n", k=KC, t=HT)
                for t in range(HT):
                    for k in range(KC):
                        mm = nc.tensor.transpose(v[:, k, t], XQ[:, h * HT + t, k * P:(k + 1) * P], ident_b[:, :])
                mm.then_inc(s_xqt_ps, 1)
            for t in range(T):
                if t % HT == 0:
                    pe.wait_ge(s_xqt, t // HT + 1)
                if t == 0:
                    pe.wait_ge(s_cqt, 1)
                if t >= 4:
                    pe.wait_ge(s_da_used, t - 3)
                b = t // 2
                for k in range(KC):
                    mm = nc.tensor.matmul(bank[4 + t % 4][:, k * D:(k + 1) * D],
                                          XQT[:, t // HT, k, (t % HT) * P:(t % HT + 1) * P],
                                          CQT[:, k, b * S:(b + 1) * S], start=True, stop=True)
                mm.then_inc(s_da, 1)
            pe.wait_ge(s_da_used, T)
            pe.wait_ge(s_ctx, 16)
            pe.wait_ge(s_masks, 4)
            for t in range(T):
                o = bank[4 + t // 2][:, (t % 2) * D:(t % 2 + 1) * D]
                mm = nc.tensor.matmul(o, after[:, :], CN[:, t], start=True, stop=bool(t % 2))
                if t % 2 == 0:
                    nc.tensor.matmul(o, ones[:, :], CN[:, t + 1], start=False, stop=True)
                else:
                    mm.then_inc(s_suf_ps, 1)
            for t in range(T):
                pe.wait_ge(s_hhl, t + 1)
                pe.wait_ge(s_hhi, t + 1)
                v = bank[t // 2][:, :].bitcast(F16).rearrange("p (t k s n) -> p t k s n", t=2, k=KC, s=2)
                for k in range(KC):
                    for s in range(2):
                        mm = nc.tensor.transpose(v[:, t % 2, k, s], HHL[:, t, s, k * P:(k + 1) * P],
                                                 ident_h[:, :])
                if t % 2:
                    mm.then_inc(s_ht_ps, 1)
            pe.wait_ge(s_w0, 2)
            pe.wait_ge(s_act, 3)
            pe.wait_ge(s_suf, T // 2)
            passes = ((0, 0), (0, 1), (1, 0))
            for t in range(T):
                if t % 2 == 0:
                    pe.wait_ge(s_ht, t // 2 + 1)
                n = 0
                for a, b in passes:
                    for k in range(KC):
                        mm = nc.tensor.matmul(bank[4][:, t * E:(t + 1) * E], HT_[:, k, a, t * P:(t + 1) * P],
                                              GWA[:, b, k], start=(n == 0), stop=(n == 5))
                        n += 1
            mm.then_inc(s_lg, 1)
            def gate_rows(n):
                h, c = UNITS[n]
                if ROUTED[n] > 2:
                    pe.wait_ge(s_gg, ROUTED[n] - 2)
                nc.tensor.matmul(bank[5 + ROUTED[n] % 2][:, :], select[:, c:c + 1].broadcast_to([3 * (E + 1), P]),
                                 gates3_t[:, h * 512:(h + 1) * 512], start=True, stop=True).then_inc(s_bc, 1)

            def down(t):
                pe.wait_ge(s_ghl, CA * (t // HT + 1))
                if t == 0:
                    pe.wait_ge(s_act, 4)
                    pe.wait_ge(s_w2low, 1)
                if t in (4, 5):
                    pe.wait_ge(s_gg, 2 * E)
                elif t > 1:
                    pe.wait_ge(s_down_used, {2: 1, 3: 2, 6: 3, 7: 5}[t])
                dst = bank[DOWN_BANK[t]][:, 0:D]
                n = 0
                for c in range(CA):
                    for a, b in passes:
                        nc.tensor.matmul(dst, GHL[:, a, c, t * P:(t + 1) * P], W2A[:, b, c],
                                         start=(n == 0), stop=False)
                        n += 1
                nc.tensor.matmul(dst, gates_t[:, t * P:(t + 1) * P], B9[:, :],
                                 start=False, stop=True).then_inc(s_down, 1)

            for i, (h, c) in enumerate(UNITS):
                if i >= 4:
                    pe.wait_ge(s_gelu, i - 3)
                n = 0
                for a, b in passes:
                    for k in range(KC):
                        mm = nc.tensor.matmul(bank[i % 4][:, :], W1A[:, b, c, k],
                                              HT_[:, k, a, h * 512:(h + 1) * 512],
                                              start=(n == 0), stop=(n == 5))
                        n += 1
                mm.then_inc(s_up, 1)
                if i == 3:
                    pe.wait_ge(s_gates, 2)
                    for t in range(T):
                        v = bank[5][:, :].bitcast(BF16)
                        nc.tensor.transpose(v[0:3 * (E + 1), t * P:(t + 1) * P],
                                            gates3[:, t].rearrange("p s e -> p (s e)"), ident_b[:, :])
                        mm = nc.tensor.transpose(bank[7 if t < HT else 4][0:E + 1, (t % HT) * P:(t % HT + 1) * P],
                                                 gates[:, t], ident[:, :])
                    mm.then_inc(s_gt_ps, 1)
                    pe.wait_ge(s_gt3, 1)
                    pe.wait_ge(s_sel, 1)
                    gate_rows(2)
                if i >= 3 and c < E:
                    gate_rows(i)
                if i in DOWN_AFTER:
                    if i == CA + 3:
                        pe.wait_ge(s_gt, 2)
                    down(DOWN_AFTER[i])
            down(4)

            def transpose_q(b, j):
                i, h0 = j // 2, 8 * (j % 2)
                if j % 2 == 0:
                    pe.wait_ge(s_qtok, 4 * b + 2 * i + 2)
                if b and j == 0:
                    pe.wait_ge(s_nms, b)
                elif b and j < 3:
                    pe.wait_ge(s_mx, 12 * b)
                elif j == 3:
                    pe.wait_ge(s_qst, 4 * b + 1)
                v = T_BANK[j][:, :].bitcast(BF16).rearrange("p (h n) -> p h n", h=8)
                for h in range(8):
                    mm = nc.tensor.transpose(v[0:ROWS, h], QTOK[:, i, h0 + h].rearrange("p r d -> p (r d)"),
                                             ident_b[:, :])
                mm.then_inc(s_qt_ps, 1)

            def scores_for_max(b, u):
                n = 12 * b + u
                if u == 0:
                    pe.wait_ge(s_kst[b % 2], 96 * (b // 2 + 1))
                    pe.wait_ge(s_va, min(3 + b, 4))
                    pe.wait_ge(s_qst, 4 * b + 2)
                if u == 1:
                    pe.wait_ge(s_qst, 4 * b + 3)
                if u == 4:
                    pe.wait_ge(s_qst, 4 * b + 4)
                if n >= 2:
                    pe.wait_ge(s_mx, n - 1)
                i = 0 if u < 4 else 1
                nh, nk = (4, P) if i == 0 else (2, S)
                h0 = 4 * u if i == 0 else 2 * (u - 4)
                v = s1_bank[n % 2][:, :].rearrange("p (h n) -> p h n", h=nh)
                nc.tensor.matmul(v[:, :, nk - P:nk], ident_b[:, :],
                                 neg_mask[:, :].unsqueeze(1).broadcast_to([P, nh, P]),
                                 start=True, stop=False, skip_group_check=True)
                for h in range(nh):
                    mm = nc.tensor.matmul(v[:, h], QST[b % 2][0:ROWS, h0 + h, i * P:(i + 1) * P],
                                          KST[b % 2][0:ROWS, h0 + h, 0:nk], start=False, stop=h == nh - 1,
                                          skip_group_check=True)
                mm.then_inc(s_p1, 1)

            def transpose_minus_max(b):
                pe.wait_ge(s_nmp, b + 1)
                pe.wait_ge(s_qst, 4 * b + 4)
                v = qt_bank[:, :].bitcast(BF16)
                for i in range(2):
                    mm = nc.tensor.transpose(v[0:3 * HEADS, i * P:(i + 1) * P],
                                             NMP[:, i].rearrange("p s h -> p (s h)"), ident_b[:, :])
                mm.then_inc(s_nm_ps, 1)

            def scores_by_key(b, u):
                n = 12 * b + u
                g, w = u // 3, u % 3
                if u == 0:
                    pe.wait_ge(s_nmrow, 48 * (b + 1))
                if n >= 2:
                    pe.wait_ge(s_pt, n - 1)
                k, nh, nq = (0, 2, S) if w < 2 else (1, 4, P)
                h0 = 4 * g + (2 * w if w < 2 else 0)
                v = s2_bank[n % 2][:, :].rearrange("p (h n) -> p h n", h=nh)
                nc.tensor.matmul(v[:, :, 0:P], neg_mask[:, :], ident_b[:, :].unsqueeze(1).broadcast_to([P, nh, P]),
                                 start=True, stop=False, skip_group_check=True)
                for h in range(nh):
                    mm = nc.tensor.matmul(v[:, h], KST[b % 2][0:ROWS + 3, h0 + h, k * P:(k + 1) * P],
                                          QST[b % 2][0:ROWS + 3, h0 + h, k * P:S], start=False, stop=h == nh - 1,
                                          skip_group_check=True)
                mm.then_inc(s_p2, 1)

            def weighted_values(b, g):
                n = 12 * b + 3 * g
                pe.wait_ge(s_pt, n + 3)
                if g % 2 == 0 and b:
                    pe.wait_ge(s_ot, 2 * (b - 1) + g // 2 + 1)
                c0 = (g % 2) * S
                ob = o_bank[g // 2]
                for j in range(4):
                    p = PT[:, (n + j // 2) % 6].rearrange("p (h n) -> p h n", h=2)[:, j % 2]
                    nc.tensor.matmul(ob[32 * j:32 * j + DH + 1, c0:c0 + S], VA[:, 2 * b, 4 * g + j], p,
                                     start=True, stop=False, skip_group_check=True)
                for j in range(4):
                    p = PT[:, (n + 2) % 6].rearrange("p (h n) -> p h n", h=4)[:, j]
                    mm = nc.tensor.matmul(ob[32 * j:32 * j + DH + 1, c0 + P:c0 + S], VA[:, 2 * b + 1, 4 * g + j],
                                          p, start=False, stop=True, skip_group_check=True)
                mm.then_inc(s_pv, 1)

            def transpose_o(b, i):
                pe.wait_ge(s_ot, 2 * b + 2)
                if b or i:
                    pe.wait_ge(s_o_used, 2 * b + i)
                for g in range(4):
                    c0 = (g % 2) * S + i * P
                    mm = nc.tensor.transpose(ot_bank[:, g * P:(g + 1) * P], OT[:, g // 2, c0:c0 + P], ident[:, :])
                mm.then_inc(s_o_ps, 1)

            def transpose_rows(j):
                if j >= 2:
                    pe.wait_ge(s_dht, j - 1)
                v = bank[j % 2][:, :].bitcast(F16).rearrange("p (t k s n) -> p t k s n", t=2, k=KC, s=2)
                for i in range(2):
                    pe.wait_ge(s_dhl, 2 * j + i + 1)
                    for k in range(KC):
                        for s in range(2):
                            mm = nc.tensor.transpose(v[:, i, k, s], DHL[:, 2 * j + i, s, k * P:(k + 1) * P],
                                                     ident_h[:, :])
                mm.then_inc(s_dt_ps, 1)

            down(5)
            pe.wait_ge(s_gelu, 2 * CA)
            pe.wait_ge(s_down_used, 4)
            for j in range(4):
                transpose_q(0, j)
            for u in range(12):
                scores_for_max(0, u)
            down(6)
            transpose_minus_max(0)
            down(7)
            pe.wait_ge(s_down_used, T)
            pe.wait_ge(s_obank, 2)
            for b in range(B):
                for u in range(12):
                    if b + 1 < B and u in (1, 2):
                        for j in ((0, 1, 2), (3,))[u - 1]:
                            transpose_q(b + 1, j)
                    if b and u in (0, 2):
                        transpose_o(b - 1, u // 2)
                    if b + 1 < B and 3 <= u < 9:
                        for m in (2 * u - 6, 2 * u - 5):
                            scores_for_max(b + 1, m)
                    if b + 1 < B and u == 10:
                        transpose_minus_max(b + 1)
                    if b == B - 1 and u in (6, 9):
                        transpose_rows(u // 9)
                    scores_by_key(b, u)
                    if u % 3 == 2 and u >= 5:
                        weighted_values(b, u // 3 - 1)
                weighted_values(b, 3)
            for i in range(2):
                transpose_o(B - 1, i)
            for j in range(2, 4):
                transpose_rows(j)
            pe.wait_ge(s_rw, 2)
            for h in range(2):
                pe.wait_ge(s_dht, 2 * h + 2)
                n = 0
                for a, b in passes:
                    for k in range(KC):
                        mm = nc.tensor.matmul(bank[4 + h][:, :], RW1[:, b, k], DHT[:, k, a, h * 512:(h + 1) * 512],
                                              start=(n == 0), stop=(n == 5))
                        n += 1
                mm.then_inc(s_r, 1)
            for t in range(T):
                pe.wait_ge(s_rhl, t // HT + 1)
                for n, (a, b) in enumerate(passes):
                    mm = nc.tensor.matmul(bank[6][:, t * E:(t + 1) * E], RHL[:, a, t * P:(t + 1) * P], RW2[:, b],
                                          start=(n == 0), stop=(n == 2))
            mm.then_inc(s_dlg, 1)
            pe.wait_ge(s_m, 1)
            pe.wait_ge(s_dconst, 4)
            rank = bank[4][:, 0:T * E]
            nc.tensor.matmul(rank, before_b[:, :], MSB[:, :, :].rearrange("p t e -> p (t e)"),
                             start=True, stop=False, skip_group_check=True)
            for t in range(T - 1):
                nc.tensor.matmul(rank[:, (t + 1) * E:].rearrange("p (t e) -> p t e", e=E), ones_b[:, :],
                                 MSB[:, t:t + 1].broadcast_to([P, T - 1 - t, E]), start=False,
                                 stop=t == T - 2, skip_group_check=True)
            for t in range(T):
                mm = nc.tensor.matmul(bank[5][:, 0:2 * E], ones_b[:, :],
                                      M01B[:, t].rearrange("p k e -> p (k e)"), start=t == 0, stop=t == T - 1)
            mm.then_inc(s_rank, 1)
            pe.wait_ge(s_gb16, 2)
            experts = list(range(E // 2, E)) + list(range(E // 2))
            for n, e in enumerate(experts):
                if n == E // 2:
                    pe.wait_ge(s_wlo, BLOCKS - 2)
                    pe.wait_ge(s_wlate, 2)
                for c in range(HC8):
                    for s in range(2):
                        mm = nc.tensor.matmul(bank[7][0:2 * E, 0:D], GB16[:, c, e], W2[:, e, c, s],
                                              start=(n == 0 and c == 0 and s == 0),
                                              stop=(n == E - 1 and c == HC8 - 1 and s == 1))
            mm.then_inc(s_ce, 1)
            def transpose_tile(j, q, m, first=False):
                pe.wait_ge(s_xr[q], 16 * m + 16)
                if not first:
                    pe.wait_ge(s_xt, j - 1)
                v = bank[q][:, :].bitcast(F16)[:, 0:4 * P].rearrange("p (k s n) -> p k s n", k=KC, s=2)
                for k in range(KC):
                    for s in range(2):
                        mm = nc.tensor.transpose(v[:, k, s], XR[:, q, s, k * P:(k + 1) * P], ident_h[:, :])
                mm.then_inc(s_xt_ps, 1)

            def expert_of(j):
                return pe.value_load(EID[0:1, bass.ds(j, 1)], min_val=0, max_val=E - 1)

            def tile_up(j, q, e, first=False):
                pe.wait_ge(s_xt, j + 1)
                for hb in range(UP_BANKS):
                    if not first:
                        pe.wait_ge(s_dadd, UP_BANKS * j + hb - UP_BANKS + 1)
                    for c in (2 * hb, 2 * hb + 1):
                        o = up_bank[hb][:, (c % 2) * 2 * P:(c % 2 + 1) * 2 * P]
                        for k in range(KC):
                            nc.tensor.matmul(o, W1[:, e, 0, k, c * P:(c + 1) * P],
                                             XT[:, q, k].rearrange("p s n -> p (s n)"),
                                             start=(k == 0), stop=False, skip_group_check=True)
                            mm = nc.tensor.matmul(o[:, 0:P], W1[:, e, 1, k, c * P:(c + 1) * P], XT[:, q, k, 0],
                                                  start=False, stop=(k == KC - 1), skip_group_check=True)
                    mm.then_inc(s_dup, 1)

            def tile_down(j, q, e, first=False):
                if first and q:
                    pe.wait_ge(s_ce_sb, 1)
                if not first:
                    pe.wait_ge(s_ys, j - 1)
                for hb in range(2):
                    pe.wait_ge(s_dgl, 2 * j + hb + 1)
                    for c in range(4 * hb, 4 * hb + 4):
                        nc.tensor.matmul(bank[6 + q][:, :], GDL[:, q, 0, c * P:(c + 1) * P],
                                         W2[:, e, c].rearrange("p s d -> p (s d)"), start=(c == 0), stop=False,
                                         skip_group_check=True)
                        mm = nc.tensor.matmul(bank[6 + q][:, 0:D], GDL[:, q, 1, c * P:(c + 1) * P],
                                              W2[:, e, c, 0], start=False, stop=(c == HC8 - 1),
                                              skip_group_check=True)
                mm.then_inc(s_dd, 1)

            pe.wait_ge(s_eid, 1)
            transpose_tile(0, 0, 0, first=True)
            for j in range(HEAD):
                e = expert_of(j)
                tile_up(j, j % 2, e, first=j == 0)
                transpose_tile(j + 1, (j + 1) % 2, (j + 1) // 2, first=j == 0)
                if j:
                    tile_down(j - 1, (j - 1) % 2, e_before, first=True)
                e_before = e
            with pe.Fori(0, LOOPS) as i:
                e_before = expert_of(UNROLL * i + HEAD - 1)
                for r in range(UNROLL):
                    j, q = UNROLL * i + HEAD + r, (HEAD + r) % 2
                    e = expert_of(j)
                    tile_up(j, q, e)
                    transpose_tile(j + 1, 1 - q, UNROLL // 2 * i + (HEAD + r + 1) // 2)
                    tile_down(j - 1, 1 - q, e_before)
                    e_before = e
            e_before = expert_of(TAIL - 1)
            for j in range(TAIL, TILES):
                e = expert_of(j)
                tile_up(j, j % 2, e)
                if j + 1 < TILES:
                    transpose_tile(j + 1, (j + 1) % 2, (j + 1) // 2)
                tile_down(j - 1, (j - 1) % 2, e_before)
                e_before = e
            tile_down(TILES - 1, (TILES - 1) % 2, e_before)
            pe.wait_ge(s_coef, 1)
            for t in range(T):
                mm = nc.tensor.transpose(bank[2 + t // 4][0:3 * E, (t % 4) * P:(t % 4 + 1) * P], COEF[:, t],
                                         ident[:, :])
            mm.then_inc(s_cf_ps, 1)
            pe.wait_ge(s_cf, 2)
            for t in range(T):
                if t >= 2:
                    pe.wait_ge(s_base_used, t - 1)
                nc.tensor.matmul(bank[4 + t % 2][:, 0:D], COEF_T[0:3 * E, t * P:(t + 1) * P], B24[0:3 * E, :],
                                 start=True, stop=True).then_inc(s_base, 1)

        @block.vector
        def _(dve):
            done = Count(s_dve)

            def step(instruction):
                dve.wait_ge(s_dve, done.on(instruction))

            def mark(instruction):
                return done.on(instruction)

            def here():
                dve.wait_ge(s_dve, done.n)

            v = nc.vector

            def ln_variance(h, n, size=HT):
                ts = slice(h * size, (h + 1) * size)
                for t in range(h * size, (h + 1) * size):
                    mark(v.bn_stats(stats[:, t], X[:, t]))
                here()
                for t in range(h * size, (h + 1) * size):
                    mark(v.bn_aggr(mv[:, t], stats[:, t]))
                here()
                v.tensor_scalar(ve[:, ts], mv[:, ts, 1], EPS, None, ALU.add).then_inc(s_ve, 1)

            def ln_rstd(h, n, scale, size=HT):
                ts = slice(h * size, (h + 1) * size)
                dve.wait_ge(s_rstd0, n + 1)
                dve.wait_ge(s_ve, n + 1)
                step(v.tensor_tensor(rt[:, ts], ve[:, ts], rstd0[:, ts], ALU.mult))
                step(v.tensor_tensor(rt[:, ts], rt[:, ts], rstd0[:, ts], ALU.mult))
                step(v.tensor_scalar(rt[:, ts], rt[:, ts], -0.5 * scale, 1.5 * scale, ALU.mult, ALU.add))
                step(v.tensor_tensor(rstd[:, ts], rt[:, ts], rstd0[:, ts], ALU.mult))

            def round_step(val, tmp):
                step(v.tensor_scalar(tmp.bitcast(U32), val.bitcast(U32), 0x7F800000, None, ALU.bitwise_and))
                return v.tensor_scalar(tmp, tmp, FP8_MIN_NORMAL, ROUND_FP8, ALU.max, ALU.mult)

            def round_fp8(dst, val, tmp):
                step(round_step(val, tmp))
                step(v.tensor_tensor(val, val, tmp, ALU.add))
                return v.tensor_tensor(dst, val, tmp, ALU.subtract)

            dve.wait_ge(s_const, 3)
            with nc.allow_low_precision("ones and zeros"):
                v.tensor_reduce(select[:, :], ident[0:3 * (E + 1), 0:3 * (E + 1)].rearrange("p (s e) -> p e s", s=3),
                                AX.X, ALU.add).then_inc(s_sel, 1)
            dve.wait_ge(s_ct, 16)
            v.tensor_reduce(camax[:, :, :], CT.rearrange("p k (t n) -> p k t n", t=T), AX.X, ALU.max,
                            apply_absolute_value=True).then_inc(s_camax, 1)
            for h in range(2):
                dve.wait_ge(s_x[h], 16)
                ln_variance(h, h)
            dve.wait_ge(s_camax_all, 1)
            step(v.tensor_scalar(sw[:, :, :], camax_all[:, :, :], 1e-6, None, ALU.max))
            step(v.reciprocal(rw[:, :, :], sw[:, :, :]))
            v.tensor_scalar(rw[:, :, :], rw[:, :, :], FP8_MAX, None, ALU.mult).then_inc(s_rw8, 1)
            dve.wait_ge(s_tg, 1)
            step(v.tensor_scalar(sw[:, :, :], sw[:, :, :], tg[:, 0:1], 1.0 / FP8_MAX, ALU.mult, ALU.mult))
            for h in range(2):
                if h == 1:
                    dve.wait_ge(s_vc, 1)
                    round_step(VC, C2).then_inc(s_c2, 1)
                ts = slice(h * HT, (h + 1) * HT)
                ln_rstd(h, h, 1.0)
                for t in range(h * HT, (h + 1) * HT):
                    mark(v.tensor_scalar(XC[:, t], X[:, t], mv[:, t, 0:1], rstd[:, t:t + 1],
                                         ALU.subtract, ALU.mult))
                here()
                xk = XC[:, ts].rearrange("p t (k n) -> p (t k) n", k=KC)
                vk = V[:, ts].rearrange("p t (k n) -> p (t k) n", k=KC)
                flat = lambda a: a[:, ts].rearrange("p t k -> p (t k)")
                step(v.tensor_reduce(flat(xamax), xk, AX.X, ALU.max, apply_absolute_value=True))
                step(v.tensor_scalar(flat(sx), flat(xamax), 1e-4, None, ALU.max))
                step(v.reciprocal(flat(rx), flat(sx)))
                step(v.tensor_scalar(flat(rx), flat(rx), FP8_MAX, None, ALU.mult))
                step(v.tensor_scalar(flat(sx), flat(sx), 1.0 / FP8_MAX, None, ALU.mult))
                step(v.tensor_tensor(vk, xk, flat(rx).unsqueeze(2).broadcast_to([P, HT * KC, P]), ALU.mult))
                round_fp8(XQ[:, ts], V[:, ts], C1[:, ts]).then_inc(s_xq, 1)
            for nb in range(2):
                for k in range(KC):
                    mark(v.tensor_tensor(
                        sxw[:, :, nb, k].rearrange("p (b i) -> p b i", i=2),
                        sx[:, :, k].rearrange("p (b i) -> p b i", i=2),
                        sw[:, k, :].rearrange("p (b n) -> p b n", n=2)[:, :, nb:nb + 1].broadcast_to([P, B, 2]),
                        ALU.mult))
            here()
            for t in range(T):
                dve.wait_ge(s_da, t + 1)
                for k in range(KC):
                    for nb in range(2):
                        ins = v.scalar_tensor_tensor(
                            out=X[:, t, nb * P:(nb + 1) * P], in0=bank[4 + t % 4][:, k * D + nb * P:k * D + (nb + 1) * P],
                            scalar=sxw[:, t, nb, k:k + 1], in1=X[:, t, nb * P:(nb + 1) * P],
                            op0=ALU.mult, op1=ALU.add)
                        if (k, nb) == (KC - 1, 1):
                            ins.then_inc(s_da_used, 1)
                        else:
                            mark(ins)
                            if nb:
                                here()
            dve.wait_ge(s_da_used, T)
            for h in range(2):
                ln_variance(h, 2 + h)
            dve.wait_ge(s_act, 3)
            dve.wait_ge(s_wl0, 80)
            for raw, w in ((GWR.rearrange("p k e -> p (k e)"), GWA.rearrange("p s k e -> p s (k e)")),
                           (WRAW, W1A.rearrange("p s c k h -> p s (c k h)"))):
                v.scalar_tensor_tensor(out=w[:, 1], in0=raw, scalar=W_SCALE, in1=w[:, 0],
                                       op0=ALU.mult, op1=ALU.subtract).then_inc(s_w0, 1)
            step(v.tensor_scalar(B9[:, :], B9[:, :], G_SCALE * W_SCALE, None, ALU.mult))
            for h in range(2):
                ln_rstd(h, 2 + h, X_SCALE)
                for t in range(h * HT, (h + 1) * HT):
                    v.tensor_scalar(HS[:, t], X[:, t], mv[:, t, 0:1], rstd[:, t:t + 1],
                                    ALU.subtract, ALU.mult).then_inc(s_hs, 1)
                for t in range(h * HT, (h + 1) * HT):
                    dve.wait_ge(s_hhi, t + 1)
                    v.tensor_tensor(HHL[:, t, 1], HS[:, t], HHL[:, t, 0], ALU.subtract).then_inc(s_hhl, 1)
            dve.wait_ge(s_lg, 1)
            step(v.tensor_copy(logits[:, :, :].rearrange("p t e -> p (t e)"), bank[4][:, 0:T * E]))
            for t in range(T):
                mark(v.max(top[:, t], logits[:, t]))
            here()
            for t in range(T):
                mark(v.max_index(topi[:, t], top[:, t], logits[:, t]))
            v.tensor_tensor(z12[:, :], top[:, :, 0], top[:, :, 1], ALU.subtract).then_inc(s_z12, 1)
            here()
            step(v.tensor_copy(topf[:, :, :], topi[:, :, 0:2]))
            for k, m in enumerate((mask0, mask1)):
                mark(v.tensor_tensor(m[:, :, :], iota_e[:, :].unsqueeze(1).broadcast_to([P, T, E]),
                                     topf[:, :, k:k + 1].broadcast_to([P, T, E]), ALU.is_equal))
            dve.wait_ge(s_th, 1)
            mark(v.tensor_scalar(wk[:, 0], th[:, :], 0.5, 0.5, ALU.mult, ALU.add))
            mark(v.tensor_scalar(wk[:, 1], th[:, :], -0.5, 0.5, ALU.mult, ALU.add))
            mark(v.memset(gates[:, :, E:E + 1], 1.0))
            here()
            for k, m in enumerate((mask0, mask1)):
                mark(v.tensor_tensor(m[:, :, :], m[:, :, :], wk[:, k].unsqueeze(2).broadcast_to([P, T, E]), ALU.mult))
            here()
            v.tensor_tensor(gates[:, :, 0:E], mask0[:, :, :], mask1[:, :, :], ALU.add).then_inc(s_gates, 1)
            dve.wait_ge(s_gates, 1)
            r9 = COEF[:, :, 0:E + 1]
            step(v.tensor_scalar(r9, gates[:, :, :], G_SCALE, None, ALU.mult))
            for part in range(3):
                ins = v.tensor_copy(gates3[:, :, part], r9)
                if part < 2:
                    step(ins)
                    step(v.tensor_tensor(r9, r9, gates3[:, :, part], ALU.subtract))
                else:
                    ins.then_inc(s_gates, 1)
            mark(v.tensor_scalar(tgs[:, :], tg[:, 2:3], 1.0 / (G_SCALE * W_SCALE), None, ALU.mult))

            def hidden_low(n):
                h, c = UNITS[n]
                hi, lo = (GHL[:, s, c, h * 512:(h + 1) * 512] for s in range(2))
                dve.wait_ge(s_ghi, n + 1)
                if c < E:
                    v.tensor_tensor(lo, GG[:, n % 2], hi, ALU.subtract).then_inc(s_ghl, 1)
                else:
                    v.scalar_tensor_tensor(out=lo, in0=G32[:, n % 2], scalar=G_SCALE, in1=hi,
                                           op0=ALU.mult, op1=ALU.subtract).then_inc(s_ghl, 1)

            def add_down(t):
                dve.wait_ge(s_down, t + 1)
                v.scalar_tensor_tensor(out=X[:, t], in0=bank[DOWN_BANK[t]][:, 0:D], scalar=tgs[:, 0:1],
                                       in1=X[:, t], op0=ALU.mult, op1=ALU.add).then_inc(s_down_used, 1)

            for n, (h, c) in enumerate(UNITS):
                dve.wait_ge(s_gelu, n + 1)
                if c < E:
                    dve.wait_ge(s_bc, ROUTED[n])
                    if n >= 2:
                        dve.wait_ge(s_ghi, n - 1)
                        dve.wait_ge(s_ghl, n - 1)
                    v.tensor_tensor(GG[:, n % 2], G32[:, n % 2], bank[5 + ROUTED[n] % 2][:, :],
                                    ALU.mult).then_inc(s_gg, 1)
                if n and UNITS[n - 1][1] < E:
                    hidden_low(n - 1)
                if c >= E:
                    hidden_low(n)
                if n == 1:
                    dve.wait_ge(s_gt_ps, 1)
                    v.tensor_copy(gates3_t[:, :], bank[5][:, :].bitcast(BF16)[0:3 * (E + 1), :]).then_inc(s_gt3, 1)
                if n - 2 in DOWN_AFTER:
                    add_down(DOWN_AFTER[n - 2])
            hidden_low(2 * CA - 1)
            def attention_q(b):
                if b:
                    dve.wait_ge(s_qt_ps, 4 * b)
                heads = lambda a: a.rearrange("p (h d) -> p h d", h=HEADS)
                for i in range(2):
                    t = 2 * b + i
                    step(v.tensor_scalar(HC[:, i], X[:, t], mv[:, t, 0:1], rstd[:, t:t + 1],
                                         ALU.subtract, ALU.mult))
                    step(v.tensor_copy(QTOK[:, i, :, 0], heads(HC[:, i])))
                    step(v.tensor_tensor(heads(RC[:, i]), heads(HC[:, i]), QTOK[:, i, :, 0], ALU.subtract))
                    step(v.tensor_copy(QTOK[:, i, :, 3], heads(RC[:, i])))
                    v.tensor_tensor(QTOK[:, i, :, 5], heads(RC[:, i]), QTOK[:, i, :, 3],
                                    ALU.subtract).then_inc(s_q1, 1)

            def maximum(b, u):
                n = 12 * b + u
                dve.wait_ge(s_p1, n + 1)
                i = 0 if u < 4 else 1
                nh = 4 if i == 0 else 2
                h0 = 4 * u if i == 0 else 2 * (u - 4)
                v.tensor_reduce(MX[:, b % 2, i, h0:h0 + nh], s1_bank[n % 2][:, :].rearrange("p (h n) -> p h n", h=nh),
                                AX.X, ALU.max).then_inc(s_mx, 1)

            def minus_maximum(b):
                dve.wait_ge(s_mx, 12 * (b + 1))
                p = b % 2
                step(v.tensor_tensor(NM[:, p], MX[:, p], floor[:, :].unsqueeze(2).broadcast_to([P, 2, HEADS]),
                                     ALU.max))
                mark(v.tensor_scalar(WZ[:, p], NM[:, p], -1.0, CAUSAL_FILL, ALU.mult, ALU.add))
                step(v.tensor_scalar(NMR[:, :, :], NM[:, p], -1.0, None, ALU.mult))
                v.tensor_scalar(WZ[:, p], WZ[:, p], 0.0, None, ALU.min).then_inc(s_wz, 1)
                if b:
                    dve.wait_ge(s_nm_ps, b)
                step(v.tensor_copy(NMP[:, :, 0], NMR[:, :, :]))
                step(v.tensor_tensor(NMR2[:, :, :], NMR[:, :, :], NMP[:, :, 0], ALU.subtract))
                step(v.tensor_copy(NMP[:, :, 1], NMR2[:, :, :]))
                v.tensor_tensor(NMP[:, :, 2], NMR2[:, :, :], NMP[:, :, 1], ALU.subtract).then_inc(s_nmp, 1)

            def attention_out(b, i):
                t = 2 * b + i
                dve.wait_ge(s_wm, b + 1)
                step(v.tensor_scalar(DENR[:, :], WM[:, b % 2, i], hidden_n[:, i:i + 1], None, ALU.mult))
                dve.wait_ge(s_o_ps, t + 1)
                o = ot_bank[:, :].rearrange("p (h c) -> p h c", c=32)
                step(v.tensor_tensor(DEN[:, :], o[:, :, DH], DENR[:, :], ALU.add))
                step(v.reciprocal(DENR[:, :], DEN[:, :]))
                dve.wait_ge(s_hv, t + 1)
                num = NUM[:, :].rearrange("p (h d) -> p h d", h=HEADS)
                v.tensor_tensor(num, o[:, :, 0:DH], HV[:, i].rearrange("p (h d) -> p h d", h=HEADS),
                                ALU.add).then_inc(s_o_used, 1)
                dve.wait_ge(s_o_used, t + 1)
                step(v.tensor_tensor(num, num, DENR[:, :].unsqueeze(2).broadcast_to([P, HEADS, DH]), ALU.mult))
                step(v.scalar_tensor_tensor(out=X[:, t], in0=NUM[:, :], scalar=tg[:, 1:2], in1=X[:, t],
                                            op0=ALU.mult, op1=ALU.add))

            def scaled_rows(g):
                ln_rstd(g, 8 + g, X_SCALE, 2)
                for t in (2 * g, 2 * g + 1):
                    v.tensor_scalar(DHS[:, t], X[:, t], mv[:, t, 0:1], rstd[:, t:t + 1],
                                    ALU.subtract, ALU.mult).then_inc(s_dhs, 1)

            def row_low(t):
                dve.wait_ge(s_dhhi, t + 1)
                v.tensor_tensor(DHL[:, t, 1], DHS[:, t], DHL[:, t, 0], ALU.subtract).then_inc(s_dhl, 1)

            dve.wait_ge(s_masks, 4)
            dve.wait_ge(s_down_used, 2)
            ln_variance(0, 4, 2)
            add_down(3)
            dve.wait_ge(s_down_used, 4)
            ln_variance(1, 5, 2)
            ln_rstd(0, 4, 1.0, 2)
            attention_q(0)
            add_down(4)
            add_down(5)
            for u in range(12):
                maximum(0, u)
            minus_maximum(0)
            add_down(6)
            ln_rstd(1, 5, 1.0, 2)
            attention_q(1)
            add_down(7)
            dve.wait_ge(s_down_used, T)
            for j in range(2):
                v.memset(o_bank[j][:, :], 0.0).then_inc(s_obank, 1)
            for g in range(2, 4):
                ln_variance(g, 4 + g, 2)
            for b in range(B):
                if b:
                    for i in range(2):
                        attention_out(b - 1, i)
                if b + 1 < B:
                    for u in range(12):
                        maximum(b + 1, u)
                    minus_maximum(b + 1)
                if b + 2 < B:
                    ln_rstd(b + 2, b + 6, 1.0, 2)
                    attention_q(b + 2)
                if b == B - 2:
                    for g in range(2):
                        ln_variance(g, 8 + g, 2)
                    dve.wait_ge(s_qt_ps, 4 * B)
                    for g in range(2):
                        scaled_rows(g)
                if b == B - 1:
                    ln_variance(2, 10, 2)
                    for t in range(HT):
                        row_low(t)
                    scaled_rows(2)
            for i in range(2):
                attention_out(B - 1, i)
            ln_variance(3, 11, 2)
            scaled_rows(3)
            for t in range(HT, T):
                row_low(t)
            dve.wait_ge(s_rwh, 2)
            dve.wait_ge(s_dw_small, 64)
            v.scalar_tensor_tensor(out=RW1[:, 1].rearrange("p k h -> p (k h)"),
                                   in0=RW1R.rearrange("p k h -> p (k h)"), scalar=W_SCALE,
                                   in1=RW1[:, 0].rearrange("p k h -> p (k h)"),
                                   op0=ALU.mult, op1=ALU.subtract).then_inc(s_rw, 1)
            v.scalar_tensor_tensor(out=RW2[:, 1], in0=RW2R[:, :], scalar=W_SCALE, in1=RW2[:, 0],
                                   op0=ALU.mult, op1=ALU.subtract).then_inc(s_rw, 1)
            for h in range(2):
                dve.wait_ge(s_rg, h + 1)
                hi, lo = (RHL[:, s, h * 512:(h + 1) * 512] for s in range(2))
                src = R32[:, h * 512:(h + 1) * 512]
                step(v.tensor_scalar(hi, src, G_SCALE, None, ALU.mult))
                v.scalar_tensor_tensor(out=lo, in0=src, scalar=G_SCALE, in1=hi,
                                       op0=ALU.mult, op1=ALU.subtract).then_inc(s_rhl, 1)
            dve.wait_ge(s_dlg, 1)
            step(v.tensor_copy(LG[:, :, :].rearrange("p t e -> p (t e)"), bank[6][:, 0:T * E]))
            step(v.tensor_reduce(LM[:, :], LG[:, :, :], AX.X, ALU.max))
            v.tensor_tensor(LG[:, :, :], LG[:, :, :], LM[:, :].unsqueeze(2).broadcast_to([P, T, E]),
                            ALU.subtract).then_inc(s_dl, 1)
            dve.wait_ge(s_ex, 1)
            step(v.tensor_reduce(LM[:, :], PR[:, :, :], AX.X, ALU.add))
            step(v.reciprocal(LM[:, :], LM[:, :]))
            step(v.tensor_tensor(PR[:, :, :], PR[:, :, :], LM[:, :].unsqueeze(2).broadcast_to([P, T, E]), ALU.mult))
            for t in range(T):
                mark(v.max(DTOP[:, t], PR[:, t]))
            here()
            for t in range(T):
                mark(v.max_index(DTOPI[:, t], DTOP[:, t], PR[:, t]))
            here()
            step(v.tensor_copy(DTOPF[:, :, :], DTOPI[:, :, 0:2]))
            for k in range(2):
                mark(v.tensor_tensor(M01[:, :, k], iota_e[:, :].unsqueeze(1).broadcast_to([P, T, E]),
                                     DTOPF[:, :, k:k + 1].broadcast_to([P, T, E]), ALU.is_equal))
            here()
            mark(v.tensor_copy(M01B[:, :, :, :].rearrange("p t k e -> p (t k e)"),
                               M01[:, :, :, :].rearrange("p t k e -> p (t k e)")))
            v.tensor_tensor(MSB[:, :, :], M01[:, :, 0], M01[:, :, 1], ALU.add).then_inc(s_m, 1)
            here()
            dve.wait_ge(s_rank, 1)
            step(v.tensor_copy(NE01[:, :, :].rearrange("p k e -> p (k e)"), bank[5][:, 0:2 * E]))
            step(v.tensor_tensor(NE[:, :], NE01[:, 0], NE01[:, 1], ALU.add))
            dve.wait_ge(s_dconst, 4)
            step(v.tensor_tensor(USED[:, :, :], NE[:, :].unsqueeze(2).broadcast_to([P, E, T]),
                                 iota_full[:, :].unsqueeze(1).broadcast_to([P, E, T]), ALU.is_gt))
            step(v.tensor_reduce(NT[:, :], USED[:, :, :], AX.X, ALU.add))
            step(v.tensor_tensor_scan(ENDT[:, :], ones[:, 0:E], NT[:, :], 0.0, ALU.mult, ALU.add))
            step(v.tensor_tensor(BASE[:, :], ENDT[:, :], NT[:, :], ALU.subtract))
            step(v.tensor_scalar(BASE[:, :], BASE[:, :], float(P), None, ALU.mult))
            step(v.tensor_tensor(SLOTQ[:, :, :], bank[4][:, 0:T * E].rearrange("p (t e) -> p t e", e=E),
                                 BASE[:, :].unsqueeze(1).broadcast_to([P, T, E]), ALU.add))
            for k in range(2):
                mark(v.tensor_tensor(SLOTM[:, k], M01[:, :, k], SLOTQ[:, :, :], ALU.mult))
            here()
            step(v.tensor_reduce(SLOTF[:, :, :], SLOTM[:, :, :, :], AX.X, ALU.add))
            v.tensor_copy(SLOT[:, :, :], SLOTF[:, :, :]).then_inc(s_slot, 1)
            step(v.tensor_tensor(EOF_[:, :, :], iota_tile[:, :].unsqueeze(2).broadcast_to([P, TILES, E]),
                                 ENDT[:, :].unsqueeze(1).broadcast_to([P, TILES, E]), ALU.is_ge))
            step(v.tensor_reduce(EIDF[:, :], EOF_[:, :, :], AX.X, ALU.add))
            step(v.tensor_scalar(EIDF[:, :], EIDF[:, :], float(E - 1), None, ALU.min))
            v.tensor_copy(EID[:, :], EIDF[:, :]).then_inc(s_eid, 1)
            dve.wait_ge(s_gb, 1)
            step(v.tensor_scalar(GBH[:, :, :], GB[:, :, :], G_SCALE, None, ALU.mult))
            step(v.scalar_tensor_tensor(out=GBL[:, :, :], in0=GB[:, :, :], scalar=G_SCALE, in1=GBH[:, :, :],
                                        op0=ALU.mult, op1=ALU.subtract))
            step(v.memset(GB16.rearrange("p c e x -> p (c e x)").bitcast(F32), 0.0))
            for s, part in enumerate((GBH, GBL)):
                spread = GB16.rearrange("p c e x -> p c (e x)")[:, :, s * E::2 * E + 1]
                v.tensor_copy(spread, part[:, :, :].rearrange("p e c -> p c e")).then_inc(s_gb16, 1)
            for k in range(2):
                mark(v.tensor_scalar(WKD[:, k], DTOP[:, :, k], tg[:, 3:4], 1.0 / (G_SCALE * W_SCALE),
                                     ALU.mult, ALU.mult))
            step(v.tensor_scalar(ACTV[:, :, :], NE01[:, :, :], 0.0, None, ALU.is_gt))
            for k in range(2):
                step(v.tensor_scalar(CF[:, k], M01[:, :, k], -1.0, 1.0, ALU.mult, ALU.add))
                step(v.tensor_tensor(CF[:, k], CF[:, k], ACTV[:, k].unsqueeze(1).broadcast_to([P, T, E]), ALU.mult))
                step(v.tensor_tensor(CF[:, k], CF[:, k], DTOP[:, :, k:k + 1].broadcast_to([P, T, E]), ALU.mult))
                step(v.tensor_tensor(SLOTM[:, k], M01[:, :, k], DTOP[:, :, k:k + 1].broadcast_to([P, T, E]), ALU.mult))
            for r in range(2):
                mark(v.tensor_tensor(COEF[:, :, r * E:(r + 1) * E], CF[:, 0], CF[:, 1], ALU.add))
            step(v.tensor_tensor(SLOTQ[:, :, :], SLOTM[:, 0], SLOTM[:, 1], ALU.add))
            v.tensor_tensor(COEF[:, :, 2 * E:3 * E], COEF[:, :, 0:E], SLOTQ[:, :, :], ALU.add).then_inc(s_coef, 1)
            for i in D_BLOCKS[-2:]:
                _, hi, lo = weight_block(i)
                dve.wait_ge(s_whi, i + 1)
                v.tensor_tensor(lo, STG[:, i % 2].rearrange("p (c d) -> p c d", d=D), hi,
                                ALU.subtract).then_inc(s_wlate, 1)
            dve.wait_ge(s_ce, 1)
            v.tensor_scalar(B24[0:2 * E, :], bank[7][0:2 * E, 0:D], 1.0 / (G_SCALE * W_SCALE), None,
                            ALU.mult).then_inc(s_ce_sb, 1)
            def rows_t(j, q, first=False):
                dve.wait_ge(s_xt_ps, j + 1)
                if not first:
                    dve.wait_ge(s_dup, UP_BANKS * (j - 1))
                v.tensor_copy(XT[:, q].rearrange("p k s n -> p (k s n)"),
                              bank[q][:, :].bitcast(F16)[:, 0:4 * P]).then_inc(s_xt, 1)

            def add_halves(j, q, first=False):
                if not first:
                    dve.wait_ge(s_dgh, 2 * j - 2)
                    dve.wait_ge(s_dgl, 2 * j - 2)
                for hb in range(UP_BANKS):
                    dve.wait_ge(s_dup, UP_BANKS * j + hb + 1)
                    o = up_bank[hb][:, :].rearrange("p (c s n) -> p c n s", c=2, s=2)
                    half = GD[:, q, hb * 2 * P:(hb + 1) * 2 * P].rearrange("p (c n) -> p c n", c=2)
                    v.tensor_reduce(half, o, AX.X, ALU.add).then_inc(s_dadd, 1)

            def split_hidden(j, q, hb):
                dve.wait_ge(s_dgh, 2 * j + hb + 1)
                hi, lo = (GDL[:, q, s, hb * 512:(hb + 1) * 512] for s in range(2))
                v.scalar_tensor_tensor(out=lo, in0=GD[:, q, hb * 512:(hb + 1) * 512], scalar=G_SCALE, in1=hi,
                                       op0=ALU.mult, op1=ALU.subtract).then_inc(s_dgl, 1)

            def tile_out(j, q, m, first=False):
                dve.wait_ge(s_dd, j + 1)
                if not first:
                    dve.wait_ge(s_yst[q], 16 * m)
                v.tensor_reduce(YS[:, q], bank[6 + q][:, :].rearrange("p (s d) -> p d s", s=2), AX.X,
                                ALU.add).then_inc(s_ys, 1)

            rows_t(0, 0, first=True)
            for j in range(HEAD):
                add_halves(j, j % 2, first=j < 2)
                rows_t(j + 1, (j + 1) % 2, first=j == 0)
                for hb in range(2):
                    split_hidden(j, j % 2, hb)
                if j:
                    tile_out(j - 1, (j - 1) % 2, 0, first=True)
            with dve.Fori(0, LOOPS) as i:
                for r in range(UNROLL):
                    j, q = UNROLL * i + HEAD + r, (HEAD + r) % 2
                    add_halves(j, q)
                    rows_t(j + 1, 1 - q)
                    for hb in range(2):
                        split_hidden(j, q, hb)
                    tile_out(j - 1, 1 - q, UNROLL // 2 * i + (HEAD + r - 1) // 2)
            for j in range(TAIL, TILES):
                add_halves(j, j % 2)
                if j + 1 < TILES:
                    rows_t(j + 1, (j + 1) % 2)
                for hb in range(2):
                    split_hidden(j, j % 2, hb)
                tile_out(j - 1, (j - 1) % 2, (j - 1) // 2)
            tile_out(TILES - 1, (TILES - 1) % 2, (TILES - 1) // 2)
            dve.wait_ge(s_cf_ps, 1)
            for h in range(2):
                v.tensor_copy(COEF_T[0:3 * E, h * 512:(h + 1) * 512], bank[2 + h][0:3 * E, :]).then_inc(s_cf, 1)
            for t in range(T):
                dve.wait_ge(s_base, t + 1)
                v.scalar_tensor_tensor(out=X[:, t], in0=bank[4 + t % 2][:, 0:D], scalar=tg[:, 3:4], in1=X[:, t],
                                       op0=ALU.mult, op1=ALU.add).then_inc(s_base_used, 1)
            for t in range(T):
                dve.wait_ge(s_yg[t], 32)
                step(v.scalar_tensor_tensor(out=X[:, t], in0=YG[:, t, 0], scalar=WKD[:, 0, t:t + 1], in1=X[:, t],
                                            op0=ALU.mult, op1=ALU.add))
                v.scalar_tensor_tensor(out=X[:, t], in0=YG[:, t, 1], scalar=WKD[:, 1, t:t + 1], in1=X[:, t],
                                       op0=ALU.mult, op1=ALU.add).then_inc(s_xout, 1)


def lay_out(x, ctx_2048, g_xattn, g_ffn, L0_ffn_gate_w, L0_ffn_w1, L0_ffn_b1, L0_ffn_w2, L0_ffn_b2,
            L0_ffn_shared_w1, L0_ffn_shared_b1, L0_ffn_shared_w2, L0_ffn_shared_b2,
            L1_ffn_rw1, L1_ffn_rw2, L1_ffn_w1, L1_ffn_b1, L1_ffn_w2, L1_ffn_b2):
    tokens, d = x.shape[0] * x.shape[1], x.shape[2]
    k = d // P
    experts = L0_ffn_gate_w.shape[1]
    shared = L0_ffn_shared_w1.shape[1] // P
    hidden = L1_ffn_w1.shape[2]
    ctx = ctx_2048.reshape(tokens, d)
    return {
        "x": x.reshape(tokens, d),
        "ctx": ctx,
        "ctx_t": ctx.T.reshape(k, P, tokens).transpose(1, 0, 2),
        "gates": np.concatenate([g_xattn, g_ffn]),
        "gate_w": L0_ffn_gate_w.reshape(k, P, experts).transpose(1, 0, 2),
        "l0_w1": np.concatenate([L0_ffn_w1.reshape(experts, k, P, P).transpose(2, 0, 1, 3),
                                 L0_ffn_shared_w1.reshape(k, P, shared, P).transpose(1, 2, 0, 3)], 1),
        "l0_b1": np.concatenate([L0_ffn_b1, L0_ffn_shared_b1.reshape(shared, P)], 0).T,
        "l0_w2": np.concatenate([L0_ffn_w2.transpose(1, 0, 2),
                                 L0_ffn_shared_w2.reshape(shared, P, d).transpose(1, 0, 2)], 1),
        "l0_b2": np.concatenate([L0_ffn_b2, L0_ffn_shared_b2[None]], 0),
        "router_w1": L1_ffn_rw1.reshape(k, P, -1).transpose(1, 0, 2),
        "router_w2": L1_ffn_rw2,
        "l1_w1": L1_ffn_w1.reshape(experts, k, P, hidden).transpose(2, 0, 1, 3),
        "l1_b1": L1_ffn_b1.reshape(experts, hidden // P, P).transpose(2, 0, 1),
        "l1_w2": L1_ffn_w2.reshape(experts, hidden // P, P, d).transpose(2, 0, 1, 3),
        "l1_b2": L1_ffn_b2,
    }


def kernel(**inputs):
    import concourse.bacc as bacc
    from concourse.bass_utils import run_bass_kernel_spmd

    shape = inputs["x"].shape
    nc = bacc.Bacc("TRN2", target_bir_lowering=False, num_devices=1)
    arrays, args = {}, []
    for name, a in lay_out(**{n: np.asarray(a) for n, a in inputs.items()}).items():
        a = np.ascontiguousarray(a)
        arrays[f"in_{name}_dram"] = a
        args.append(nc.dram_tensor(f"in_{name}_dram", a.shape, mybir.dt.from_np(a.dtype),
                                   kind="ExternalInput").ap())
    args.append(nc.dram_tensor("out_dram", (shape[0] * shape[1], shape[2]), F32, kind="ExternalOutput").ap())
    flamingo(nc, *args)
    result = run_bass_kernel_spmd(nc, [arrays], core_ids=[0])
    return result.results[0]["out_dram"].reshape(shape)
```
